# Optimizing a Trainium2 kernel written in Bass

```python
import numpy as np
import jax
import jax.numpy as jnp

def _softmax(x, axis=-1):
    return jax.nn.softmax(x, axis=axis)

def _gelu(x):
    return jax.nn.gelu(x, approximate=True)

def _silu(x):
    return jax.nn.silu(x)

def _sigmoid(x):
    return jax.nn.sigmoid(x)

def _layernorm(x, axis=-1, eps=1e-05):
    m = jnp.mean(x, axis=axis, keepdims=True)
    v = jnp.var(x, axis=axis, keepdims=True)
    return (x - m) / jnp.sqrt(v + eps)

def _scatter_add(tgt, idx, src, axis=0):
    return tgt.at[idx].add(src)

def _segment_sum(src, seg, n):
    return jax.ops.segment_sum(src, seg, n)
kernel_name = 'mk_gps_d1_gnn_r8_956198'

def setup_inputs(seed: int=0):
    np.random.seed(seed)
    _w = jnp.asarray

    def _rec_inputs():
        import jax
        import jax.numpy as jnp
        _gk = jax.random.key(seed)
        x = -0.0001126 + 1 * jax.random.normal(jax.random.fold_in(_gk, 1), (3750, 256), jnp.float32)
        src = jax.random.randint(jax.random.fold_in(_gk, 2), (120000,), 0, 3750, jnp.int32)
        dst = jnp.minimum((3750 * jax.random.uniform(jax.random.fold_in(_gk, 3), (120000,)) ** 2.0).astype(jnp.int32), 29999)
        _o = jnp.argsort(dst, stable=True)
        src = src[_o]
        dst = dst[_o]
        edge_type_8 = jax.random.randint(jax.random.fold_in(_gk, 12), (120000,), 0, 8, jnp.int32)
        return (x, src, dst, edge_type_8)
    x, src, dst, edge_type_8 = _rec_inputs()

    def _L0_gnn_setup():
        import jax, jax.numpy as jnp
        import numpy as np
        N_NODES = 3750
        N_EDGES = 60000
        IN_FEAT = 256
        OUT_FEAT = 256
        N_RELS = 8
        N_HEADS = 4
        HEAD_DIM = OUT_FEAT // N_HEADS
        LEAKY_SLOPE = 0.2
        key = jax.random.key(seed)
        ks = jax.random.split(key, 8)
        inputs = jax.random.normal(ks[0], (N_NODES, IN_FEAT), dtype=jnp.float32)
        conv_weights = jax.random.normal(ks[1], (N_RELS, N_HEADS, IN_FEAT, HEAD_DIM), dtype=jnp.float32) * (1.0 / np.sqrt(IN_FEAT))
        attn_l = jax.random.normal(ks[2], (N_RELS, N_HEADS, HEAD_DIM), dtype=jnp.float32) * 0.1
        attn_r = jax.random.normal(ks[3], (N_RELS, N_HEADS, HEAD_DIM), dtype=jnp.float32) * 0.1
        h_bias = jax.random.normal(ks[4], (OUT_FEAT,), dtype=jnp.float32) * 0.02
        edge_src = jax.random.randint(ks[5], (N_EDGES,), 0, N_NODES, dtype=jnp.int32)
        edge_dst = jax.random.randint(ks[6], (N_EDGES,), 0, N_NODES, dtype=jnp.int32)
        edge_type = jax.random.randint(ks[7], (N_EDGES,), 0, N_RELS, dtype=jnp.int32)
        return {'inputs': inputs, 'conv_weights': conv_weights, 'attn_l': attn_l, 'attn_r': attn_r, 'h_bias': h_bias, 'edge_src': edge_src, 'edge_dst': edge_dst, 'edge_type': edge_type}
    _L0_gnn_all = _L0_gnn_setup()
    _L0_gnn_in = {k: v for k, v in _L0_gnn_all.items() if k in ('conv_weights', 'attn_l', 'attn_r', 'h_bias')}
    del _L0_gnn_all

    def _L0_mix_setup():
        import jax, jax.numpy as jnp
        import numpy as np
        HEADS = 8
        DIM_HEAD = 64
        EPS = 1e-05

        def _inst_norm(t):
            mu = jnp.mean(t, axis=-1, keepdims=True)
            var = jnp.var(t, axis=-1, keepdims=True)
            return (t - mu) / jnp.sqrt(var + EPS)
        key = jax.random.key(seed)
        k1, k2, k3, k4 = jax.random.split(key, 4)
        b, n, dim = (4, 1024, 256)
        inner = HEADS * DIM_HEAD
        x = jax.random.normal(k1, (b, n, dim), dtype=jnp.float32)
        w_qkv = jax.random.normal(k2, (dim, 3 * inner), dtype=jnp.float32) * (1.0 / DIM_HEAD)
        w_out = jax.random.normal(k3, (inner, dim), dtype=jnp.float32) * dim ** (-0.5)
        b_out = jax.random.normal(k4, (dim,), dtype=jnp.float32) * 0.01
        return {'x': x, 'w_qkv': w_qkv, 'w_out': w_out, 'b_out': b_out}
    _L0_mix_all = _L0_mix_setup()
    _L0_mix_in = {k: v for k, v in _L0_mix_all.items() if k in ('w_qkv', 'w_out', 'b_out')}
    del _L0_mix_all

    def _L0_ffn_setup():
        import jax, jax.numpy as jnp
        import numpy as np
        B, S, D = (8, 512, 256)
        H = 4 * D
        CAPACITY = 0.5
        key = jax.random.key(seed)
        ks = jax.random.split(key, 6)
        x = jax.random.normal(ks[0], (B, S, D), dtype=jnp.float32)
        attention_mask = jnp.zeros((B, 1, 1, S), dtype=jnp.float32)
        wr = jax.random.normal(ks[1], (D, 1), dtype=jnp.float32) * 0.02
        br = jnp.zeros((1,), dtype=jnp.float32)
        w1 = jax.random.normal(ks[2], (D, H), dtype=jnp.float32) * 0.02
        b1 = jnp.zeros((H,), dtype=jnp.float32)
        w2 = jax.random.normal(ks[3], (H, D), dtype=jnp.float32) * 0.02
        b2 = jnp.zeros((D,), dtype=jnp.float32)
        return {'x': x, 'attention_mask': attention_mask, 'wr': wr, 'br': br, 'w1': w1, 'b1': b1, 'w2': w2, 'b2': b2}
    _L0_ffn_all = _L0_ffn_setup()
    _L0_ffn_in = {k: v for k, v in _L0_ffn_all.items() if k in ('attention_mask', 'wr', 'br', 'w1', 'b1', 'w2', 'b2')}
    del _L0_ffn_all
    return {'x': x, 'src': src, 'dst': dst, 'edge_type_8': edge_type_8, 'L0_gnn_conv_weights': _L0_gnn_in['conv_weights'], 'L0_gnn_attn_l': _L0_gnn_in['attn_l'], 'L0_gnn_attn_r': _L0_gnn_in['attn_r'], 'L0_gnn_h_bias': _L0_gnn_in['h_bias'], 'L0_mix_w_qkv': _L0_mix_in['w_qkv'], 'L0_mix_w_out': _L0_mix_in['w_out'], 'L0_mix_b_out': _L0_mix_in['b_out'], 'L0_ffn_attention_mask': _L0_ffn_in['attention_mask'], 'L0_ffn_wr': _L0_ffn_in['wr'], 'L0_ffn_br': _L0_ffn_in['br'], 'L0_ffn_w1': _L0_ffn_in['w1'], 'L0_ffn_b1': _L0_ffn_in['b1'], 'L0_ffn_w2': _L0_ffn_in['w2'], 'L0_ffn_b2': _L0_ffn_in['b2']}

def reference(x, src, dst, edge_type_8, L0_gnn_conv_weights, L0_gnn_attn_l, L0_gnn_attn_r, L0_gnn_h_bias, L0_mix_w_qkv, L0_mix_w_out, L0_mix_b_out, L0_ffn_attention_mask, L0_ffn_wr, L0_ffn_br, L0_ffn_w1, L0_ffn_b1, L0_ffn_w2, L0_ffn_b2):
    import jax
    import jax.numpy as jnp

    def _L0_gnn_ref(inputs, conv_weights, attn_l, attn_r, h_bias, edge_src, edge_dst, edge_type):
        import jax, jax.numpy as jnp
        import numpy as np
        N_NODES = 3750
        N_EDGES = 60000
        IN_FEAT = 256
        OUT_FEAT = 256
        N_RELS = 8
        N_HEADS = 4
        HEAD_DIM = OUT_FEAT // N_HEADS
        LEAKY_SLOPE = 0.2
        feat_all = jnp.einsum('ni,rhid->rnhd', inputs, conv_weights)
        feat_src_e = feat_all[edge_type, edge_src]
        feat_dst_e = feat_all[edge_type, edge_dst]
        el = jnp.sum(feat_src_e * attn_l[edge_type], axis=-1)
        er = jnp.sum(feat_dst_e * attn_r[edge_type], axis=-1)
        e = jax.nn.leaky_relu(el + er, negative_slope=LEAKY_SLOPE)
        m = jax.ops.segment_max(e, edge_dst, num_segments=N_NODES)
        ex = jnp.exp(e - m[edge_dst])
        denom = jax.ops.segment_sum(ex, edge_dst, num_segments=N_NODES)
        alpha = ex / denom[edge_dst]
        h = jax.ops.segment_sum(alpha[..., None] * feat_src_e, edge_dst, num_segments=N_NODES)
        h = h.reshape(N_NODES, OUT_FEAT) + h_bias
        return h

    def _L0_mix_ref(x, w_qkv, w_out, b_out):
        import jax, jax.numpy as jnp
        import numpy as np
        HEADS = 8
        DIM_HEAD = 64
        EPS = 1e-05

        def _inst_norm(t):
            mu = jnp.mean(t, axis=-1, keepdims=True)
            var = jnp.var(t, axis=-1, keepdims=True)
            return (t - mu) / jnp.sqrt(var + EPS)
        b, n, dim = x.shape
        qkv = x @ w_qkv
        q, k, v = jnp.split(qkv, 3, axis=-1)
        to_heads = lambda t: t.reshape(b, n, HEADS, DIM_HEAD).transpose(0, 2, 1, 3)
        q, k, v = (to_heads(q), to_heads(k), to_heads(v))
        k = _inst_norm(k)
        v = _inst_norm(v)
        dots = jnp.einsum('bhnd,bhne->bhde', k, v)
        out = jnp.einsum('bhnd,bhde->bhne', q, dots) * (1.0 / n)
        out = out.transpose(0, 2, 1, 3).reshape(b, n, HEADS * DIM_HEAD)
        return out @ w_out + b_out

    def _L0_ffn_ref(x, attention_mask, wr, br, w1, b1, w2, b2):
        import jax, jax.numpy as jnp
        import numpy as np
        B, S, D = (8, 512, 256)
        H = 4 * D
        CAPACITY = 0.5
        b, s, d = x.shape
        weights = (jnp.einsum('bsd,do->bso', x, wr) + br)[..., 0]
        k = max(1, int(CAPACITY * s))
        kk = k - 1 if k > 1 else 1
        _, idx = jax.lax.top_k(weights, k)
        sel_idx = idx[:, :kk]
        sel = jnp.take_along_axis(x, sel_idx[:, :, None], axis=1)
        h = jax.nn.gelu(jnp.einsum('bkd,dh->bkh', sel, w1) + b1)
        y = jnp.einsum('bkh,hd->bkd', h, w2) + b2
        w_sel = jnp.take_along_axis(weights, sel_idx, axis=1)
        y = y * w_sel[..., None]
        batch_idx = jnp.arange(b)[:, None]
        processed = jnp.zeros_like(x).at[batch_idx, sel_idx].set(y)
        return processed + x
    xn = _layernorm(x, axis=-1)
    x = x + _L0_gnn_ref(xn, L0_gnn_conv_weights, L0_gnn_attn_l, L0_gnn_attn_r, L0_gnn_h_bias, src, dst, edge_type_8) + _L0_mix_ref(xn[None], L0_mix_w_qkv, L0_mix_w_out, L0_mix_b_out)[0]
    x = x + _L0_ffn_ref(_layernorm(x, axis=-1)[None], L0_ffn_attention_mask, L0_ffn_wr, L0_ffn_br, L0_ffn_w1, L0_ffn_b1, L0_ffn_w2, L0_ffn_b2)[0]
    return x

_drawn_inputs = setup_inputs


def setup_inputs(seed=0):
    import zlib

    import numpy as np

    out = dict(_drawn_inputs(seed))
    spreads = {'L0_ffn_b1': (0.0, 0.8), 'L0_ffn_b2': (0.0, 0.691)}
    factors = {'L0_gnn_h_bias': 3.075,
     'L0_mix_b_out': 6.54,
     'L0_ffn_wr': 3.806,
     'L0_ffn_w1': 4.348,
     'L0_ffn_w2': 4.061}
    for name, (base, spread) in spreads.items():
        noise = np.random.default_rng([zlib.crc32(name.encode()), seed]).standard_normal(out[name].shape)
        drawn = base * np.exp(spread * noise) if base else spread * noise
        out[name] = jnp.asarray(drawn.astype(out[name].dtype))
    for name, factor in factors.items():
        out[name] = (out[name] * factor).astype(out[name].dtype)
    return out
```

```python
import concourse.bass as bass
from concourse import mybir
from contextlib import ExitStack

NODES, DIM = 3750, 256
P = 128
NODE_TILES = -(-NODES // P)
NODES_PAD = NODE_TILES * P
RELS, HEADS, HEAD_DIM = 8, 4, 64
HEAD_COLS = HEAD_DIM + 1
ROW = HEADS * HEAD_COLS
EDGES = 120000
CHUNK_COLS = 17
CHUNK_EDGES = P * CHUNK_COLS
CHUNKS = -(-EDGES // CHUNK_EDGES)
EDGES_PAD = CHUNKS * CHUNK_EDGES
CE = CHUNK_COLS * HEADS
MIX_HEADS, MIX_DIM = 8, 64
INNER = MIX_HEADS * MIX_DIM
HIDDEN = 4 * DIM
HID_TILES = HIDDEN // P
SELECTED = NODES // 2 - 1
GROUP_TILES = 3
GROUPS = NODE_TILES // GROUP_TILES
GROUP_TOKENS = GROUP_TILES * P
EPS = 1e-5
SLOPE = 0.2
BIG = 1e38
assert CHUNKS % 2 == 0 and NODE_TILES % 2 == 0 and NODE_TILES % GROUP_TILES == 0


def gps_layer(nc, a, out):
    f32, i32, bf16 = mybir.dt.float32, mybir.dt.int32, mybir.dt.bfloat16
    ALU, ACT, AX = mybir.AluOpType, mybir.ActivationFunctionType, mybir.AxisListType
    ds = bass.ds

    ctx = ExitStack()
    with ctx:
        def sb(name, shape, dt=f32, where=ctx):
            return where.enter_context(nc.sbuf_tensor(name, shape, dt))

        def sem(name):
            return ctx.enter_context(nc.semaphore(name))

        def dram(name, shape):
            return nc.dram_tensor(name, shape, f32, kind="Internal").ap()

        features = dram("features", (NODES_PAD * RELS, ROW))
        dst_logits = dram("dst_logits", (NODES_PAD * RELS, HEADS))
        node_weights = dram("node_weights", (NODE_TILES, P))

        ident = sb("ident", [P, P])
        iota_free = sb("iota_free", [P, P])
        iota_part = sb("iota_part", [P, 1])
        block_base = sb("block_base", [P, NODE_TILES])
        x_res = sb("x_res", [P, NODE_TILES, DIM])
        bn = sb("bn", [P, NODE_TILES, 6])
        ln_mean = sb("ln_mean", [P, NODE_TILES])
        ln_rstd = sb("ln_rstd", [P, NODE_TILES])
        ln_t = sb("ln_t", [P, NODE_TILES])
        ln_u = sb("ln_u", [P, NODE_TILES])
        ET = CHUNKS * CHUNK_COLS
        feat_idx = sb("feat_idx", [P, ET], i32)
        er_idx = sb("er_idx", [P, ET], i32)
        dst_f = sb("dst_f", [P, ET])
        prev_mask = sb("prev_mask", [P, ET])
        next_mask = sb("next_mask", [P, ET])
        first_run = sb("first_run", [P, ET])
        last_run = sb("last_run", [P, ET])
        prev_open = sb("prev_open", [P, CHUNKS])
        next_open = sb("next_open", [P, CHUNKS])
        prev_pass = sb("prev_pass", [P, CHUNKS])
        next_pass = sb("next_pass", [P, CHUNKS])
        last_block = sb("last_block", [P, CHUNKS + 1], i32)

        psum = ctx.enter_context(nc.psum_tensor("psum", [P, 8, 512], f32))

        edges_in, x_in, conv_in, attn_in = sem("edges_in"), sem("x_in"), sem("conv_in"), sem("attn_in")
        const_ready, setup_done = sem("const_ready"), sem("setup_done")
        std_ready, weights_done, xn_ready = sem("std_ready"), sem("weights_done"), sem("xn_ready")
        xt_psum, xt_ready = sem("xt_psum"), sem("xt_ready")
        feat_psum = sem("feat_psum")
        feat_even, feat_odd, logits_out = sem("feat_even"), sem("feat_odd"), sem("logits_out")
        store = [sem("store0"), sem("store1")]
        tile_seen, staged_seen = sem("tile_seen"), sem("staged_seen")

        with ExitStack() as st:
            raw = sb("raw", [P, 5, ET], i32, st)
            conv = sb("conv", [P, 2, RELS * HEADS, HEAD_COLS], f32, st)
            attn = sb("attn", [P, 2, RELS * HEADS, HEAD_DIM], f32, st)
            prod = sb("prod", [P, RELS * HEADS, HEAD_DIM], f32, st)
            conv_er = sb("conv_er", [P, 2, RELS * HEADS], f32, st)
            table = sb("table", [P, 2, RELS, ROW], f32, st)
            er_tab = sb("er_tab", [P, 2, RELS * HEADS], f32, st)
            xn = sb("xn", [P, 2, DIM], f32, st)
            xt = sb("xt", [P, 2, 2, P], f32, st)
            run_start = sb("run_start", [P, ET], f32, st)
            block = st.enter_context(nc.Block())

            @block.sync
            def _(sp):
                sp.dma_start(raw[:], a["edges"]).then_inc(edges_in, 16)
                sp.dma_start(x_res[:], a["x"].rearrange("(t p) d -> p t d", p=P)).then_inc(x_in, 16)
                for k in range(2):
                    sp.dma_start(conv[:, k, :, 0:HEAD_DIM],
                                 a["conv"].rearrange("r h (k p) d -> k p (r h) d", p=P)[k]).then_inc(conv_in, 16)
                for k, name in enumerate(("attn_l", "attn_r")):
                    sp.dma_start(attn[:, k], a[name].rearrange("r h d -> (r h) d").partition_broadcast(P)).then_inc(attn_in, 16)
                with sp.Fori(0, NODE_TILES // 2) as i:
                    for u in range(2):
                        t = i * 2 + u
                        sp.wait_ge(feat_even, t * 4 + 4 + 2)
                        sp.sem_inc(tile_seen, 1)
                        sp.wait_ge(feat_odd, t * 4 + 4 + 2)
                        sp.sem_inc(tile_seen, 1)
                        sp.wait_ge(logits_out, t + 1 + 1)
                        sp.sem_inc(tile_seen, 1)
                        sp.dma_start(features.rearrange("(n r) c -> n (r c)", r=RELS)[ds(t * P, P), :],
                                     table[:, u].rearrange("p r c -> p (r c)")).then_inc(store[u], 16)
                        sp.dma_start(dst_logits.rearrange("(n r) c -> n (r c)", r=RELS)[ds(t * P, P), :],
                                     er_tab[:, u]).then_inc(store[u], 16)
                for u in range(2):
                    sp.wait_ge(store[u], 32 * NODE_TILES // 2 + 32)

            @block.gpsimd
            def _(pool):
                pool.memset(ident[:], 0.0).then_inc(const_ready, 1)
                pool.iota(iota_free[:], pattern=[[1, P]], base=0, channel_multiplier=0,
                          allow_small_or_imprecise_dtypes=True).then_inc(const_ready, 1)
                pool.iota(iota_part[:], pattern=[[0, 1]], base=0, channel_multiplier=1,
                          allow_small_or_imprecise_dtypes=True).then_inc(const_ready, 1)
                pool.iota(block_base[:], pattern=[[P, NODE_TILES]], base=0, channel_multiplier=0,
                          allow_small_or_imprecise_dtypes=True).then_inc(const_ready, 1)
                pool.wait_ge(const_ready, 4)
                pool.affine_select(out=ident[:], in_=ident[:], compare_op=ALU.not_equal, fill=1.0, base=0,
                                   pattern=[[-1, P]], channel_multiplier=1).then_inc(const_ready, 1)

            @block.vector
            def _(dve):
                done = [0]

                def then(ins):
                    done[0] += 1
                    ins.then_inc(setup_done, 1)
                    dve.wait_ge(setup_done, done[0])

                dve.wait_ge(edges_in, 16)
                src, dst, before, after, kind = (raw[:, j] for j in range(5))
                same = run_start
                dve.scalar_tensor_tensor(feat_idx[:], src, float(RELS), kind, ALU.mult, ALU.add)
                dve.scalar_tensor_tensor(er_idx[:], dst, float(RELS), kind, ALU.mult, ALU.add)
                dve.tensor_copy(dst_f[:], dst)
                then(dve.tensor_tensor(prev_mask[:], dst, before, ALU.is_equal))
                then(dve.tensor_tensor(next_mask[:], dst, after, ALU.is_equal))

                def cols(tile):
                    return tile[:].rearrange("p (t c) -> p t c", c=CHUNK_COLS)

                for mask, open_, pass_, run, edge, far, order in (
                        (prev_mask, prev_open, prev_pass, first_run, 0, CHUNK_COLS - 1, 1),
                        (next_mask, next_open, next_pass, last_run, CHUNK_COLS - 1, 0, -1)):
                    then(dve.tensor_scalar(open_[:], cols(mask)[:, :, edge], -1.0, BIG, ALU.add, ALU.mult))
                    then(dve.memset(cols(mask)[:, :, edge], 0.0))
                    then(dve.memset(same[:], 0.0))
                    then(dve.memset(cols(same)[:, :, edge], 1.0))
                    then(dve.tensor_tensor_scan(out=run[:, ::order], data0=mask[:, ::order], data1=same[:, ::order],
                                                initial=0.0, op0=ALU.mult, op1=ALU.max))
                    then(dve.tensor_scalar(run[:], run[:], -1.0, BIG, ALU.add, ALU.mult))
                    then(dve.tensor_tensor(pass_[:], cols(run)[:, :, far], open_[:], ALU.min))
                    then(dve.tensor_scalar(mask[:], mask[:], -1.0, BIG, ALU.add, ALU.mult))
                then(dve.memset(last_block[:], 0))
                then(dve.tensor_single_scalar(last_block[:, 1:CHUNKS + 1],
                                              dst.rearrange("p (t c) -> p t c", c=CHUNK_COLS)[:, :, CHUNK_COLS - 1],
                                              P.bit_length() - 1, ALU.arith_shift_right))

                dve.wait_ge(x_in, 16)
                n0 = done[0]
                with dve.Fori(0, NODE_TILES) as t:
                    dve.bn_stats(bn[:, ds(t, 1), :].rearrange("p o s -> p (o s)"),
                                 x_res[:, ds(t, 1), :].rearrange("p o d -> p (o d)")).then_inc(setup_done, 1)
                done[0] = n0 + NODE_TILES
                dve.wait_ge(setup_done, done[0])

                def variance(eps=EPS):
                    dve.tensor_tensor(ln_t[:], bn[:, :, 1], bn[:, :, 4], ALU.subtract)
                    dve.tensor_tensor(ln_u[:], bn[:, :, 2], bn[:, :, 5], ALU.add)
                    then(dve.tensor_tensor(ln_mean[:], bn[:, :, 1], bn[:, :, 4], ALU.add))
                    dve.tensor_scalar(ln_mean[:], ln_mean[:], 0.5, None, ALU.mult)
                    then(dve.tensor_tensor(ln_t[:], ln_t[:], ln_t[:], ALU.mult))
                    then(dve.tensor_scalar(ln_u[:], ln_u[:], 1.0 / DIM, eps, ALU.mult, ALU.add))
                    then(dve.scalar_tensor_tensor(ln_u[:], ln_t[:], 0.25, ln_u[:], ALU.mult, ALU.add))

                variance()
                var_count = done[0]
                dve.wait_ge(std_ready, 1)
                then(dve.reciprocal(ln_rstd[:], ln_rstd[:]))

                dve.wait_ge(conv_in, 32)
                dve.wait_ge(attn_in, 32)
                for k in range(2):
                    then(dve.tensor_tensor(prod[:], conv[:, k, :, 0:HEAD_DIM], attn[:, 0], ALU.mult))
                    then(dve.tensor_reduce(conv[:, k, :, HEAD_DIM], prod[:], AX.X, ALU.add))
                    then(dve.tensor_tensor(prod[:], conv[:, k, :, 0:HEAD_DIM], attn[:, 1], ALU.mult))
                    then(dve.tensor_reduce(conv_er[:, k], prod[:], AX.X, ALU.add))
                dve.memset(ln_t[:, 0:1], 0.0).then_inc(weights_done, 1)

                dve.sem_inc(feat_odd, 2)
                with dve.Fori(0, NODE_TILES // 2) as i:
                    for u in range(2):
                        t = i * 2 + u
                        dve.wait_ge(xt_psum, t + 1)
                        dve.tensor_scalar(xn[:, u], x_res[:, ds(t, 1), :].rearrange("p o d -> p (o d)"),
                                          ln_mean[:, ds(t, 1)], ln_rstd[:, ds(t, 1)],
                                          ALU.subtract, ALU.mult).then_inc(xn_ready, 1)
                        dve.wait_ge(store[u], 32 * i + 32)
                        for r in range(1, RELS, 2):
                            dve.wait_ge(feat_psum, RELS * t + r + 1)
                            dve.tensor_copy(table[:, u, r], psum[:, 2 + r % 4, 0:ROW]).then_inc(feat_odd, 1)
                assert var_count > 0

            @block.scalar
            def _(act):
                act.sem_inc(store[0], 32)
                act.sem_inc(store[1], 32)
                act.sem_inc(feat_even, 2)
                act.sem_inc(logits_out, 1)
                act.wait_ge(setup_done, VAR_COUNT)
                nc.scalar.activation(ln_rstd[:], ln_u[:], ACT.Sqrt).then_inc(std_ready, 1)
                with act.Fori(0, NODE_TILES // 2) as i:
                    for u in range(2):
                        t = i * 2 + u
                        act.wait_ge(xt_psum, t + 3)
                        nc.scalar.copy(xt[:, u], psum[:, u, 0:2 * P].rearrange("p (k n) -> p k n", k=2)).then_inc(xt_ready, 1)
                        act.wait_ge(store[u], 32 * i + 32)
                        for r in range(0, RELS, 2):
                            act.wait_ge(feat_psum, RELS * t + r + 1)
                            nc.scalar.copy(table[:, u, r], psum[:, 2 + r % 4, 0:ROW]).then_inc(feat_even, 1)
                        act.wait_ge(feat_psum, RELS * t + RELS)
                        nc.scalar.copy(er_tab[:, u], psum[:, 6, 0:RELS * HEADS]).then_inc(logits_out, 1)

            @block.tensor
            def _(pe):
                pe.sem_inc(xt_psum, 2)
                pe.wait_ge(const_ready, 5)
                with pe.Fori(0, NODE_TILES // 2) as i:
                    for u in range(2):
                        t = i * 2 + u
                        pe.wait_ge(xn_ready, t + 1)
                        for k in range(2):
                            last = nc.tensor.transpose(psum[:, u, k * P:(k + 1) * P], xn[:, u, k * P:(k + 1) * P], ident[:])
                        last.then_inc(xt_psum, 1)
                        pe.wait_ge(weights_done, 1)
                        pe.wait_ge(xt_ready, t + 1)
                        pe.wait_ge(logits_out, t + 1)
                        for k in range(2):
                            nc.tensor.matmul(psum[:, 6, 0:RELS * HEADS], xt[:, u, k], conv_er[:, k],
                                             start=(k == 0), stop=(k == 1))
                        for r in range(RELS):
                            pe.wait_ge(feat_odd if r % 2 else feat_even, 4 * t + r // 2 + 1)
                            for k in range(2):
                                last = nc.tensor.matmul(psum[:, 2 + r % 4, 0:ROW], xt[:, u, k],
                                                        conv[:, k, r * HEADS:(r + 1) * HEADS, :].rearrange("p h c -> p (h c)"),
                                                        start=(k == 0), stop=(k == 1))
                            last.then_inc(feat_psum, 1)

        mixw_in, bias_in = sem("mixw_in"), sem("bias_in")
        centre_done, xnb_ready, xtb_psum, xtb_ready = sem("centre_done"), sem("xnb_ready"), sem("xtb_psum"), sem("xtb_ready")
        kv_psum, squares_ready, var_ready, stdb_ready = sem("kv_psum"), sem("squares_ready"), sem("var_ready"), sem("stdb_ready")
        v_ready, k_ready, dots_psum, dots_added, rk_ready = sem("v_ready"), sem("k_ready"), sem("dots_psum"), sem("dots_added"), sem("rk_ready")
        wq_psum, wq_ready, g_psum, g_ready, eff_psum, eff_ready = (sem(n) for n in ("wq_psum", "wq_ready", "g_psum", "g_ready", "eff_psum", "eff_ready"))
        dots_masked, mix_psum, mix_added = sem("dots_masked"), sem("mix_psum"), sem("mix_added")
        PAIRS = MIX_HEADS // 2
        with ExitStack() as st:
            wqkv = sb("wqkv", [P, 2, 3 * INNER], f32, st)
            wout = sb("wout", [P, PAIRS, DIM], f32, st)
            bias = sb("bias", [P, 2, DIM], f32, st)
            bsum = sb("bsum", [P, DIM], f32, st)
            hmean = sb("hmean", [P, 2, 2 * MIX_HEADS], f32, st)
            xn = sb("xnb", [P, 2, DIM], f32, st)
            xt = sb("xtb", [P, 2, 2, P], f32, st)
            squares = sb("squares", [P, 2, INNER], f32, st)
            kv_var = sb("kv_var", [P, 2 * MIX_HEADS], f32, st)
            kv_prod = sb("kv_prod", [P, MIX_HEADS], f32, st)
            rk = sb("rk", [P, MIX_HEADS], f32, st)
            ks = sb("ks", [P, INNER], f32, st)
            vs = sb("vs", [P, INNER], f32, st)
            dots = sb("dots", [P, PAIRS, P], f32, st)
            dots_diag = sb("dots_diag", [P, PAIRS, P], f32, st)
            wqt = sb("wqt", [P, PAIRS, 2, P], f32, st)
            g = sb("g", [P, PAIRS, DIM], f32, st)
            eff = sb("eff", [P, 2, DIM], f32, st)
            mixt = sb("mixt", [P, DIM], f32, st)
            block = st.enter_context(nc.Block())

            @block.sync
            def _(sp):
                sp.dma_start(wqkv[:], a["wqkv"].rearrange("(k p) n -> p k n", p=P)).then_inc(mixw_in, 16)
                sp.dma_start(wout[:], a["wout"].rearrange("(k p) n -> p k n", p=P)).then_inc(mixw_in, 16)
                sp.dma_start(bias[:, 0], a["h_bias"].partition_broadcast(P)).then_inc(bias_in, 16)
                sp.dma_start(bias[:, 1], a["b_out"].partition_broadcast(P)).then_inc(bias_in, 16)

            @block.vector
            def _(dve):
                dve.wait_ge(mixw_in, 32)
                wkv = [wqkv[:, k, INNER:3 * INNER].rearrange("p (h d) -> p h d", d=MIX_DIM) for k in range(2)]
                for k in range(2):
                    dve.tensor_reduce(hmean[:, k], wkv[k], AX.X, ALU.add).then_inc(centre_done, 1)
                dve.wait_ge(centre_done, 2)
                dve.tensor_scalar(hmean[:], hmean[:], 1.0 / MIX_DIM, None, ALU.mult).then_inc(centre_done, 1)
                dve.wait_ge(centre_done, 3)
                for k in range(2):
                    dve.tensor_tensor(wkv[k], wkv[k], hmean[:, k].unsqueeze(2).to_broadcast([P, 2 * MIX_HEADS, MIX_DIM]),
                                      ALU.subtract).then_inc(centre_done, 1)
                dve.memset(dots[:], 0.0).then_inc(centre_done, 1)
                dve.memset(dots_diag[:], 0.0).then_inc(centre_done, 1)
                dve.wait_ge(bias_in, 32)
                dve.tensor_tensor(bsum[:], bias[:, 0], bias[:, 1], ALU.add).then_inc(centre_done, 1)
                dve.wait_ge(centre_done, 8)
                with dve.Fori(0, NODE_TILES // 2) as i:
                    for u in range(2):
                        t = i * 2 + u
                        dve.tensor_scalar(xn[:, u], x_res[:, ds(t, 1), :].rearrange("p o d -> p (o d)"),
                                          ln_mean[:, ds(t, 1)], ln_rstd[:, ds(t, 1)],
                                          ALU.subtract, ALU.mult).then_inc(xnb_ready, 1)
                        dve.wait_ge(squares_ready, 2 * t + 2)
                        dve.tensor_reduce(kv_var[:], squares[:].rearrange("p a (h d) -> p (a h) d", d=MIX_DIM), AX.X,
                                          ALU.add).then_inc(var_ready, 1)
                        dve.wait_ge(var_ready, 3 * t + 1)
                        dve.tensor_scalar(kv_var[:], kv_var[:], 1.0 / MIX_DIM, EPS, ALU.mult, ALU.add).then_inc(var_ready, 1)
                        dve.wait_ge(var_ready, 3 * t + 2)
                        dve.tensor_tensor(kv_prod[:], kv_var[:, 0:MIX_HEADS], kv_var[:, MIX_HEADS:], ALU.mult).then_inc(var_ready, 1)
                        dve.wait_ge(stdb_ready, t + 1)
                        dve.reciprocal(rk[:], rk[:]).then_inc(rk_ready, 1)
                        dve.wait_ge(rk_ready, t + 1)
                        dve.tensor_tensor(ks[:].rearrange("p (h d) -> p h d", d=MIX_DIM),
                                          psum[:, 2, :].rearrange("p (h d) -> p h d", d=MIX_DIM),
                                          rk[:].unsqueeze(2).to_broadcast([P, MIX_HEADS, MIX_DIM]), ALU.mult).then_inc(k_ready, 1)
                        dve.wait_ge(dots_psum, t + 1)
                        dve.tensor_tensor(dots[:].rearrange("p a b -> p (a b)"), dots[:].rearrange("p a b -> p (a b)"),
                                          psum[:, 4, :], ALU.add).then_inc(dots_added, 1)
                        dve.wait_ge(dots_added, t + 1)
                for lo in (0, MIX_DIM):
                    dve.tensor_scalar(dots_diag[lo:lo + MIX_DIM, :, lo:lo + MIX_DIM], dots[lo:lo + MIX_DIM, :, lo:lo + MIX_DIM],
                                      1.0 / NODES, None, ALU.mult).then_inc(dots_masked, 1)
                dve.wait_ge(g_psum, 1)
                dve.tensor_copy(g[:].rearrange("p a b -> p (a b)").rearrange("p (a b) -> p a b", a=2), psum[:, 5:7, :]).then_inc(g_ready, 1)
                dve.wait_ge(eff_psum, 1)
                dve.tensor_copy(eff[:].rearrange("p a b -> p (a b)"), psum[:, 7, :]).then_inc(eff_ready, 1)
                with dve.Fori(0, NODE_TILES // 2) as i:
                    for u in range(2):
                        t = i * 2 + u
                        x_t = x_res[:, ds(t, 1), :].rearrange("p o d -> p (o d)")
                        dve.tensor_scalar(xn[:, u], x_t, ln_mean[:, ds(t, 1)], ln_rstd[:, ds(t, 1)],
                                          ALU.subtract, ALU.mult).then_inc(xnb_ready, 1)
                        dve.wait_ge(mix_psum, t + 1)
                        dve.tensor_tensor(mixt[:], psum[:, 2 + u, 0:DIM], bsum[:], ALU.add).then_inc(mix_added, 1)
                        dve.wait_ge(mix_added, 2 * t + 1)
                        dve.tensor_tensor(x_t, x_t, mixt[:], ALU.add).then_inc(mix_added, 1)
                        dve.wait_ge(mix_added, 2 * t + 2)

            @block.scalar
            def _(act):
                with act.Fori(0, NODE_TILES // 2) as i:
                    for u in range(2):
                        t = i * 2 + u
                        act.wait_ge(xtb_psum, t + 1)
                        nc.scalar.copy(xt[:, u], psum[:, u, 0:2 * P].rearrange("p (k n) -> p k n", k=2)).then_inc(xtb_ready, 1)
                        act.wait_ge(kv_psum, t + 1)
                        for j in range(2):
                            nc.scalar.activation(squares[:, j], psum[:, 2 + j, :], ACT.Square).then_inc(squares_ready, 1)
                        nc.scalar.copy(vs[:], psum[:, 3, :]).then_inc(v_ready, 1)
                        act.wait_ge(var_ready, 3 * t + 3)
                        nc.scalar.activation(rk[:], kv_prod[:], ACT.Sqrt).then_inc(stdb_ready, 1)
                act.wait_ge(wq_psum, 1)
                nc.scalar.copy(wqt[:].rearrange("p a k n -> p (a k n)").rearrange("p (b n) -> p b n", b=2),
                               psum[:, 0:2, :]).then_inc(wq_ready, 1)
                with act.Fori(0, NODE_TILES // 2) as i:
                    for u in range(2):
                        t = i * 2 + u
                        act.wait_ge(xtb_psum, t + NODE_TILES + 1)
                        nc.scalar.copy(xt[:, u], psum[:, u, 0:2 * P].rearrange("p (k n) -> p k n", k=2)).then_inc(xtb_ready, 1)

            @block.tensor
            def _(pe):
                pe.wait_ge(centre_done, 8)
                with pe.Fori(0, NODE_TILES // 2) as i:
                    for u in range(2):
                        t = i * 2 + u
                        pe.wait_ge(xnb_ready, t + 1)
                        for k in range(2):
                            last = nc.tensor.transpose(psum[:, u, k * P:(k + 1) * P], xn[:, u, k * P:(k + 1) * P], ident[:])
                        last.then_inc(xtb_psum, 1)
                        pe.wait_ge(xtb_ready, t + 1)
                        for j in range(2):
                            for k in range(2):
                                last = nc.tensor.matmul(psum[:, 2 + j, :], xt[:, u, k], wqkv[:, k, (1 + j) * INNER:(2 + j) * INNER],
                                                        start=(k == 0), stop=(k == 1))
                        last.then_inc(kv_psum, 1)
                        pe.wait_ge(v_ready, t + 1)
                        pe.wait_ge(k_ready, t + 1)
                        for j in range(PAIRS):
                            last = nc.tensor.matmul(psum[:, 4, j * P:(j + 1) * P], vs[:, j * P:(j + 1) * P], ks[:, j * P:(j + 1) * P],
                                                    start=True, stop=True)
                        last.then_inc(dots_psum, 1)
                for j in range(PAIRS):
                    for k in range(2):
                        n = (2 * j + k) * P
                        last = nc.tensor.transpose(psum[:, n // 512, n % 512:n % 512 + P], wqkv[:, k, j * P:(j + 1) * P], ident[:])
                last.then_inc(wq_psum, 1)
                pe.wait_ge(dots_masked, 2)
                for j in range(PAIRS):
                    n = j * DIM
                    last = nc.tensor.matmul(psum[:, 5 + n // 512, n % 512:n % 512 + DIM], dots_diag[:, j], wout[:, j], start=True, stop=True)
                last.then_inc(g_psum, 1)
                pe.wait_ge(wq_ready, 1)
                pe.wait_ge(g_ready, 1)
                for k in range(2):
                    for j in range(PAIRS):
                        last = nc.tensor.matmul(psum[:, 7, k * DIM:(k + 1) * DIM], wqt[:, j, k], g[:, j],
                                                start=(j == 0), stop=(j == PAIRS - 1))
                last.then_inc(eff_psum, 1)
                pe.wait_ge(eff_ready, 1)
                with pe.Fori(0, NODE_TILES // 2) as i:
                    for u in range(2):
                        t = i * 2 + u
                        pe.wait_ge(xnb_ready, t + NODE_TILES + 1)
                        for k in range(2):
                            last = nc.tensor.transpose(psum[:, u, k * P:(k + 1) * P], xn[:, u, k * P:(k + 1) * P], ident[:])
                        last.then_inc(xtb_psum, 1)
                        pe.wait_ge(xtb_ready, t + NODE_TILES + 1)
                        for k in range(2):
                            last = nc.tensor.matmul(psum[:, 2 + u, 0:DIM], xt[:, u, k], eff[:, k], start=(k == 0), stop=(k == 1))
                        last.then_inc(mix_psum, 1)

        PREP = 15
        gathered = [sem("gathered0"), sem("gathered1")]
        idx_staged, chunk_free, prep = sem("idx_staged"), sem("chunk_free"), sem("prep")
        tails_psum, masks_copied, carries_psum, exp_ready = sem("tails_psum"), sem("masks_copied"), sem("carries_psum"), sem("exp_ready")
        onehot_ready, sums_psum, acc_step = sem("onehot_ready"), sem("sums_psum"), sem("acc_step")
        main_init = sem("main_init")
        tail = ExitStack()
        acc = sb("acc", [P, NODE_TILES, HEADS, HEAD_COLS])
        with ExitStack() as st:
            rows = sb("rows", [P, 2, CHUNK_COLS, ROW], f32, st)
            er = sb("er", [P, 2, CHUNK_COLS, HEADS], f32, st)
            idx_now = sb("idx_now", [P, 2, 2, CHUNK_COLS], i32, st)
            onehot = sb("onehot", [P, CHUNK_COLS, P], f32, st)
            e = sb("e", [P, CE], f32, st)
            lin = sb("lin", [P, CE], f32, st)
            mask_f = sb("mask_f", [P, CE], f32, st)
            mask_b = sb("mask_b", [P, CE], f32, st)
            max_f = sb("max_f", [P, CE], f32, st)
            max_b = sb("max_b", [P, CE], f32, st)
            seg_max = sb("seg_max", [P, CE], f32, st)
            reach = sb("reach", [P, CE], f32, st)
            pass_now = sb("pass_now", [P, 2, HEADS], f32, st)
            pass_t = sb("pass_t", [HEADS, 2 * P], f32, st)
            carry_f = sb("carry_f", [HEADS, 2, P + 1], f32, st)
            carry_b = sb("carry_b", [HEADS, P + 1], f32, st)
            from_prev = sb("from_prev", [P, HEADS], f32, st)
            from_next = sb("from_next", [P, HEADS], f32, st)
            arg = sb("arg", [P, CE + HEADS], f32, st)
            ex = sb("ex", [P, CE + HEADS], f32, st)
            decay = sb("decay", [1, HEADS], f32, st)
            factor = sb("factor", [P, HEADS], f32, st)
            scaled = sb("scaled", [P, HEADS, HEAD_COLS], f32, st)
            block = st.enter_context(nc.Block())
            GATHER_INCS = 16 * 2 * CHUNK_COLS

            @block.gpsimd
            def _(pool):
                pool.sem_inc(chunk_free, 2)
                with pool.Fori(0, CHUNKS // 2) as i:
                    for u in range(2):
                        t = i * 2 + u
                        pool.wait_ge(chunk_free, t + 1)
                        pool.tensor_copy(idx_now[:, u, 0], feat_idx[:, ds(t * CHUNK_COLS, CHUNK_COLS)]).then_inc(idx_staged, 1)
                        pool.tensor_copy(idx_now[:, u, 1], er_idx[:, ds(t * CHUNK_COLS, CHUNK_COLS)]).then_inc(idx_staged, 1)
                        pool.wait_ge(idx_staged, 2 * t + 2)
                        pool.sem_inc(staged_seen, 1)
                        for c in range(CHUNK_COLS):
                            pool.indirect_dma_start(out=er[:, u, c], out_offset=None, in_=dst_logits,
                                                    in_offset=bass.IndirectOffsetOnAxis(ap=idx_now[:, u, 1, c:c + 1], axis=0),
                                                    bounds_check=NODES_PAD * RELS - 1, oob_is_err=True).then_inc(gathered[u], 16)
                            pool.indirect_dma_start(out=rows[:, u, c], out_offset=None, in_=features,
                                                    in_offset=bass.IndirectOffsetOnAxis(ap=idx_now[:, u, 0, c:c + 1], axis=0),
                                                    bounds_check=NODES_PAD * RELS - 1, oob_is_err=True).then_inc(gathered[u], 16)

            def hc(tile, n=CE):
                return tile[:, 0:n].rearrange("p (h c) -> p h c", h=HEADS)

            def by_head(edge_data, t):
                return edge_data[:, ds(t * CHUNK_COLS, CHUNK_COLS)].unsqueeze(1).to_broadcast([P, HEADS, CHUNK_COLS])

            @block.vector
            def _(dve):
                dve.memset(acc[:], 0.0).then_inc(main_init, 1)
                dve.memset(carry_f[:], -BIG).then_inc(main_init, 1)
                dve.memset(carry_b[:], -BIG).then_inc(main_init, 1)
                dve.wait_ge(main_init, 3)
                dve.sem_inc(acc_step, 1)
                with dve.Fori(0, CHUNKS // 2) as i:
                    for u in range(2):
                        t = i * 2 + u

                        def after(n):
                            dve.wait_ge(prep, PREP * t + n)

                        first = dve.value_load(last_block[P - 1:P, ds(t, 1)], min_val=0, max_val=NODE_TILES - 1)
                        last_b = dve.value_load(last_block[P - 1:P, ds(t + 1, 1)], min_val=0, max_val=NODE_TILES - 1)
                        dve.tensor_copy(hc(mask_f), by_head(prev_mask, t))
                        dve.tensor_copy(hc(mask_b), by_head(next_mask, t))
                        dve.tensor_copy(pass_now[:, 0], prev_pass[:, ds(t, 1)].to_broadcast([P, HEADS]))
                        dve.tensor_copy(pass_now[:, 1], next_pass[:, ds(t, 1)].to_broadcast([P, HEADS])).then_inc(prep, 1)
                        dve.wait_ge(gathered[u], i * GATHER_INCS + GATHER_INCS)
                        dve.tensor_tensor(hc(lin), rows[:, u, :, HEAD_DIM::HEAD_COLS].rearrange("p c h -> p h c"),
                                          er[:, u].rearrange("p c h -> p h c"), ALU.add).then_inc(prep, 1)
                        after(2)
                        dve.scalar_tensor_tensor(e[:], lin[:], SLOPE, lin[:], ALU.mult, ALU.max).then_inc(prep, 1)
                        after(3)
                        dve.tensor_tensor_scan(out=max_f[:], data0=mask_f[:], data1=e[:], initial=-BIG, op0=ALU.add, op1=ALU.max)
                        dve.tensor_tensor_scan(out=max_b[:, ::-1], data0=mask_b[:, ::-1], data1=e[:, ::-1], initial=-BIG,
                                               op0=ALU.add, op1=ALU.max).then_inc(prep, 1)
                        after(4)
                        dve.tensor_tensor(seg_max[:], max_f[:], max_b[:], ALU.max).then_inc(prep, 1)
                        dve.wait_ge(masks_copied, t + 1)
                        dve.tensor_tensor_scan(out=carry_f[:, u, 1:P + 1], data0=pass_t[:, 0:P], data1=psum[0:HEADS, 0, 0:P],
                                               initial=carry_f[:, 1 - u, P:P + 1], op0=ALU.add, op1=ALU.max)
                        dve.tensor_tensor_scan(out=carry_b[:, 0:P][:, ::-1],
                                               data0=pass_t[:, P:2 * P][:, ::-1], data1=psum[0:HEADS, 0, P:2 * P][:, ::-1],
                                               initial=-BIG, op0=ALU.add, op1=ALU.max).then_inc(prep, 1)
                        dve.wait_ge(carries_psum, t + 1)
                        dve.tensor_scalar(from_prev[:], psum[:, 1, 0:HEADS], prev_open[:, ds(t, 1)], None, ALU.add)
                        dve.tensor_scalar(from_next[:], psum[:, 1, HEADS:2 * HEADS], next_open[:, ds(t, 1)], None, ALU.add).then_inc(prep, 1)
                        after(7)
                        dve.tensor_tensor(hc(reach), by_head(first_run, t),
                                          from_prev[:].unsqueeze(2).to_broadcast([P, HEADS, CHUNK_COLS]), ALU.add).then_inc(prep, 1)
                        after(8)
                        dve.tensor_tensor(seg_max[:], seg_max[:], reach[:], ALU.max).then_inc(prep, 1)
                        after(9)
                        dve.tensor_tensor(hc(reach), by_head(last_run, t),
                                          from_next[:].unsqueeze(2).to_broadcast([P, HEADS, CHUNK_COLS]), ALU.add).then_inc(prep, 1)
                        after(10)
                        dve.tensor_tensor(seg_max[:], seg_max[:], reach[:], ALU.max).then_inc(prep, 1)
                        after(11)
                        dve.tensor_tensor(arg[:, 0:CE], e[:], seg_max[:], ALU.subtract)
                        dve.tensor_tensor(arg[:, CE:], from_prev[:], hc(seg_max)[:, :, 0], ALU.subtract).then_inc(prep, 1)
                        dve.wait_ge(exp_ready, t + 1)
                        dve.tensor_scalar(decay[:], ex[0:1, CE:], -1.0, None, ALU.add).then_inc(prep, 1)
                        row4 = rows[:, u].rearrange("p c (h d) -> p c h d", d=HEAD_COLS)
                        dve.tensor_tensor(row4, row4, hc(ex).rearrange("p h c -> p c h").unsqueeze(3).to_broadcast(
                            [P, CHUNK_COLS, HEADS, HEAD_COLS]), ALU.mult).then_inc(prep, 1)
                        after(14)
                        dve.tensor_copy(row4[:, :, :, HEAD_DIM], hc(ex).rearrange("p h c -> p c h")).then_inc(prep, 1)
                        with dve.Fori(first, last_b + 1) as b:
                            s = t + b
                            dve.scalar_tensor_tensor(onehot[:], iota_free[:].unsqueeze(1).to_broadcast([P, CHUNK_COLS, P]),
                                                     block_base[:, ds(b, 1)],
                                                     dst_f[:, ds(t * CHUNK_COLS, CHUNK_COLS)].unsqueeze(2).to_broadcast([P, CHUNK_COLS, P]),
                                                     ALU.add, ALU.is_equal).then_inc(onehot_ready, 1)
                            dve.wait_ge(sums_psum, s + 1)
                            dve.wait_ge(acc_step, 3 * s + 1)
                            dve.tensor_scalar(factor[:], psum[:, 3, 0:HEADS], 1.0, None, ALU.add).then_inc(acc_step, 1)
                            dve.wait_ge(acc_step, 3 * s + 2)
                            acc_b = acc[:, ds(b, 1)].rearrange("p o h c -> p (o h) c")
                            dve.tensor_tensor(scaled[:], acc_b, factor[:].unsqueeze(2).to_broadcast([P, HEADS, HEAD_COLS]),
                                              ALU.mult).then_inc(acc_step, 1)
                            dve.wait_ge(acc_step, 3 * s + 3)
                            dve.tensor_tensor(acc_b, scaled[:], psum[:, 2, 0:ROW].rearrange("p (h c) -> p h c", h=HEADS),
                                              ALU.add).then_inc(acc_step, 1)
                        dve.tensor_copy(carry_f[:, 1 - u, 0:1], carry_f[:, u, P:P + 1]).then_inc(chunk_free, 1)

            @block.scalar
            def _(act):
                with act.Fori(0, CHUNKS // 2) as i:
                    for u in range(2):
                        t = i * 2 + u
                        act.wait_ge(tails_psum, t + 1)
                        nc.scalar.copy(pass_t[:], psum[0:HEADS, 0, 2 * P:4 * P]).then_inc(masks_copied, 1)
                        act.wait_ge(prep, PREP * t + 12)
                        nc.scalar.activation(ex[:], arg[:], ACT.Exp).then_inc(exp_ready, 1)

            @block.tensor
            def _(pe):
                with pe.Fori(0, CHUNKS // 2) as i:
                    for u in range(2):
                        t = i * 2 + u
                        pe.wait_ge(prep, PREP * t + 4)
                        for j, tile in enumerate((hc(max_f)[:, :, CHUNK_COLS - 1], hc(max_b)[:, :, 0], pass_now[:, 0], pass_now[:, 1])):
                            last = nc.tensor.matmul(psum[0:HEADS, 0, j * P:(j + 1) * P], tile, ident[:], start=True, stop=True)
                        last.then_inc(tails_psum, 1)
                        pe.wait_ge(prep, PREP * t + 6)
                        nc.tensor.matmul(psum[:, 1, 0:HEADS], carry_f[:, u, 0:P], ident[0:HEADS, 0:HEADS], start=True, stop=True)
                        nc.tensor.matmul(psum[:, 1, HEADS:2 * HEADS], carry_b[:, 1:P + 1], ident[0:HEADS, 0:HEADS],
                                         start=True, stop=True).then_inc(carries_psum, 1)
                        first = pe.value_load(last_block[P - 1:P, ds(t, 1)], min_val=0, max_val=NODE_TILES - 1)
                        last_b = pe.value_load(last_block[P - 1:P, ds(t + 1, 1)], min_val=0, max_val=NODE_TILES - 1)
                        with pe.Fori(first, last_b + 1) as b:
                            pe.wait_ge(onehot_ready, t + b + 1)
                            nc.tensor.matmul(psum[:, 3, 0:HEADS], onehot[0:1, 0, :], decay[:], start=True, stop=True)
                            for c in range(CHUNK_COLS):
                                last = nc.tensor.matmul(psum[:, 2, 0:ROW], onehot[:, c], rows[:, u, c],
                                                        start=(c == 0), stop=(c == CHUNK_COLS - 1))
                            last.then_inc(sums_psum, 1)

        tail_step, ln2_std, wts_in, small_in = sem("tail_step"), sem("ln2_std"), sem("wts_in"), sem("small_in")
        wT_psum, wT_ready, w_stored, w_row_in = sem("wT_psum"), sem("wT_ready"), sem("w_stored"), sem("w_row_in")
        xf_staged, xf_psum, xf_ready = sem("xf_staged"), sem("xf_psum"), sem("xf_ready")
        h_psum, h_ready, y_psum, y_ready, ones_ready, ranked = (sem(n) for n in ("h_psum", "h_ready", "y_psum", "y_ready", "ones_ready", "ranked"))
        out_ready, out_stored = sem("out_ready"), [sem("out_stored0"), sem("out_stored1")]
        with ExitStack() as st:
            w1 = sb("w1", [P, 2, HIDDEN], f32, st)
            w2 = sb("w2", [P, HID_TILES, DIM], f32, st)
            b1 = sb("b1", [P, HID_TILES], f32, st)
            wr = sb("wr", [P, DIM], f32, st)
            br = sb("br", [P, 1], f32, st)
            b2 = sb("b2", [1, DIM], f32, st)
            ones = sb("ones", [1, P], f32, st)
            rden = sb("rden", [P, NODE_TILES * HEADS], f32, st)
            y_all = sb("y_all", [P, NODE_TILES, DIM], f32, st)
            weight = sb("weight", [P, NODE_TILES], f32, st)
            weight_t = sb("weight_t", [NODE_TILES, P], f32, st)
            w_row = sb("w_row", [P, NODES], f32, st)
            junk = sb("junk", [P, 2, NODES], bf16, st)
            lower = sb("lower", [P, P], f32, st)
            count = sb("count", [P, 3, NODE_TILES], f32, st)
            chosen = sb("chosen", [P, NODE_TILES], f32, st)
            xf = sb("xf", [P, GROUP_TILES, DIM], f32, st)
            xft = sb("xft", [P, 2, GROUP_TOKENS], f32, st)
            hid = sb("hid", [P, HID_TILES, GROUP_TOKENS], f32, st)
            out_t = sb("out_t", [P, 2, DIM], f32, st)
            xn2 = acc[:].rearrange("p t h c -> p (t h c)")[:, 0:NODE_TILES * DIM].rearrange("p (t d) -> p t d", d=DIM)
            flat_x = x_res[:].rearrange("p t d -> p (t d)")
            block = st.enter_context(nc.Block())

            @block.sync
            def _(sp):
                sp.dma_start(wr[:], a["wr"].partition_broadcast(P)).then_inc(small_in, 16)
                sp.dma_start(br[:], a["br"].partition_broadcast(P)).then_inc(small_in, 16)
                sp.dma_start(b1[:], a["b1"]).then_inc(small_in, 16)
                sp.dma_start(b2[:], a["b2"]).then_inc(small_in, 16)
                sp.dma_start(w1[:], a["w1"].rearrange("(k p) n -> p k n", p=P)).then_inc(wts_in, 16)
                sp.dma_start(w2[:], a["w2"].rearrange("(k p) n -> p k n", p=P)).then_inc(wts_in, 16)
                sp.wait_ge(wT_ready, 1)
                sp.dma_start(node_weights, weight_t[:]).then_inc(w_stored, 16)
                sp.wait_ge(w_stored, 16)
                sp.dma_start(w_row[:], node_weights.rearrange("t p -> (t p)")[0:NODES].partition_broadcast(P)).then_inc(w_row_in, 16)
                for t in range(NODE_TILES):
                    n = min(P, NODES - t * P)
                    sp.wait_ge(out_ready, t + 1)
                    sp.dma_start(out[t * P:t * P + n, :], out_t[0:n, t % 2]).then_inc(out_stored[t % 2], 16)
                sp.wait_ge(out_stored[0], 16 * NODE_TILES // 2 + 16)
                sp.wait_ge(out_stored[1], 16 * NODE_TILES // 2 + 16)

            @block.gpsimd
            def _(pool):
                pool.memset(ones[:], 1.0).then_inc(ones_ready, 1)
                pool.memset(lower[:], 1.0).then_inc(ones_ready, 1)
                pool.wait_ge(ones_ready, 2)
                pool.affine_select(out=lower[:], in_=lower[:], compare_op=ALU.is_gt, fill=0.0, base=0,
                                   pattern=[[-1, P]], channel_multiplier=1).then_inc(ones_ready, 1)

            @block.vector
            def _(dve):
                done = [0]

                def then(ins):
                    done[0] += 1
                    ins.then_inc(tail_step, 1)
                    dve.wait_ge(tail_step, done[0])

                dve.sem_inc(out_stored[0], 16)
                dve.sem_inc(out_stored[1], 16)
                heads = acc[:].rearrange("p t h c -> p (t h) c")
                then(dve.tensor_scalar(rden[:], heads[:, :, HEAD_DIM], 1e-30, None, ALU.max))
                then(dve.reciprocal(rden[:], rden[:]))
                then(dve.tensor_tensor(heads[:, :, 0:HEAD_DIM], heads[:, :, 0:HEAD_DIM],
                                       rden[:].unsqueeze(2).to_broadcast([P, NODE_TILES * HEADS, HEAD_DIM]), ALU.mult))
                x_heads = flat_x.rearrange("p (t d) -> p t d", d=HEAD_DIM)
                then(dve.tensor_tensor(x_heads, x_heads, heads[:, :, 0:HEAD_DIM], ALU.add))
                n0 = done[0]
                with dve.Fori(0, NODE_TILES) as t:
                    dve.bn_stats(bn[:, ds(t, 1), :].rearrange("p o s -> p (o s)"),
                                 x_res[:, ds(t, 1), :].rearrange("p o d -> p (o d)")).then_inc(tail_step, 1)
                done[0] = n0 + NODE_TILES
                dve.wait_ge(tail_step, done[0])
                dve.tensor_tensor(ln_t[:], bn[:, :, 1], bn[:, :, 4], ALU.subtract)
                dve.tensor_tensor(ln_u[:], bn[:, :, 2], bn[:, :, 5], ALU.add)
                then(dve.tensor_tensor(ln_mean[:], bn[:, :, 1], bn[:, :, 4], ALU.add))
                dve.tensor_scalar(ln_mean[:], ln_mean[:], 0.5, None, ALU.mult)
                then(dve.tensor_tensor(ln_t[:], ln_t[:], ln_t[:], ALU.mult))
                then(dve.tensor_scalar(ln_u[:], ln_u[:], 1.0 / DIM, EPS, ALU.mult, ALU.add))
                then(dve.scalar_tensor_tensor(ln_u[:], ln_t[:], 0.25, ln_u[:], ALU.mult, ALU.add))
                assert done[0] == TAIL_VAR_COUNT, done[0]
                dve.wait_ge(ln2_std, 1)
                then(dve.reciprocal(ln_rstd[:], ln_rstd[:]))
                n0 = done[0]
                with dve.Fori(0, NODE_TILES) as t:
                    dve.tensor_scalar(xn2[:, ds(t, 1), :].rearrange("p o d -> p (o d)"),
                                      x_res[:, ds(t, 1), :].rearrange("p o d -> p (o d)"),
                                      ln_mean[:, ds(t, 1)], ln_rstd[:, ds(t, 1)], ALU.subtract, ALU.mult).then_inc(tail_step, 1)
                done[0] = n0 + NODE_TILES
                dve.wait_ge(tail_step, done[0])
                assert done[0] == TAIL_XN_COUNT, done[0]
                dve.wait_ge(small_in, 64)
                then(dve.tensor_tensor(y_all[:], xn2, wr[:].unsqueeze(1).to_broadcast([P, NODE_TILES, DIM]), ALU.mult))
                then(dve.tensor_reduce(weight[:], y_all[:], AX.X, ALU.add))
                then(dve.tensor_scalar(weight[:], weight[:], br[:], None, ALU.add))
                assert done[0] == TAIL_WEIGHT_COUNT, done[0]
                then(dve.tensor_tensor(x_res[:], x_res[:], xn2, ALU.add))
                dve.wait_ge(w_row_in, 16)
                dve.wait_ge(ones_ready, 3)
                then(dve.memset(count[:], 0.0))
                for t in range(NODE_TILES):
                    lo, hi = t * P, min((t + 1) * P, NODES)
                    w_t = weight[:, t:t + 1]
                    if t:
                        dve.tensor_scalar(junk[:, 0, 0:lo], w_row[:, 0:lo], w_t, None, ALU.is_ge, ALU.add,
                                          accum_out=count[:, 0, t:t + 1])
                    dve.tensor_scalar(junk[:, 0, lo:NODES], w_row[:, lo:NODES], w_t, None, ALU.is_gt, ALU.add,
                                      accum_out=count[:, 1, t:t + 1])
                    then(dve.scalar_tensor_tensor(junk[:, 1, 0:hi - lo], w_row[:, lo:hi], w_t, lower[:, 0:hi - lo],
                                                  ALU.is_equal, ALU.mult, accum_out=count[:, 2, t:t + 1]))
                then(dve.tensor_tensor(count[:, 0], count[:, 0], count[:, 1], ALU.add))
                then(dve.tensor_tensor(count[:, 0], count[:, 0], count[:, 2], ALU.add))
                then(dve.tensor_scalar(chosen[:], count[:, 0], float(SELECTED), None, ALU.is_lt))
                then(dve.tensor_tensor(chosen[:], chosen[:], weight[:], ALU.mult))
                with dve.Fori(0, NODE_TILES // 2) as i:
                    for u in range(2):
                        t = i * 2 + u
                        dve.wait_ge(y_ready, t + 1)
                        dve.wait_ge(out_stored[u], 16 * i + 16)
                        dve.scalar_tensor_tensor(out_t[:, u], y_all[:, ds(t, 1), :].rearrange("p o d -> p (o d)"),
                                                 chosen[:, ds(t, 1)], x_res[:, ds(t, 1), :].rearrange("p o d -> p (o d)"),
                                                 ALU.mult, ALU.add).then_inc(out_ready, 1)

            @block.scalar
            def _(act):
                act.wait_ge(tail_step, TAIL_VAR_COUNT)
                nc.scalar.activation(ln_rstd[:], ln_u[:], ACT.Sqrt).then_inc(ln2_std, 1)
                act.wait_ge(wT_psum, 1)
                nc.scalar.copy(weight_t[:], psum[0:NODE_TILES, 7, 0:P]).then_inc(wT_ready, 1)
                act.wait_ge(wts_in, 32)
                with act.Fori(0, GROUPS) as g:
                    for j in range(GROUP_TILES):
                        nc.scalar.copy(xf[:, j], xn2[:, ds(g * GROUP_TILES + j, 1), :].rearrange("p o d -> p (o d)")).then_inc(xf_staged, 1)
                    for j in range(GROUP_TILES):
                        act.wait_ge(xf_psum, GROUP_TILES * g + j + 1)
                        nc.scalar.copy(xft[:, :, j * P:(j + 1) * P], psum[:, j % 2, 0:2 * P].rearrange("p (k n) -> p k n", k=2)).then_inc(xf_ready, 1)
                    for c in range(HID_TILES):
                        act.wait_ge(h_psum, HID_TILES * g + c + 1)
                        nc.scalar.activation(hid[:, c], psum[:, 2 + c % 2, 0:GROUP_TOKENS], ACT.Gelu_apprx_tanh,
                                             bias=b1[:, c:c + 1]).then_inc(h_ready, 1)
                    for j in range(GROUP_TILES):
                        act.wait_ge(y_psum, GROUP_TILES * g + j + 1)
                        nc.scalar.copy(y_all[:, ds(g * GROUP_TILES + j, 1), :].rearrange("p o d -> p (o d)"),
                                       psum[:, 4 + j % 2, 0:DIM]).then_inc(y_ready, 1)

            @block.tensor
            def _(pe):
                pe.wait_ge(tail_step, TAIL_WEIGHT_COUNT)
                nc.tensor.matmul(psum[0:NODE_TILES, 7, 0:P], weight[:], ident[:], start=True, stop=True).then_inc(wT_psum, 1)
                pe.wait_ge(wts_in, 32)
                pe.wait_ge(small_in, 64)
                pe.wait_ge(ones_ready, 3)
                with pe.Fori(0, GROUPS) as g:
                    for j in range(GROUP_TILES):
                        pe.wait_ge(xf_staged, GROUP_TILES * g + j + 1)
                        if j == 2:
                            pe.wait_ge(xf_ready, GROUP_TILES * g + 1)
                        for k in range(2):
                            last = nc.tensor.transpose(psum[:, j % 2, k * P:(k + 1) * P], xf[:, j, k * P:(k + 1) * P], ident[:])
                        last.then_inc(xf_psum, 1)
                    pe.wait_ge(xf_ready, GROUP_TILES * g + GROUP_TILES)
                    for c in range(HID_TILES):
                        if c >= 2:
                            pe.wait_ge(h_ready, HID_TILES * g + c - 1)
                        for k in range(2):
                            last = nc.tensor.matmul(psum[:, 2 + c % 2, 0:GROUP_TOKENS], w1[:, k, c * P:(c + 1) * P], xft[:, k],
                                                    start=(k == 0), stop=(k == 1))
                        last.then_inc(h_psum, 1)
                    pe.wait_ge(h_ready, HID_TILES * g + HID_TILES)
                    for j in range(GROUP_TILES):
                        if j == 2:
                            pe.wait_ge(y_ready, GROUP_TILES * g + 1)
                        nc.tensor.matmul(psum[:, 4 + j % 2, 0:DIM], ones[:], b2[:], start=True, stop=False)
                        for c in range(HID_TILES):
                            last = nc.tensor.matmul(psum[:, 4 + j % 2, 0:DIM], hid[:, c, j * P:(j + 1) * P], w2[:, c],
                                                    start=False, stop=(c == HID_TILES - 1))
                        last.then_inc(y_psum, 1)


VAR_COUNT = 2 + 16 + 2 + NODE_TILES + 4
TAIL_VAR_COUNT = 4 + NODE_TILES + 4
TAIL_XN_COUNT = TAIL_VAR_COUNT + 1 + NODE_TILES
TAIL_WEIGHT_COUNT = TAIL_XN_COUNT + 3


def kernel(x, src, dst, edge_type_8, L0_gnn_conv_weights, L0_gnn_attn_l, L0_gnn_attn_r, L0_gnn_h_bias,
           L0_mix_w_qkv, L0_mix_w_out, L0_mix_b_out, L0_ffn_attention_mask, L0_ffn_wr, L0_ffn_br,
           L0_ffn_w1, L0_ffn_b1, L0_ffn_w2, L0_ffn_b2):
    import numpy as np
    import concourse.bacc as bacc
    from concourse.bass_utils import run_bass_kernel_spmd as run

    def chunks(values, fill):
        padded = np.full(EDGES_PAD, fill, values.dtype)
        padded[:EDGES] = values
        return padded

    def lay(padded):
        return padded.reshape(CHUNKS, P, CHUNK_COLS).transpose(1, 0, 2).reshape(P, -1)

    src, dst, kind = (np.asarray(v) for v in (src, dst, edge_type_8))
    dst_pad = chunks(dst, NODES_PAD - 1)
    before = np.concatenate([np.full(1, -1, dst.dtype), dst_pad[:-1]])
    after = np.concatenate([dst_pad[1:], np.full(1, -1, dst.dtype)])
    x = np.asarray(x)
    x_pad = np.zeros((NODES_PAD, DIM), x.dtype)
    x_pad[:NODES] = x
    arrays = {
        "edges": np.stack([lay(v) for v in (chunks(src, NODES_PAD - 1), dst_pad, before, after, chunks(kind, 0))], 1),
        "x": x_pad,
        "conv": np.asarray(L0_gnn_conv_weights),
        "attn_l": np.asarray(L0_gnn_attn_l), "attn_r": np.asarray(L0_gnn_attn_r),
        "h_bias": np.asarray(L0_gnn_h_bias), "b_out": np.asarray(L0_mix_b_out),
        "wqkv": np.asarray(L0_mix_w_qkv), "wout": np.asarray(L0_mix_w_out),
        "wr": np.asarray(L0_ffn_wr).reshape(DIM), "br": np.asarray(L0_ffn_br),
        "w1": np.asarray(L0_ffn_w1), "w2": np.asarray(L0_ffn_w2),
        "b1": np.asarray(L0_ffn_b1).reshape(HID_TILES, P).T, "b2": np.asarray(L0_ffn_b2).reshape(1, DIM),
    }
    nc = bacc.Bacc("TRN2", target_bir_lowering=False, num_devices=1)
    arrays = {f"in_{k}": np.ascontiguousarray(v) for k, v in arrays.items()}
    aps = {k[3:]: nc.dram_tensor(k, v.shape, mybir.dt.from_np(v.dtype), kind="ExternalInput").ap() for k, v in arrays.items()}
    out = nc.dram_tensor("out", (NODES, DIM), mybir.dt.float32, kind="ExternalOutput").ap()
    gps_layer(nc, aps, out)
    r = run(nc, [arrays], core_ids=[0])
    return r.results[0]["out"]
```

```python
import concourse.bass as bass
from concourse import mybir
from contextlib import ExitStack

NODES, DIM = 3750, 256
P = 128
NODE_TILES = -(-NODES // P)
NODES_PAD = NODE_TILES * P
RELS, HEADS, HEAD_DIM = 8, 4, 64
HEAD_COLS = HEAD_DIM + 1
ROW = HEADS * HEAD_COLS
EDGES = 120000
CHUNK_COLS = 15
SLOTS = 3
CHUNK_EDGES = P * CHUNK_COLS
CHUNKS = -(-EDGES // CHUNK_EDGES)
EDGES_PAD = CHUNKS * CHUNK_EDGES
CE = CHUNK_COLS * HEADS
MIX_HEADS, MIX_DIM = 8, 64
INNER = MIX_HEADS * MIX_DIM
HIDDEN = 4 * DIM
HID_TILES = HIDDEN // P
SELECTED = NODES // 2 - 1
GROUP_TILES = 3
GROUPS = NODE_TILES // GROUP_TILES
GROUP_TOKENS = GROUP_TILES * P
ITERS = CHUNKS // SLOTS
KV_ITERS = NODE_TILES // 2
MIX_ITERS = ITERS - KV_ITERS
MIX_TILES = NODE_TILES // MIX_ITERS
SEARCH_ROW = 504
SEARCH_ROWS = EDGES_PAD // SEARCH_ROW
PART_EDGES = EDGES_PAD // P
PIECE = 105
PIECES = PART_EDGES // PIECE
EPS = 1e-5
SLOPE = 0.2
BIG = 1e38
assert CHUNKS % SLOTS == 0 and NODE_TILES % 2 == 0 and NODE_TILES % GROUP_TILES == 0
assert MIX_ITERS * MIX_TILES == NODE_TILES and MIX_TILES <= 2 * SLOTS
assert SEARCH_ROW * SEARCH_ROWS == EDGES_PAD and PART_EDGES * P == EDGES_PAD and PIECE * PIECES == PART_EDGES


def gps_layer(nc, a, out):
    f32, i32, bf16 = mybir.dt.float32, mybir.dt.int32, mybir.dt.bfloat16
    ALU, ACT, AX = mybir.AluOpType, mybir.ActivationFunctionType, mybir.AxisListType
    ds = bass.ds

    ctx = ExitStack()
    with ctx:
        def sb(name, shape, dt=f32, where=ctx):
            return where.enter_context(nc.sbuf_tensor(name, shape, dt))

        def sem(name):
            return ctx.enter_context(nc.semaphore(name))

        def dram(name, shape):
            return nc.dram_tensor(name, shape, f32, kind="Internal").ap()

        features = dram("features", (NODES_PAD * RELS, ROW))
        dst_logits = dram("dst_logits", (NODES_PAD, RELS * HEADS))
        heads_of_runs = dram("heads_of_runs", (EDGES_PAD, RELS * HEADS))
        edge_logits = dram("edge_logits", (EDGES_PAD, HEADS))
        dst_flat = dram("dst_flat", (SEARCH_ROWS, SEARCH_ROW))
        node_weights = dram("node_weights", (NODE_TILES, P))

        ident = sb("ident", [P, P])
        iota_free = sb("iota_free", [P, P])
        block_base = sb("block_base", [P, NODE_TILES + 1])
        x_res = sb("x_res", [P, NODE_TILES, DIM])
        acc = sb("acc", [P, NODE_TILES, HEADS, HEAD_COLS])
        bn = sb("bn", [P, NODE_TILES, 6])
        ln_mean = sb("ln_mean", [P, NODE_TILES])
        ln_rstd = sb("ln_rstd", [P, NODE_TILES])
        ln_shift = sb("ln_shift", [P, NODE_TILES])
        ln_t = sb("ln_t", [P, NODE_TILES])
        ln_u = sb("ln_u", [P, NODE_TILES])
        ET = CHUNKS * CHUNK_COLS
        feat_idx = sb("feat_idx", [P, ET], i32)
        dst_f = sb("dst_f", [P, ET])
        prev_mask = sb("prev_mask", [P, ET], bf16)
        next_mask = sb("next_mask", [P, ET], bf16)
        first_run = sb("first_run", [P, ET], bf16)
        last_run = sb("last_run", [P, ET], bf16)
        prev_open = sb("prev_open", [P, CHUNKS])
        next_open = sb("next_open", [P, CHUNKS])
        prev_pass = sb("prev_pass", [P, CHUNKS])
        next_pass = sb("next_pass", [P, CHUNKS])
        last_block = sb("last_block", [P, CHUNKS + 2], i32)

        psum = ctx.enter_context(nc.psum_tensor("psum", [P, 8, 512], f32))

        def tile_of(tensor, t):
            return tensor[:, ds(t, 1), :].rearrange("p o d -> p (o d)")

        def moments(dve, then, lo, hi, eps=EPS):
            b, t, u, m = bn[:, lo:hi], ln_t[:, lo:hi], ln_u[:, lo:hi], ln_mean[:, lo:hi]
            dve.tensor_tensor(t, b[:, :, 1], b[:, :, 4], ALU.subtract)
            dve.tensor_tensor(u, b[:, :, 2], b[:, :, 5], ALU.add)
            then(dve.tensor_tensor(m, b[:, :, 1], b[:, :, 4], ALU.add))
            dve.tensor_scalar(m, m, 0.5, None, ALU.mult)
            then(dve.tensor_tensor(t, t, t, ALU.mult))
            then(dve.tensor_scalar(u, u, 1.0 / DIM, eps, ALU.mult, ALU.add))
            then(dve.scalar_tensor_tensor(u, t, 0.25, u, ALU.mult, ALU.add))

        flat_in, edges_in, x_in, conv_in, attn_in = (sem(n) for n in ("flat_in", "edges_in", "x_in", "conv_in", "attn_in"))
        const_ready, setup_done, std_ready = sem("const_ready"), sem("setup_done"), sem("std_ready")
        xn_ready, xt_psum, xt_ready = sem("xn_ready"), sem("xt_psum"), sem("xt_ready")
        logit_psum, logit_ready, logits_stored = sem("logit_psum"), sem("logit_ready"), sem("logits_stored")
        feat_psum, feat_ready = sem("feat_psum"), sem("feat_ready")
        store = [sem("store0"), sem("store1")]
        zeroed, flat_stored, rows_found = sem("zeroed"), sem("flat_stored"), [sem("rows_found0"), sem("rows_found1")]
        firsts_found, scattered, start_in = sem("firsts_found"), sem("scattered"), sem("start_in")
        piece_in, piece_done, piece_stored = [sem("piece_in0"), sem("piece_in1")], sem("piece_done"), [sem("piece_stored0"), sem("piece_stored1")]
        tile_seen, staged_seen = sem("tile_seen"), sem("staged_seen")
        HALF = NODE_TILES // 2
        LOGITS = RELS * HEADS
        marks = {}

        with ExitStack() as st:
            conv = sb("conv", [P, 2, LOGITS, HEAD_COLS], f32, st)
            attn = sb("attn", [P, 2, LOGITS, HEAD_DIM], f32, st)
            conv_er = sb("conv_er", [P, 2, LOGITS], f32, st)
            table = sb("table", [P, 2, RELS, ROW], f32, st)
            er_all = sb("er_all", [P, NODE_TILES, LOGITS], f32, st)
            xn = sb("xn", [P, 2, DIM], f32, st)
            xt = sb("xt", [P, 2, 2, P], f32, st)
            zeros = sb("zeros", [P, PART_EDGES], f32, st)
            pieces = sb("pieces", [P, 3, PIECE * LOGITS], f32, st)
            row_first_i = sb("row_first_i", [P, SEARCH_ROWS], i32, st)
            row_first = sb("row_first", [P, SEARCH_ROWS], f32, st)
            node_id = sb("node_id", [P, NODE_TILES], f32, st)
            below = sb("below", [P, NODE_TILES], f32, st)
            row_of = sb("row_of", [P, NODE_TILES], f32, st)
            row_idx = sb("row_idx", [P, NODE_TILES], i32, st)
            first_f = sb("first_f", [P, NODE_TILES], f32, st)
            first_idx = sb("first_idx", [P, NODE_TILES], i32, st)
            dst_at_first = sb("dst_at_first", [P, NODE_TILES], f32, st)
            absent = sb("absent", [P, NODE_TILES], f32, st)
            scatter_idx = sb("scatter_idx", [P, NODE_TILES], i32, st)
            flat_f = sb("flat_f", [P, PART_EDGES], f32, st)
            keep = sb("keep", [P, PART_EDGES], f32, st)
            kind_f = sb("kind_f", [P, PART_EDGES], f32, st)
            kind_no = sb("kind_no", [P, RELS], f32, st)
            kind_is = sb("kind_is", [P, 2, PIECE, RELS], f32, st)
            start_idx = sb("start_idx", [P, 1], i32, st)
            start = sb("start", [P, LOGITS], f32, st)
            carry = sb("carry", [P, LOGITS], f32, st)
            edge_er = sb("edge_er", [P, 2, PIECE, HEADS], f32, st)
            scratch = acc[:].rearrange("p t h c -> p (t h c)").bitcast(i32)
            raw = scratch[:, 0:5 * ET].rearrange("p (j e) -> p j e", j=5)
            flat = scratch[:, 5 * ET:5 * ET + 3 * PART_EDGES].rearrange("p (j e) -> p j e", j=3)
            found = pieces[:].rearrange("p a b -> p (a b)")[:, 0:HALF * SEARCH_ROW].rearrange("p (t e) -> p t e", e=SEARCH_ROW)
            block = st.enter_context(nc.Block())

            @block.vector
            def _(dve):
                done = [0]

                def then(ins):
                    done[0] += 1
                    ins.then_inc(setup_done, 1)
                    dve.wait_ge(setup_done, done[0])

                then(dve.memset(zeros[:], 0.0))
                marks["zeros"] = done[0]
                dve.wait_ge(x_in, 16)
                with dve.Fori(0, NODE_TILES) as t:
                    dve.bn_stats(tile_of(bn, t), tile_of(x_res, t)).then_inc(setup_done, 1)
                done[0] += NODE_TILES
                dve.wait_ge(setup_done, done[0])
                moments(dve, then, 0, NODE_TILES)
                marks["variance"] = done[0]
                prod = pieces[:].rearrange("p a b -> p (a b)")[:, 0:LOGITS * HEAD_DIM].rearrange("p (h d) -> p h d", d=HEAD_DIM)
                dve.wait_ge(conv_in, 32)
                dve.wait_ge(attn_in, 32)
                then(dve.tensor_tensor(prod, conv[:, 0, :, 0:HEAD_DIM], attn[:, 1], ALU.mult))
                dve.wait_ge(std_ready, 1)
                then(dve.reciprocal(ln_rstd[:], ln_rstd[:]))
                then(dve.scalar_tensor_tensor(ln_shift[:], ln_mean[:], -1.0, ln_rstd[:], ALU.mult, ALU.mult))
                marks["norm"] = done[0]
                then(dve.tensor_reduce(conv_er[:, 0], prod, AX.X, ALU.add))
                then(dve.tensor_tensor(prod, conv[:, 1, :, 0:HEAD_DIM], attn[:, 1], ALU.mult))
                then(dve.tensor_reduce(conv_er[:, 1], prod, AX.X, ALU.add))
                marks["dst weights"] = done[0]
                for k in range(2):
                    then(dve.tensor_tensor(prod, conv[:, k, :, 0:HEAD_DIM], attn[:, 0], ALU.mult))
                    then(dve.tensor_reduce(conv[:, k, :, HEAD_DIM], prod, AX.X, ALU.add))
                marks["src weights"] = done[0]

                dve.wait_ge(flat_in, 32)
                dve.tensor_copy(row_first[:], row_first_i[:])
                dve.tensor_copy(start_idx[:], flat[:, 0, 0:1])
                then(dve.tensor_copy(flat_f[:], flat[:, 0]))
                marks["flat"] = done[0]
                dve.wait_ge(const_ready, 7)
                lower_row = pieces[:].rearrange("p a b -> p (a b)")[:, 0:NODE_TILES * SEARCH_ROWS].rearrange("p (t e) -> p t e", e=SEARCH_ROWS)
                then(dve.tensor_tensor(lower_row, row_first[:].unsqueeze(1).to_broadcast([P, NODE_TILES, SEARCH_ROWS]),
                                       node_id[:].unsqueeze(2).to_broadcast([P, NODE_TILES, SEARCH_ROWS]), ALU.is_lt))
                then(dve.tensor_reduce(row_of[:], lower_row, AX.X, ALU.add))
                then(dve.tensor_scalar(row_of[:], row_of[:], -1.0, 0.0, ALU.add, ALU.max))
                then(dve.tensor_copy(row_idx[:], row_of[:]))
                marks["rows"] = done[0]
                dve.tensor_tensor(keep[:], flat[:, 0], flat[:, 1], ALU.is_equal)
                then(dve.tensor_copy(kind_f[:], flat[:, 2]))
                for h in range(2):
                    dve.wait_ge(rows_found[h], 16 * HALF)
                    for t in range(h * HALF, (h + 1) * HALF):
                        row = found[:, t - h * HALF]
                        then(dve.tensor_scalar(row, row, node_id[:, t:t + 1], None, ALU.is_lt, ALU.add, accum_out=below[:, t:t + 1]))
                    marks["half %d" % h] = done[0]
                then(dve.scalar_tensor_tensor(first_f[:], row_of[:], float(SEARCH_ROW), below[:], ALU.mult, ALU.add))
                then(dve.tensor_copy(first_idx[:], first_f[:]))
                marks["firsts"] = done[0]

                dve.wait_ge(edges_in, 16)
                src, dst, before, after, kind = (raw[:, j] for j in range(5))
                run_start = pieces[:, 2, 0:ET]
                dve.scalar_tensor_tensor(feat_idx[:], src, float(RELS), kind, ALU.mult, ALU.add)
                dve.tensor_copy(dst_f[:], dst)
                dve.tensor_tensor(prev_mask[:], dst, before, ALU.is_equal)
                then(dve.tensor_tensor(next_mask[:], dst, after, ALU.is_equal))

                def cols(tile):
                    return tile.rearrange("p (t c) -> p t c", c=CHUNK_COLS)

                for mask, open_, pass_, run, edge, far, order in (
                        (prev_mask, prev_open, prev_pass, first_run, 0, CHUNK_COLS - 1, 1),
                        (next_mask, next_open, next_pass, last_run, CHUNK_COLS - 1, 0, -1)):
                    then(dve.tensor_scalar(open_[:], cols(mask[:])[:, :, edge], -1.0, BIG, ALU.add, ALU.mult))
                    then(dve.memset(cols(mask[:])[:, :, edge], 0.0))
                    then(dve.memset(run_start, 0.0))
                    then(dve.memset(cols(run_start)[:, :, edge], 1.0))
                    then(dve.tensor_tensor_scan(out=run[:, ::order], data0=mask[:, ::order], data1=run_start[:, ::order],
                                                initial=0.0, op0=ALU.mult, op1=ALU.max))
                    then(dve.tensor_scalar(run[:], run[:], -1.0, BIG, ALU.add, ALU.mult))
                    then(dve.tensor_tensor(pass_[:], cols(run[:])[:, :, far], open_[:], ALU.min))
                    then(dve.tensor_scalar(mask[:], mask[:], -1.0, BIG, ALU.add, ALU.mult))
                then(dve.memset(last_block[:], 0))
                then(dve.tensor_single_scalar(last_block[:, 2:CHUNKS + 2], cols(dst)[:, :, CHUNK_COLS - 1],
                                              P.bit_length() - 1, ALU.arith_shift_right))

                dve.wait_ge(firsts_found, 16 * NODE_TILES)
                then(dve.tensor_tensor(absent[:], dst_at_first[:], node_id[:], ALU.not_equal))
                then(dve.scalar_tensor_tensor(first_f[:], absent[:], float(2 * EDGES_PAD), first_f[:], ALU.mult, ALU.add))
                then(dve.tensor_copy(scatter_idx[:], first_f[:]))
                marks["scatter"] = done[0]

                dve.wait_ge(start_in, 16)
                then(dve.tensor_copy(carry[:], start[:]))
                for i in range(PIECES):
                    z = i % 2
                    piece = pieces[:, z].rearrange("p (e j) -> p e j", j=LOGITS)
                    picked = pieces[:, 2].rearrange("p (e j) -> p e j", j=LOGITS)
                    part = slice(i * PIECE, (i + 1) * PIECE)
                    dve.tensor_tensor(kind_is[:, z], kind_f[:, part].unsqueeze(2).to_broadcast([P, PIECE, RELS]),
                                      kind_no[:].unsqueeze(1).to_broadcast([P, PIECE, RELS]), ALU.is_equal)
                    dve.wait_ge(piece_in[z], 16 * (i // 2 + 1))
                    for j in range(LOGITS):
                        last = dve.tensor_tensor_scan(out=piece[:, :, j], data0=keep[:, part], data1=piece[:, :, j],
                                                      initial=carry[:, j:j + 1], op0=ALU.mult, op1=ALU.add)
                    then(last)
                    dve.tensor_copy(carry[:], piece[:, PIECE - 1, :])
                    then(dve.tensor_tensor(picked.rearrange("p e (r h) -> p e r h", h=HEADS), piece.rearrange("p e (r h) -> p e r h", h=HEADS),
                                           kind_is[:, z].unsqueeze(3).to_broadcast([P, PIECE, RELS, HEADS]), ALU.mult))
                    marks["piece %d" % i] = done[0]
                    if i >= 2:
                        dve.wait_ge(piece_stored[z], 16 * (i // 2))
                    dve.tensor_reduce(edge_er[:, z], picked.rearrange("p e (r h) -> p e h r", h=HEADS), AX.X, ALU.add).then_inc(piece_done, 1)
                    dve.wait_ge(piece_done, i + 1)

            @block.sync
            def _(sp):
                sp.dma_start(x_res[:], a["x"].rearrange("(t p) d -> p t d", p=P)).then_inc(x_in, 16)
                for k in range(2):
                    sp.dma_start(conv[:, k, :, 0:HEAD_DIM],
                                 a["conv"].rearrange("r h (k p) d -> k p (r h) d", p=P)[k]).then_inc(conv_in, 16)
                for k, name in enumerate(("attn_l", "attn_r")):
                    sp.dma_start(attn[:, k], a[name].rearrange("r h d -> (r h) d").partition_broadcast(P)).then_inc(attn_in, 16)
                sp.dma_start(flat, a["flat"]).then_inc(flat_in, 16)
                sp.dma_start(row_first_i[:], a["row_first"].partition_broadcast(P)).then_inc(flat_in, 16)
                sp.dma_start(raw, a["edges"]).then_inc(edges_in, 16)
                runs = heads_of_runs.rearrange("(q e) j -> q (e j)", q=P)
                sp.wait_ge(setup_done, marks["zeros"])
                sp.dma_start(runs.rearrange("q (r e) -> q r e", e=PART_EDGES),
                             zeros[:].unsqueeze(1).to_broadcast([P, LOGITS, PART_EDGES])).then_inc(zeroed, 16)
                sp.wait_ge(setup_done, marks["flat"])
                sp.dma_start(dst_flat.rearrange("r e -> (r e)").rearrange("(q e) -> q e", q=P), flat_f[:]).then_inc(flat_stored, 16)
                sp.wait_ge(logit_ready, NODE_TILES)
                sp.dma_start(dst_logits.rearrange("(t p) j -> p t j", p=P), er_all[:]).then_inc(logits_stored, 16)
                er_flat = edge_logits.rearrange("(q e) h -> q e h", q=P)
                sp.wait_ge(scattered, 16 * NODE_TILES)
                sp.wait_ge(setup_done, marks["scatter"])
                for i in range(PIECES + 1):
                    if i < PIECES:
                        if i >= 2:
                            sp.wait_ge(setup_done, marks["piece %d" % (i - 2)])
                        sp.dma_start(pieces[:, i % 2], runs[:, i * PIECE * LOGITS:(i + 1) * PIECE * LOGITS]).then_inc(piece_in[i % 2], 16)
                    if i >= 1:
                        sp.wait_ge(piece_done, i)
                        sp.dma_start(er_flat[:, (i - 1) * PIECE:i * PIECE, :], edge_er[:, (i - 1) % 2]).then_inc(piece_stored[(i - 1) % 2], 16)
                sp.wait_ge(piece_stored[0], 16 * ((PIECES + 1) // 2))
                sp.wait_ge(piece_stored[1], 16 * (PIECES // 2))

            @block.gpsimd
            def _(pool):
                pool.memset(ident[:], 0.0).then_inc(const_ready, 1)
                for tile, pattern, step in ((iota_free, [[1, P]], 0), (block_base, [[P, NODE_TILES + 1]], 0),
                                            (node_id, [[P, NODE_TILES]], 1), (kind_no, [[1, RELS]], 0)):
                    pool.iota(tile[:], pattern=pattern, base=0, channel_multiplier=step,
                              allow_small_or_imprecise_dtypes=True).then_inc(const_ready, 1)
                pool.wait_ge(const_ready, 5)
                pool.affine_select(out=ident[:], in_=ident[:], compare_op=ALU.not_equal, fill=1.0, base=0,
                                   pattern=[[-1, P]], channel_multiplier=1).then_inc(const_ready, 2)

                def gather(out_, table_, idx, rows_, signal):
                    pool.indirect_dma_start(out=out_, out_offset=None, in_=table_,
                                            in_offset=bass.IndirectOffsetOnAxis(ap=idx, axis=0),
                                            bounds_check=rows_ - 1, oob_is_err=True).then_inc(signal, 16)

                pool.wait_ge(flat_stored, 16)
                pool.wait_ge(setup_done, marks["rows"])
                for t in range(NODE_TILES):
                    if t == HALF:
                        pool.wait_ge(setup_done, marks["half 0"])
                    gather(found[:, t % HALF], dst_flat, row_idx[:, t:t + 1], SEARCH_ROWS, rows_found[t // HALF])
                pool.wait_ge(setup_done, marks["firsts"])
                for t in range(NODE_TILES):
                    gather(dst_at_first[:, t:t + 1], dst_flat.rearrange("r (e o) -> (r e) o", o=1), first_idx[:, t:t + 1],
                           EDGES_PAD, firsts_found)
                pool.wait_ge(logits_stored, 16)
                gather(start[:], dst_logits, start_idx[:], NODES_PAD, start_in)
                pool.wait_ge(zeroed, 16)
                pool.wait_ge(setup_done, marks["scatter"])
                for t in range(NODE_TILES):
                    pool.indirect_dma_start(out=heads_of_runs, out_offset=bass.IndirectOffsetOnAxis(ap=scatter_idx[:, t:t + 1], axis=0),
                                            in_=er_all[:, t], in_offset=None,
                                            bounds_check=EDGES_PAD - 1, oob_is_err=False).then_inc(scattered, 16)

            @block.scalar
            def _(act):
                act.sem_inc(store[0], 16)
                act.sem_inc(store[1], 16)
                act.sem_inc(feat_ready, 4)
                act.wait_ge(setup_done, marks["variance"])
                nc.scalar.activation(ln_rstd[:], ln_u[:], ACT.Sqrt).then_inc(std_ready, 1)
                act.wait_ge(setup_done, marks["norm"])

                def norm(t, u):
                    act.wait_ge(xt_psum, t + 1)
                    nc.scalar.activation(xn[:, u], tile_of(x_res, t), ACT.Identity, bias=ln_shift[:, ds(t % NODE_TILES if isinstance(t, int) else t, 1)],
                                         scale=ln_rstd[:, ds(t, 1)]).then_inc(xn_ready, 1)

                with act.Fori(0, NODE_TILES // 2) as i:
                    for u in range(2):
                        t = i * 2 + u
                        norm(t, u)
                    for u in range(2):
                        t = i * 2 + u
                        act.wait_ge(xt_psum, t + 3)
                        nc.scalar.copy(xt[:, u], psum[:, u, 0:2 * P].rearrange("p (k n) -> p k n", k=2)).then_inc(xt_ready, 1)
                    for u in range(2):
                        t = i * 2 + u
                        act.wait_ge(logit_psum, t + 1)
                        nc.scalar.copy(tile_of(er_all, t), psum[:, 6 + u, 0:LOGITS]).then_inc(logit_ready, 1)
                def norm2(t, u):
                    act.wait_ge(xt_psum, t + NODE_TILES + 1)
                    nc.scalar.activation(xn[:, u], tile_of(x_res, t), ACT.Identity, bias=ln_shift[:, ds(t, 1)],
                                         scale=ln_rstd[:, ds(t, 1)]).then_inc(xn_ready, 1)

                def tile(t, u, ahead):
                    if ahead:
                        norm2(t + 1, 1 - u)
                    act.wait_ge(store[u], (t // 2 if isinstance(t, int) else i_now[0]) * 16 + 16)
                    for r in range(RELS):
                        act.wait_ge(feat_psum, RELS * t + r + 1)
                        nc.scalar.copy(table[:, u, r], psum[:, 2 + r % 4, 0:ROW]).then_inc(feat_ready, 1)
                        if r == RELS // 2 and ahead:
                            act.wait_ge(xt_psum, t + 1 + NODE_TILES + 3)
                            nc.scalar.copy(xt[:, 1 - u], psum[:, 1 - u, 0:2 * P].rearrange("p (k n) -> p k n", k=2)).then_inc(xt_ready, 1)
                    act.wait_ge(feat_ready, RELS * t + RELS + 4)
                    act.dma_start(features.rearrange("(t n r) c -> t n (r c)", r=RELS, n=P)[ds(t, 1)].rearrange("o n c -> (o n) c"),
                                  table[:, u].rearrange("p r c -> p (r c)")).then_inc(store[u], 16)

                i_now = [0]
                norm2(0, 0)
                act.wait_ge(xt_psum, NODE_TILES + 3)
                nc.scalar.copy(xt[:, 0], psum[:, 0, 0:2 * P].rearrange("p (k n) -> p k n", k=2)).then_inc(xt_ready, 1)
                with act.Fori(0, NODE_TILES // 2 - 1) as i:
                    i_now[0] = i
                    for u in range(2):
                        tile(i * 2 + u, u, True)
                tile(NODE_TILES - 2, 0, True)
                tile(NODE_TILES - 1, 1, False)
                for u in range(2):
                    act.wait_ge(store[u], 16 * (NODE_TILES // 2) + 16)

            @block.tensor
            def _(pe):
                pe.sem_inc(xt_psum, 2)
                pe.wait_ge(const_ready, 7)

                def transposes(t, u):
                    pe.wait_ge(xn_ready, t + 1)
                    for k in range(2):
                        last = nc.tensor.transpose(psum[:, u, k * P:(k + 1) * P], xn[:, u, k * P:(k + 1) * P], ident[:])
                    last.then_inc(xt_psum, 1)

                pe.wait_ge(setup_done, marks["dst weights"])
                with pe.Fori(0, NODE_TILES // 2) as i:
                    for u in range(2):
                        transposes(i * 2 + u, u)
                    for u in range(2):
                        t = i * 2 + u
                        pe.wait_ge(xt_ready, t + 1)
                        for k in range(2):
                            last = nc.tensor.matmul(psum[:, 6 + u, 0:LOGITS], xt[:, u, k], conv_er[:, k],
                                                    start=(k == 0), stop=(k == 1))
                        last.then_inc(logit_psum, 1)

                def tile(t, u, ahead):
                    pe.wait_ge(xt_ready, t + NODE_TILES + 1)
                    for r in range(RELS):
                        pe.wait_ge(feat_ready, RELS * t + r + 1)
                        for k in range(2):
                            last = nc.tensor.matmul(psum[:, 2 + r % 4, 0:ROW], xt[:, u, k],
                                                    conv[:, k, r * HEADS:(r + 1) * HEADS, :].rearrange("p h c -> p (h c)"),
                                                    start=(k == 0), stop=(k == 1))
                        last.then_inc(feat_psum, 1)
                        if r == RELS // 4 and ahead:
                            transposes(t + 1 + NODE_TILES, 1 - u)

                transposes(NODE_TILES, 0)
                pe.wait_ge(setup_done, marks["src weights"])
                with pe.Fori(0, NODE_TILES // 2 - 1) as i:
                    for u in range(2):
                        tile(i * 2 + u, u, True)
                tile(NODE_TILES - 2, 0, True)
                tile(NODE_TILES - 1, 1, False)

        PREP = 14
        gathered = [sem(f"gathered{u}") for u in range(SLOTS)]
        er_in = [sem(f"er_in{u}") for u in range(SLOTS)]
        idx_staged, chunk_free, chunk_done, prep, er_seen = (sem(n) for n in ("idx_staged", "chunk_free", "chunk_done", "prep", "er_seen"))
        masks_ready, masks_free, masks_psum, tails_psum, masks_copied, carries_psum, exp_ready = sem("masks_ready"), sem("masks_free"), sem("masks_psum"), sem("tails_psum"), sem("masks_copied"), sem("carries_psum"), sem("exp_ready")
        onehot_ready, sums_psum, acc_step = sem("onehot_ready"), sem("sums_psum"), sem("acc_step")
        main_init, mixw_in, bias_in, centred = sem("main_init"), sem("mixw_in"), sem("bias_in"), sem("centred")
        xnb_ready, xtb_psum, xtb_ready, kv_psum = sem("xnb_ready"), sem("xtb_psum"), sem("xtb_ready"), sem("kv_psum")
        squares_ready, v_ready, var_ready, stdb_ready = sem("squares_ready"), sem("v_ready"), sem("var_ready"), sem("stdb_ready")
        rk_ready, k_ready, dots_psum, dots_added = sem("rk_ready"), sem("k_ready"), sem("dots_psum"), sem("dots_added")
        wq_psum, wq_ready, g_psum, g_ready, eff_psum, eff_ready = (sem(n) for n in ("wq_psum", "wq_ready", "g_psum", "g_ready", "eff_psum", "eff_ready"))
        dots_masked, mix_psum, mix_added = sem("dots_masked"), sem("mix_psum"), sem("mix_added")
        PAIRS = MIX_HEADS // 2
        TAILS, SMALL, SUMS, MORE, KEYS, VALUES = 0, 1, 2, 5, 6, 7
        with ExitStack() as st:
            rows = sb("rows", [P, SLOTS, CHUNK_COLS, ROW], f32, st)
            er = sb("er", [P, SLOTS, CHUNK_COLS, HEADS], f32, st)
            idx_now = sb("idx_now", [P, SLOTS, CHUNK_COLS], i32, st)
            onehot = sb("onehot", [P, SLOTS + 1, CHUNK_COLS, P], f32, st)
            e = sb("e", [P, CE], f32, st)
            lin = sb("lin", [P, CE], f32, st)
            mask_f = sb("mask_f", [P, SLOTS, CE], f32, st)
            mask_b = sb("mask_b", [P, SLOTS, CE], f32, st)
            max_f = sb("max_f", [P, CE], f32, st)
            max_b = sb("max_b", [P, CE], f32, st)
            seg_max = sb("seg_max", [P, CE], f32, st)
            reach = sb("reach", [P, CE], f32, st)
            pass_now = sb("pass_now", [P, SLOTS, 2, HEADS], f32, st)
            pass_t = sb("pass_t", [HEADS, 2 * P], f32, st)
            carry_f = sb("carry_f", [HEADS, SLOTS, P + 1], f32, st)
            carry_b = sb("carry_b", [HEADS, P + 1], f32, st)
            from_prev = sb("from_prev", [P, HEADS], f32, st)
            from_next = sb("from_next", [P, HEADS], f32, st)
            ones_row = sb("ones_row", [P, CE], f32, st)
            arg = sb("arg", [P, CE + HEADS], f32, st)
            ex = sb("ex", [P, CE + HEADS], f32, st)
            decay = sb("decay", [1, SLOTS, HEADS], f32, st)
            factor = sb("factor", [P, HEADS], f32, st)
            scaled = sb("scaled", [P, HEADS, HEAD_COLS], f32, st)
            wqkv = sb("wqkv", [P, 2, 3 * INNER], f32, st)
            wout = sb("wout", [P, PAIRS, DIM], f32, st)
            bias = sb("bias", [1, 2, DIM], f32, st)
            bsum = sb("bsum", [1, DIM], f32, st)
            ones_b = sb("ones_b", [1, P], f32, st)
            hmean = sb("hmean", [P, 2, 2 * MIX_HEADS], f32, st)
            xn = sb("xnb", [P, 2, DIM], f32, st)
            xt = sb("xtb", [P, 2, 2, P], f32, st)
            kv_work = sb("kv_work", [P, 6, INNER], f32, st)
            squares, ks, vs = kv_work[:, 0:2], kv_work[:, 2:4], kv_work[:, 4:6]
            wqt = kv_work[:, 0:2].rearrange("p a n -> p (a n)").rearrange("p (a k n) -> p a k n", a=PAIRS, k=2)
            g = kv_work[:, 2:4].rearrange("p a n -> p (a n)").rearrange("p (a n) -> p a n", a=PAIRS)
            kv_var = sb("kv_var", [P, 2 * MIX_HEADS], f32, st)
            kv_prod = sb("kv_prod", [P, MIX_HEADS], f32, st)
            rk = sb("rk", [P, MIX_HEADS], f32, st)
            dots = sb("dots", [P, PAIRS, P], f32, st)
            dots_diag = sb("dots_diag", [P, PAIRS, P], f32, st)
            eff = sb("eff", [P, 2, DIM], f32, st)
            block = st.enter_context(nc.Block())

            def schedule(each):
                eng, body, between = each
                with eng.Fori(0, KV_ITERS) as i:
                    for u in range(SLOTS):
                        body(i * SLOTS + u, i, u, "kv", True)
                between()
                with eng.Fori(KV_ITERS, ITERS - 1) as i:
                    for u in range(SLOTS):
                        body(i * SLOTS + u, i, u, "mix", True)
                for u in range(SLOTS):
                    body((ITERS - 1) * SLOTS + u, ITERS - 1, u, "mix", u < SLOTS - 1)

            def mix_tiles(i, u):
                for j in range(2 * u, min(2 * u + 2, MIX_TILES)):
                    yield (i - KV_ITERS) * MIX_TILES + j, j % 2

            @block.sync
            def _(sp):
                sp.dma_start(wqkv[:], a["wqkv"].rearrange("(k p) n -> p k n", p=P)).then_inc(mixw_in, 16)
                sp.dma_start(wout[:], a["wout"].rearrange("(k p) n -> p k n", p=P)).then_inc(mixw_in, 16)
                sp.dma_start(bias[:, 0], a["h_bias"].rearrange("(o n) -> o n", o=1)).then_inc(bias_in, 16)
                sp.dma_start(bias[:, 1], a["b_out"].rearrange("(o n) -> o n", o=1)).then_inc(bias_in, 16)
                by_chunk = edge_logits.rearrange("(t p c) h -> t p (c h)", p=P, c=CHUNK_COLS)
                with sp.Fori(0, ITERS) as i:
                    for u in range(SLOTS):
                        t = i * SLOTS + u
                        sp.wait_ge(chunk_free, t + 1)
                        sp.sem_inc(er_seen, 1)
                        sp.dma_start(er[:, u].rearrange("p c h -> p (c h)"),
                                     by_chunk[ds(t, 1)].rearrange("o p n -> (o p) n")).then_inc(er_in[u], 16)

            @block.gpsimd
            def _(pool):
                pool.sem_inc(chunk_free, SLOTS)
                with pool.Fori(0, ITERS) as i:
                    for u in range(SLOTS):
                        t = i * SLOTS + u
                        pool.wait_ge(chunk_free, t + 1)
                        pool.tensor_copy(idx_now[:, u], feat_idx[:, ds(t * CHUNK_COLS, CHUNK_COLS)]).then_inc(idx_staged, 1)
                        pool.wait_ge(idx_staged, t + 1)
                        pool.sem_inc(staged_seen, 1)
                        for c in range(CHUNK_COLS):
                            pool.indirect_dma_start(out=rows[:, u, c], out_offset=None, in_=features,
                                                    in_offset=bass.IndirectOffsetOnAxis(ap=idx_now[:, u, c:c + 1], axis=0),
                                                    bounds_check=NODES_PAD * RELS - 1, oob_is_err=True).then_inc(gathered[u], 16)

            def hc(tile, n=CE):
                return tile[:, 0:n].rearrange("p (h c) -> p h c", h=HEADS)

            def by_head(edge_data, t):
                return edge_data[:, ds(t * CHUNK_COLS, CHUNK_COLS)].unsqueeze(1).to_broadcast([P, HEADS, CHUNK_COLS])

            @block.vector
            def _(dve):
                dve.memset(acc[:], 0.0).then_inc(main_init, 1)
                dve.memset(carry_f[:], -BIG).then_inc(main_init, 1)
                dve.memset(carry_b[:], -BIG).then_inc(main_init, 1)
                dve.memset(ones_b[:], 1.0).then_inc(main_init, 1)
                dve.memset(dots[:], 0.0).then_inc(main_init, 1)
                dve.memset(dots_diag[:], 0.0).then_inc(main_init, 1)
                dve.memset(kv_work[:], 0.0).then_inc(main_init, 1)
                dve.memset(ones_row[:], 1.0).then_inc(main_init, 1)
                dve.wait_ge(main_init, 8)
                dve.sem_inc(acc_step, 1)
                dve.sem_inc(dots_added, 1)
                dve.wait_ge(mixw_in, 32)
                wkv = [wqkv[:, k, INNER:3 * INNER].rearrange("p (h d) -> p h d", d=MIX_DIM) for k in range(2)]
                for k in range(2):
                    dve.tensor_reduce(hmean[:, k], wkv[k], AX.X, ALU.add).then_inc(centred, 1)
                dve.wait_ge(centred, 2)
                dve.tensor_scalar(hmean[:], hmean[:], 1.0 / MIX_DIM, None, ALU.mult).then_inc(centred, 1)
                dve.wait_ge(centred, 3)
                for k in range(2):
                    dve.tensor_tensor(wkv[k], wkv[k], hmean[:, k].unsqueeze(2).to_broadcast([P, 2 * MIX_HEADS, MIX_DIM]),
                                      ALU.subtract).then_inc(centred, 1)
                dve.wait_ge(bias_in, 32)
                dve.tensor_tensor(bsum[:], bias[:, 0], bias[:, 1], ALU.add).then_inc(centred, 1)

                def after(t, n):
                    dve.wait_ge(prep, PREP * t + n)

                def front(t, i, u):
                    dve.wait_ge(gathered[u], (i + 1) * 16 * CHUNK_COLS)
                    dve.wait_ge(er_in[u], (i + 1) * 16)
                    dve.tensor_tensor(hc(lin), rows[:, u, :, HEAD_DIM::HEAD_COLS].rearrange("p c h -> p h c"),
                                      er[:, u].rearrange("p c h -> p h c"), ALU.add).then_inc(prep, 2)
                    after(t, 2)
                    dve.scalar_tensor_tensor(e[:], lin[:], SLOPE, lin[:], ALU.mult, ALU.max).then_inc(prep, 1)
                    after(t, 3)
                    dve.wait_ge(masks_ready, t + 1)
                    dve.tensor_tensor_scan(out=max_f[:], data0=mask_f[:, u], data1=e[:], initial=-BIG, op0=ALU.add, op1=ALU.max)
                    dve.tensor_tensor_scan(out=max_b[:, ::-1], data0=mask_b[:, u, ::-1], data1=e[:, ::-1], initial=-BIG,
                                           op0=ALU.add, op1=ALU.max).then_inc(prep, 1)
                    after(t, 4)
                    dve.tensor_tensor(seg_max[:], max_f[:], max_b[:], ALU.max).then_inc(prep, 1)

                def across(t, u):
                    dve.wait_ge(tails_psum, t + 1)
                    dve.tensor_tensor_scan(out=carry_f[:, u, 1:P + 1], data0=pass_t[:, 0:P], data1=psum[0:HEADS, TAILS, 0:P],
                                           initial=carry_f[:, u, 0:1], op0=ALU.add, op1=ALU.max)
                    dve.tensor_tensor_scan(out=carry_b[:, 0:P][:, ::-1], data0=pass_t[:, P:2 * P][:, ::-1],
                                           data1=psum[0:HEADS, TAILS, P:2 * P][:, ::-1],
                                           initial=-BIG, op0=ALU.add, op1=ALU.max).then_inc(prep, 1)

                def numerators(t, u):
                    dve.wait_ge(carries_psum, t + 1)
                    dve.tensor_scalar(from_prev[:], psum[:, SMALL, 0:HEADS], prev_open[:, ds(t, 1)], None, ALU.add)
                    dve.tensor_scalar(from_next[:], psum[:, SMALL, HEADS:2 * HEADS], next_open[:, ds(t, 1)], None, ALU.add).then_inc(prep, 1)
                    after(t, 7)
                    dve.tensor_tensor(hc(reach), by_head(first_run, t),
                                      from_prev[:].unsqueeze(2).to_broadcast([P, HEADS, CHUNK_COLS]), ALU.add)
                    dve.tensor_copy(carry_f[:, (u + 1) % SLOTS, 0:1], carry_f[:, u, P:P + 1]).then_inc(prep, 1)
                    after(t, 8)
                    dve.tensor_tensor(seg_max[:], seg_max[:], reach[:], ALU.max).then_inc(prep, 1)
                    after(t, 9)
                    dve.tensor_tensor(hc(reach), by_head(last_run, t),
                                      from_next[:].unsqueeze(2).to_broadcast([P, HEADS, CHUNK_COLS]), ALU.add).then_inc(prep, 1)
                    after(t, 10)
                    dve.tensor_tensor(seg_max[:], seg_max[:], reach[:], ALU.max).then_inc(prep, 1)
                    after(t, 11)
                    dve.tensor_tensor(arg[:, 0:CE], e[:], seg_max[:], ALU.subtract)
                    dve.tensor_tensor(arg[:, CE:], from_prev[:], hc(seg_max)[:, :, 0], ALU.subtract).then_inc(prep, 1)
                    dve.wait_ge(exp_ready, t + 1)
                    dve.tensor_scalar(decay[:, u], ex[0:1, CE:], -1.0, None, ALU.add).then_inc(prep, 1)
                    row4 = rows[:, u].rearrange("p c (h d) -> p c h d", d=HEAD_COLS)
                    dve.tensor_tensor(row4, row4, hc(ex).rearrange("p h c -> p c h").unsqueeze(3).to_broadcast(
                        [P, CHUNK_COLS, HEADS, HEAD_COLS]), ALU.mult).then_inc(prep, 1)

                first_of = {}

                def blocks(t, u):
                    for j in range(0 if u == 0 else 2, 3):
                        first_of[u + j] = dve.value_load(last_block[P - 1:P, ds(t + j, 1)], min_val=0, max_val=NODE_TILES - 1)
                    return first_of[u], first_of[u + 1], first_of[u + 2]

                def one_hot(z, t, b):
                    dve.scalar_tensor_tensor(onehot[:, z], iota_free[:].unsqueeze(1).to_broadcast([P, CHUNK_COLS, P]),
                                             block_base[:, ds(b, 1)],
                                             dst_f[:, ds(t * CHUNK_COLS, CHUNK_COLS)].unsqueeze(2).to_broadcast([P, CHUNK_COLS, P]),
                                             ALU.add, ALU.is_equal).then_inc(onehot_ready, 1)

                def block_sums(b):
                    return acc[:, ds(b, 1)].rearrange("p o h c -> p (o h) c")

                def add_first(t, u, b):
                    dve.wait_ge(sums_psum, t + b + 1)
                    dve.wait_ge(acc_step, 3 * t + b + 1)
                    dve.tensor_scalar(factor[:], psum[:, SMALL, 16:16 + HEADS], 1.0, None, ALU.add).then_inc(acc_step, 1)
                    dve.wait_ge(acc_step, 3 * t + b + 2)
                    dve.tensor_tensor(scaled[:], block_sums(b), factor[:].unsqueeze(2).to_broadcast([P, HEADS, HEAD_COLS]),
                                      ALU.mult).then_inc(acc_step, 1)
                    dve.wait_ge(acc_step, 3 * t + b + 3)
                    dve.tensor_tensor(block_sums(b), scaled[:], psum[:, SUMS + u, 0:ROW].rearrange("p (h c) -> p h c", h=HEADS),
                                      ALU.add).then_inc(acc_step, 1)

                def add_last(t, first, last):
                    with dve.If(first < last):
                        dve.wait_ge(sums_psum, t + last + 1)
                        dve.tensor_tensor(block_sums(last), block_sums(last),
                                          psum[:, MORE, 0:ROW].rearrange("p (h c) -> p h c", h=HEADS), ALU.add).then_inc(acc_step, 1)

                def kv_variance(k, z):
                    dve.wait_ge(squares_ready, 2 * k + 2)
                    dve.tensor_reduce(kv_var[:], squares.rearrange("p a (h d) -> p (a h) d", d=MIX_DIM), AX.X,
                                      ALU.add).then_inc(var_ready, 1)
                    dve.wait_ge(var_ready, 3 * k + 1)
                    dve.tensor_scalar(kv_var[:], kv_var[:], 1.0 / MIX_DIM, EPS, ALU.mult, ALU.add).then_inc(var_ready, 1)
                    dve.wait_ge(var_ready, 3 * k + 2)
                    dve.tensor_tensor(kv_prod[:], kv_var[:, 0:MIX_HEADS], kv_var[:, MIX_HEADS:], ALU.mult).then_inc(var_ready, 1)

                def kv_scale(k, z):
                    dve.wait_ge(stdb_ready, k + 1)
                    dve.reciprocal(rk[:], rk[:]).then_inc(rk_ready, 1)
                    dve.wait_ge(rk_ready, k + 1)
                    keys = ks[:, z].rearrange("p (h d) -> p h d", d=MIX_DIM)
                    dve.tensor_tensor(keys, keys, rk[:].unsqueeze(2).to_broadcast([P, MIX_HEADS, MIX_DIM]), ALU.mult).then_inc(k_ready, 1)

                def kv_add(n):
                    dve.wait_ge(dots_psum, n + 1)
                    flat_dots = dots[:].rearrange("p a b -> p (a b)")
                    dve.tensor_tensor(flat_dots, flat_dots, psum[:, TAILS, :], ALU.add).then_inc(dots_added, 1)

                front(0, 0, 0)
                across(0, 0)
                one_hot(0, 0, 0)
                numerators(0, 0)

                def body(t, i, u, phase, more):
                    before, first, last = blocks(t, u)
                    k = i * 2 + u - 1
                    if more:
                        front(t + 1, i + (u + 1) // SLOTS, (u + 1) % SLOTS)
                    add_last(t - 1, before, first)
                    with dve.If(first < last):
                        one_hot(SLOTS, t, first + 1)
                    with dve.If(first + 1 < last):
                        if more:
                            across(t + 1, (u + 1) % SLOTS)
                        add_first(t, u, first)
                        with dve.Fori(first + 2, last + 1) as b:
                            dve.wait_ge(sums_psum, t + b)
                            dve.tensor_tensor(block_sums(b - 1), block_sums(b - 1),
                                              psum[:, MORE, 0:ROW].rearrange("p (h c) -> p h c", h=HEADS), ALU.add).then_inc(acc_step, 1)
                            one_hot(SLOTS, t, b)
                    if more:
                        one_hot((u + 1) % SLOTS, t + 1, last)
                        with dve.If(last < first + 2):
                            across(t + 1, (u + 1) % SLOTS)
                    if phase == "kv" and u:
                        kv_variance(k, u - 1)
                    if more:
                        numerators(t + 1, (u + 1) % SLOTS)
                    with dve.If(last < first + 2):
                        add_first(t, u, first)
                    dve.sem_inc(chunk_done, 1)
                    if phase == "kv" and u:
                        kv_scale(k, u - 1)
                    if phase == "kv" and u != 1:
                        kv_add(i * 2 + u // 2)

                def between():
                    kv_add(NODE_TILES)
                    dve.wait_ge(dots_added, NODE_TILES + 2)
                    for lo in (0, MIX_DIM):
                        dve.tensor_scalar(dots_diag[lo:lo + MIX_DIM, :, lo:lo + MIX_DIM], dots[lo:lo + MIX_DIM, :, lo:lo + MIX_DIM],
                                          1.0 / NODES, None, ALU.mult).then_inc(dots_masked, 1)
                    dve.wait_ge(g_psum, 1)
                    dve.tensor_copy(g.rearrange("p a b -> p (a b)").rearrange("p (a b) -> p a b", a=2), psum[:, KEYS:KEYS + 2, :]).then_inc(g_ready, 1)
                    dve.wait_ge(eff_psum, 1)
                    dve.tensor_copy(eff[:].rearrange("p a b -> p (a b)"), psum[:, TAILS, :]).then_inc(eff_ready, 1)

                def mixed_body(t, i, u, phase, more):
                    body(t, i, u, phase, more)
                    if phase == "mix":
                        pair = list(mix_tiles(i, u))
                        dve.wait_ge(mix_psum, pair[-1][0] + 1)
                        for n, z in pair:
                            dve.tensor_tensor(tile_of(x_res, n), tile_of(x_res, n), psum[:, VALUES, z * DIM:(z + 1) * DIM],
                                              ALU.add).then_inc(mix_added, 1)

                schedule((dve, mixed_body, between))
                add_last(CHUNKS - 1, first_of[SLOTS], first_of[SLOTS + 1])

            @block.scalar
            def _(act):
                def norm(n, t, z):
                    act.wait_ge(xtb_psum, n + 1)
                    nc.scalar.activation(xn[:, z], tile_of(x_res, t), ACT.Identity, bias=ln_shift[:, ds(t, 1)],
                                         scale=ln_rstd[:, ds(t, 1)]).then_inc(xnb_ready, 1)

                def evacuate(n, through, z, bank, at):
                    act.wait_ge(xtb_psum, through + 2)
                    nc.scalar.copy(xt[:, z], psum[:, bank, at:at + 2 * P].rearrange("p (k n) -> p k n", k=2)).then_inc(xtb_ready, 1)

                def masks(t, u):
                    nc.scalar.copy(hc(mask_f[:, u]), by_head(prev_mask, t))
                    nc.scalar.copy(hc(mask_b[:, u]), by_head(next_mask, t))
                    nc.scalar.copy(pass_now[:, u, 0], prev_pass[:, ds(t, 1)].to_broadcast([P, HEADS]))
                    nc.scalar.copy(pass_now[:, u, 1], next_pass[:, ds(t, 1)].to_broadcast([P, HEADS])).then_inc(masks_ready, 1)

                def open_masks(t):
                    act.wait_ge(masks_psum, t + 1)
                    nc.scalar.copy(pass_t[:], psum[0:HEADS, TAILS, 2 * P:4 * P]).then_inc(masks_copied, 1)

                def exponentials(t, u):
                    act.wait_ge(prep, PREP * t + 2)
                    act.sem_inc(masks_free, 1)
                    nc.scalar.copy(rows[:, u, :, HEAD_DIM::HEAD_COLS], ones_row[:].rearrange("p (c h) -> p c h", h=HEADS))
                    act.wait_ge(prep, PREP * t + 12)
                    nc.scalar.activation(ex[:], arg[:], ACT.Exp).then_inc(exp_ready, 1)

                act.wait_ge(main_init, 8)
                masks(0, 0)
                open_masks(0)
                masks(1, 1)
                exponentials(0, 0)

                def body(t, i, u, phase, more):
                    k = i * 2 + u
                    ahead = more and (u < SLOTS - 2 or not isinstance(t, int))
                    pair = [(n + NODE_TILES, n, z) for n, z in mix_tiles(i, u)] if phase == "mix" else []
                    if phase == "kv" and u < 2:
                        norm(k, k, u)
                    for n, tile, z in pair:
                        norm(n, tile, z)
                    if more:
                        open_masks(t + 1)
                    if phase == "kv" and u < 2:
                        evacuate(k, k + 1, u, VALUES, 0)
                    for n, tile, z in pair:
                        evacuate(n, pair[-1][0] + 1, z, KEYS, z * DIM)
                    if more:
                        exponentials(t + 1, (u + 1) % SLOTS)
                    if ahead:
                        masks(t + 2, (u + 2) % SLOTS)
                    if phase == "kv" and u:
                        act.wait_ge(var_ready, 3 * (k - 1) + 3)
                        nc.scalar.activation(rk[:], kv_prod[:], ACT.Sqrt).then_inc(stdb_ready, 1)
                    if phase == "kv" and u < 2:
                        act.wait_ge(kv_psum, k + 1)
                        for j in range(2):
                            nc.scalar.activation(squares[:, j], psum[:, KEYS + j, :], ACT.Square).then_inc(squares_ready, 1)
                        nc.scalar.copy(ks[:, u], psum[:, KEYS, :])
                        nc.scalar.copy(vs[:, u], psum[:, VALUES, :]).then_inc(v_ready, 1)

                def between():
                    act.wait_ge(wq_psum, 1)
                    nc.scalar.copy(wqt.rearrange("p a k n -> p (a k n)").rearrange("p (b n) -> p b n", b=2),
                                   psum[:, KEYS:KEYS + 2, :]).then_inc(wq_ready, 1)

                schedule((act, body, between))

            @block.tensor
            def _(pe):
                pe.sem_inc(xtb_psum, 2)
                pe.sem_inc(mix_added, 1)
                pe.sem_inc(chunk_done, 1)
                pe.sem_inc(v_ready, 1)
                pe.sem_inc(k_ready, 1)
                pe.wait_ge(main_init, 8)

                def mask_tails(t, u):
                    pe.wait_ge(masks_ready, t + 1)
                    for j in range(2):
                        last = nc.tensor.matmul(psum[0:HEADS, TAILS, (2 + j) * P:(3 + j) * P], pass_now[:, u, j], ident[:], start=True, stop=True)
                    last.then_inc(masks_psum, 1)

                def tails(t):
                    pe.wait_ge(prep, PREP * t + 4)
                    pe.wait_ge(masks_copied, t + 1)
                    for j, tile in enumerate((hc(max_f)[:, :, CHUNK_COLS - 1], hc(max_b)[:, :, 0])):
                        last = nc.tensor.matmul(psum[0:HEADS, TAILS, j * P:(j + 1) * P], tile, ident[:], start=True, stop=True)
                    last.then_inc(tails_psum, 1)

                def carries(t, u):
                    pe.wait_ge(prep, PREP * t + 6)
                    nc.tensor.matmul(psum[:, SMALL, 0:HEADS], carry_f[:, u, 0:P], ident[0:HEADS, 0:HEADS], start=True, stop=True)
                    nc.tensor.matmul(psum[:, SMALL, HEADS:2 * HEADS], carry_b[:, 1:P + 1], ident[0:HEADS, 0:HEADS],
                                     start=True, stop=True).then_inc(carries_psum, 1)

                def products(n, z):
                    pe.wait_ge(v_ready, n + 1)
                    pe.wait_ge(k_ready, n + 1)
                    for j in range(PAIRS):
                        last = nc.tensor.matmul(psum[:, TAILS, j * P:(j + 1) * P], vs[:, z, j * P:(j + 1) * P],
                                                ks[:, z, j * P:(j + 1) * P], start=True, stop=True)
                    last.then_inc(dots_psum, 1)

                def step(t, u, b, z, bank, between=lambda c: None):
                    pe.wait_ge(onehot_ready, t + b + 1)
                    if z < SLOTS:
                        pe.wait_ge(prep, PREP * t + PREP)
                    for c in range(CHUNK_COLS):
                        last = nc.tensor.matmul(psum[:, bank, 0:ROW], onehot[:, z, c], rows[:, u, c],
                                                start=(c == 0), stop=(c == CHUNK_COLS - 1))
                        between(c)
                    last.then_inc(sums_psum, 1)

                first_of = {}
                mask_tails(0, 0)
                tails(0)
                carries(0, 0)
                pe.wait_ge(centred, 6)

                def transposes(n, z, bank, at):
                    pe.wait_ge(xnb_ready, n + 1)
                    for j in range(2):
                        last = nc.tensor.transpose(psum[:, bank, at + j * P:at + (j + 1) * P], xn[:, z, j * P:(j + 1) * P], ident[:])
                    last.then_inc(xtb_psum, 1)

                def body(t, i, u, phase, more):
                    if u == 0:
                        first_of[0] = pe.value_load(last_block[P - 1:P, ds(t + 1, 1)], min_val=0, max_val=NODE_TILES - 1)
                    first_of[u + 1] = pe.value_load(last_block[P - 1:P, ds(t + 2, 1)], min_val=0, max_val=NODE_TILES - 1)
                    first, last_b = first_of[u], first_of[u + 1]

                    k = i * 2 + u
                    pair = list(mix_tiles(i, u)) if phase == "mix" else []

                    def mix():
                        if pair:
                            pe.wait_ge(mix_added, pair[0][0] + 1)
                        for n, z in pair:
                            pe.wait_ge(xtb_ready, n + NODE_TILES + 1)
                            nc.tensor.matmul(psum[:, VALUES, z * DIM:(z + 1) * DIM], ones_b[:], bsum[:], start=True, stop=False)
                            for half in range(2):
                                last = nc.tensor.matmul(psum[:, VALUES, z * DIM:(z + 1) * DIM], xt[:, z, half], eff[:, half],
                                                        start=False, stop=(half == 1))
                            last.then_inc(mix_psum, 1)

                    def between_products(c):
                        if c == 7:
                            pe.wait_ge(chunk_done, t + 1)
                            nc.tensor.matmul(psum[:, SMALL, 16:16 + HEADS], onehot[0:1, u, 0, :], decay[:, u], start=True, stop=True)
                        if more and c == 0:
                            if phase == "kv" and u != 2:
                                pe.wait_ge(dots_added, i * 2 + u + 1)
                            mask_tails(t + 1, (u + 1) % SLOTS)
                        if more and c == 3:
                            tails(t + 1)
                        if c == 5 and phase == "kv" and u < 2:
                            transposes(k, u, VALUES, 0)
                        if c == 5:
                            for n, z in pair:
                                transposes(n + NODE_TILES, z, KEYS, z * DIM)
                        if more and c == 8:
                            carries(t + 1, (u + 1) % SLOTS)
                        if c == CHUNK_COLS - 4 and phase == "kv" and u != 1:
                            products(i * 2 + u // 2, 1 - u // 2)
                        if c == CHUNK_COLS - 2:
                            mix()

                    step(t, u, first, u, SUMS + u, between_products)
                    with pe.If(first < last_b):
                        with pe.Fori(first + 1, last_b + 1) as b:
                            step(t, u, b, SLOTS, MORE)
                    pe.wait_ge(sums_psum, t + last_b + 1)
                    pe.sem_inc(chunk_free, 1)
                    if phase == "kv" and u < 2:
                        pe.wait_ge(xtb_ready, k + 1)
                        for j in range(2):
                            for half in range(2):
                                last = nc.tensor.matmul(psum[:, KEYS + j, :], xt[:, u, half], wqkv[:, half, (1 + j) * INNER:(2 + j) * INNER],
                                                        start=(half == 0), stop=(half == 1))
                        last.then_inc(kv_psum, 1)

                def between():
                    pe.wait_ge(dots_added, NODE_TILES + 1)
                    products(NODE_TILES, 1)
                    for j in range(PAIRS):
                        for half in range(2):
                            n = (2 * j + half) * P
                            last = nc.tensor.transpose(psum[:, KEYS + n // 512, n % 512:n % 512 + P], wqkv[:, half, j * P:(j + 1) * P], ident[:])
                    last.then_inc(wq_psum, 1)
                    pe.wait_ge(dots_masked, 2)
                    pe.wait_ge(wq_ready, 1)
                    for j in range(PAIRS):
                        n = j * DIM
                        last = nc.tensor.matmul(psum[:, KEYS + n // 512, n % 512:n % 512 + DIM], dots_diag[:, j], wout[:, j], start=True, stop=True)
                    last.then_inc(g_psum, 1)
                    pe.wait_ge(g_ready, 1)
                    for half in range(2):
                        for j in range(PAIRS):
                            last = nc.tensor.matmul(psum[:, TAILS, half * DIM:(half + 1) * DIM], wqt[:, j, half], g[:, j],
                                                    start=(j == 0), stop=(j == PAIRS - 1))
                    last.then_inc(eff_psum, 1)
                    pe.wait_ge(eff_ready, 1)

                schedule((pe, body, between))

        tail_step, ln2_std, wts_in, small_in = sem("tail_step"), sem("ln2_std"), sem("wts_in"), sem("small_in")
        wt_psum, wt_ready, w_stored, w_row_in = sem("wt_psum"), sem("wt_ready"), sem("w_stored"), sem("w_row_in")
        xf_staged, xf_psum, xf_ready = sem("xf_staged"), sem("xf_psum"), sem("xf_ready")
        h_psum, h_ready, y_psum, y_ready, ones_ready = (sem(n) for n in ("h_psum", "h_ready", "y_psum", "y_ready", "ones_ready"))
        out_ready, out_stored = sem("out_ready"), sem("out_stored")
        HEAD_GROUPS = 3
        OUT_TILES = 5
        with ExitStack() as st:
            w1 = sb("w1", [P, 2, HIDDEN], f32, st)
            w2 = sb("w2", [P, HID_TILES, DIM], f32, st)
            b1 = sb("b1", [P, HID_TILES], f32, st)
            wr = sb("wr", [P, DIM], f32, st)
            br = sb("br", [P, 1], f32, st)
            b2 = sb("b2", [1, DIM], f32, st)
            ones = sb("ones", [1, P], f32, st)
            rden = sb("rden", [P, NODE_TILES * HEADS], f32, st)
            y_all = sb("y_all", [P, NODE_TILES, DIM], f32, st)
            weight = sb("weight", [P, NODE_TILES], f32, st)
            weight_t = sb("weight_t", [NODE_TILES, P], f32, st)
            w_row = sb("w_row", [P, NODES], f32, st)
            junk = sb("junk", [P, 2, NODES], bf16, st)
            junk_diag = sb("junk_diag", [P, P], bf16, st)
            lower = sb("lower", [P, P], f32, st)
            count = sb("count", [P, 3, NODE_TILES], f32, st)
            chosen = sb("chosen", [P, NODE_TILES], f32, st)
            weighted = sb("weighted", [P, 2, DIM], f32, st)
            xf = sb("xf", [P, GROUP_TILES, DIM], f32, st)
            xft = sb("xft", [P, 2, GROUP_TOKENS], f32, st)
            hid = sb("hid", [P, HID_TILES, GROUP_TOKENS], f32, st)
            xn2 = acc[:].rearrange("p t h c -> p (t h c)")[:, 0:NODE_TILES * DIM].rearrange("p (t d) -> p t d", d=DIM)
            flat_x = x_res[:].rearrange("p t d -> p (t d)")
            heads = acc[:].rearrange("p t h c -> p (t h) c")
            block = st.enter_context(nc.Block())

            @block.vector
            def _(dve):
                done = [0]

                def then(ins):
                    done[0] += 1
                    ins.then_inc(tail_step, 1)
                    dve.wait_ge(tail_step, done[0])

                x_heads = flat_x.rearrange("p (t d) -> p t d", d=HEAD_DIM)
                then(dve.tensor_scalar(rden[:], heads[:, :, HEAD_DIM], 1e-30, None, ALU.max))
                then(dve.reciprocal(rden[:], rden[:]))
                mid = HEAD_GROUPS * GROUP_TILES
                for part, (lo, hi) in enumerate(((0, mid), (mid, NODE_TILES))):
                    hs = slice(lo * HEADS, hi * HEADS)
                    then(dve.tensor_tensor(heads[:, hs, 0:HEAD_DIM], heads[:, hs, 0:HEAD_DIM],
                                           rden[:, hs].unsqueeze(2).to_broadcast([P, (hi - lo) * HEADS, HEAD_DIM]), ALU.mult))
                    then(dve.tensor_tensor(x_heads[:, hs], x_heads[:, hs], heads[:, hs, 0:HEAD_DIM], ALU.add))
                    with dve.Fori(lo, hi) as t:
                        dve.bn_stats(tile_of(bn, t), tile_of(x_res, t)).then_inc(tail_step, 1)
                    done[0] += hi - lo
                    dve.wait_ge(tail_step, done[0])
                    moments(dve, then, lo, hi)
                    marks["variance %d" % part] = done[0]
                    dve.wait_ge(ln2_std, part + 1)
                    then(dve.reciprocal(ln_rstd[:, lo:hi], ln_rstd[:, lo:hi]))
                    with dve.Fori(lo, hi) as t:
                        dve.tensor_scalar(tile_of(xn2, t), tile_of(x_res, t), ln_mean[:, ds(t, 1)], ln_rstd[:, ds(t, 1)],
                                          ALU.subtract, ALU.mult).then_inc(tail_step, 1)
                    done[0] += hi - lo
                    marks["xn %d" % part] = done[0]
                    dve.wait_ge(tail_step, done[0])
                dve.wait_ge(small_in, 64)
                for t in range(NODE_TILES):
                    dve.scalar_tensor_tensor(weighted[:, t % 2], xn2[:, t], 1.0, wr[:], ALU.mult, ALU.mult,
                                             accum_out=weight[:, t:t + 1]).then_inc(tail_step, 1)
                    done[0] += 1
                    if t:
                        dve.wait_ge(tail_step, done[0] - 1)
                dve.wait_ge(tail_step, done[0])
                then(dve.tensor_scalar(weight[:], weight[:], br[:], None, ALU.add))
                marks["weight"] = done[0]
                then(dve.tensor_tensor(x_res[:], x_res[:], xn2, ALU.add))
                dve.wait_ge(w_row_in, 16)
                dve.wait_ge(ones_ready, 3)
                then(dve.memset(count[:], 0.0))
                for t in range(NODE_TILES):
                    lo, hi = t * P, min((t + 1) * P, NODES)
                    w_t = weight[:, t:t + 1]
                    if t:
                        dve.tensor_scalar(junk[:, 0, 0:lo], w_row[:, 0:lo], w_t, None, ALU.is_ge, ALU.add,
                                          accum_out=count[:, 0, t:t + 1])
                    dve.tensor_scalar(junk[:, 1, lo:NODES], w_row[:, lo:NODES], w_t, None, ALU.is_gt, ALU.add,
                                      accum_out=count[:, 1, t:t + 1])
                    then(dve.scalar_tensor_tensor(junk_diag[:, 0:hi - lo], w_row[:, lo:hi], w_t, lower[:, 0:hi - lo],
                                                  ALU.is_equal, ALU.mult, accum_out=count[:, 2, t:t + 1]))
                    if t % OUT_TILES == OUT_TILES - 1:
                        ts = slice(t + 1 - OUT_TILES, t + 1)
                        then(dve.tensor_tensor(count[:, 0, ts], count[:, 0, ts], count[:, 1, ts], ALU.add))
                        then(dve.tensor_tensor(count[:, 0, ts], count[:, 0, ts], count[:, 2, ts], ALU.add))
                        then(dve.scalar_tensor_tensor(chosen[:, ts], count[:, 0, ts], float(SELECTED), weight[:, ts],
                                                      ALU.is_lt, ALU.mult))
                        for o in range(t + 1 - OUT_TILES, t + 1):
                            dve.wait_ge(y_ready, o + 1)
                            dve.scalar_tensor_tensor(y_all[:, o], y_all[:, o], chosen[:, o:o + 1], x_res[:, o],
                                                     ALU.mult, ALU.add).then_inc(out_ready, 1)

            @block.sync
            def _(sp):
                sp.dma_start(w1[:], a["w1"].rearrange("(k p) n -> p k n", p=P)).then_inc(wts_in, 16)
                sp.dma_start(w2[:], a["w2"].rearrange("(k p) n -> p k n", p=P)).then_inc(wts_in, 16)
                sp.dma_start(wr[:], a["wr"].partition_broadcast(P)).then_inc(small_in, 16)
                sp.dma_start(br[:], a["br"].partition_broadcast(P)).then_inc(small_in, 16)
                sp.dma_start(b1[:], a["b1"]).then_inc(small_in, 16)
                sp.dma_start(b2[:], a["b2"]).then_inc(small_in, 16)
                sp.wait_ge(wt_ready, 1)
                sp.dma_start(node_weights, weight_t[:]).then_inc(w_stored, 16)
                sp.wait_ge(w_stored, 16)
                sp.dma_start(w_row[:], node_weights.rearrange("t p -> (t p)")[0:NODES].partition_broadcast(P)).then_inc(w_row_in, 16)
                full = NODES // P
                for t in range(0, NODE_TILES, OUT_TILES):
                    n = min(OUT_TILES, full - t)
                    sp.wait_ge(out_ready, t + OUT_TILES)
                    sp.dma_start(out[t * P:(t + n) * P, :].rearrange("(t p) d -> p t d", p=P), y_all[:, t:t + n]).then_inc(out_stored, 16)
                sp.dma_start(out[full * P:NODES, :], y_all[0:NODES - full * P, full]).then_inc(out_stored, 16)
                sp.wait_ge(out_stored, 16 * (NODE_TILES // OUT_TILES + 1))

            @block.gpsimd
            def _(pool):
                pool.memset(ones[:], 1.0).then_inc(ones_ready, 1)
                pool.memset(lower[:], 1.0).then_inc(ones_ready, 1)
                pool.wait_ge(ones_ready, 2)
                pool.affine_select(out=lower[:], in_=lower[:], compare_op=ALU.is_gt, fill=0.0, base=0,
                                   pattern=[[-1, P]], channel_multiplier=1).then_inc(ones_ready, 1)

            @block.scalar
            def _(act):
                lo_hi = ((0, HEAD_GROUPS * GROUP_TILES), (HEAD_GROUPS * GROUP_TILES, NODE_TILES))

                def root(part):
                    lo, hi = lo_hi[part]
                    act.wait_ge(tail_step, marks["variance %d" % part])
                    nc.scalar.activation(ln_rstd[:, lo:hi], ln_u[:, lo:hi], ACT.Sqrt).then_inc(ln2_std, 1)

                def stage(g):
                    for j in range(GROUP_TILES):
                        act.wait_ge(xf_psum, GROUP_TILES * g + j + 1)
                        nc.scalar.copy(xf[:, j], tile_of(xn2, g * GROUP_TILES + j)).then_inc(xf_staged, 1)

                def evacuate(g):
                    for j in range(GROUP_TILES):
                        act.wait_ge(xf_psum, GROUP_TILES * g + j + 1 + GROUP_TILES)
                        nc.scalar.copy(xft[:, :, j * P:(j + 1) * P], psum[:, j % 2, 0:2 * P].rearrange("p (k n) -> p k n", k=2)).then_inc(xf_ready, 1)

                def group(g, more=True):
                    if more:
                        stage(g + 1)
                    for c in range(HID_TILES):
                        act.wait_ge(h_psum, HID_TILES * g + c + 1)
                        nc.scalar.activation(hid[:, c], psum[:, 2 + c % 2, 0:GROUP_TOKENS], ACT.Gelu_apprx_tanh,
                                             bias=b1[:, c:c + 1]).then_inc(h_ready, 1)
                    if more:
                        evacuate(g + 1)
                    for j in range(GROUP_TILES):
                        act.wait_ge(y_psum, GROUP_TILES * g + j + 1)
                        nc.scalar.copy(tile_of(y_all, g * GROUP_TILES + j), psum[:, 4 + j % 2, 0:DIM]).then_inc(y_ready, 1)

                root(0)
                act.wait_ge(tail_step, marks["xn 0"])
                stage(0)
                evacuate(0)
                act.wait_ge(small_in, 64)
                group(0)
                group(1)
                root(1)
                act.wait_ge(tail_step, marks["xn 1"])
                group(2)
                group(3)
                group(4)
                act.wait_ge(wt_psum, 1)
                nc.scalar.copy(weight_t[:], psum[0:NODE_TILES, 7, 0:P]).then_inc(wt_ready, 1)
                with act.Fori(5, GROUPS - 1) as g:
                    group(g)
                group(GROUPS - 1, False)

            @block.tensor
            def _(pe):
                pe.sem_inc(xf_psum, GROUP_TILES)

                def transposes(g):
                    for j in range(GROUP_TILES):
                        pe.wait_ge(xf_staged, GROUP_TILES * g + j + 1)
                        if j == 2:
                            pe.wait_ge(xf_ready, GROUP_TILES * g + 1)
                        for k in range(2):
                            last = nc.tensor.transpose(psum[:, j % 2, k * P:(k + 1) * P], xf[:, j, k * P:(k + 1) * P], ident[:])
                        last.then_inc(xf_psum, 1)

                def group(g, more=True):
                    pe.wait_ge(xf_ready, GROUP_TILES * g + GROUP_TILES)
                    for c in range(HID_TILES):
                        if c >= 2:
                            pe.wait_ge(h_ready, HID_TILES * g + c - 1)
                        for k in range(2):
                            last = nc.tensor.matmul(psum[:, 2 + c % 2, 0:GROUP_TOKENS], w1[:, k, c * P:(c + 1) * P], xft[:, k],
                                                    start=(k == 0), stop=(k == 1))
                        last.then_inc(h_psum, 1)
                    if more:
                        transposes(g + 1)
                    pe.wait_ge(h_ready, HID_TILES * g + HID_TILES)
                    for j in range(GROUP_TILES):
                        if j == 2:
                            pe.wait_ge(y_ready, GROUP_TILES * g + 1)
                        nc.tensor.matmul(psum[:, 4 + j % 2, 0:DIM], ones[:], b2[:], start=True, stop=False)
                        for c in range(HID_TILES):
                            last = nc.tensor.matmul(psum[:, 4 + j % 2, 0:DIM], hid[:, c, j * P:(j + 1) * P], w2[:, c],
                                                    start=False, stop=(c == HID_TILES - 1))
                        last.then_inc(y_psum, 1)

                transposes(0)
                pe.wait_ge(wts_in, 32)
                pe.wait_ge(small_in, 64)
                pe.wait_ge(ones_ready, 3)
                for g in range(4):
                    group(g)
                pe.wait_ge(tail_step, marks["weight"])
                nc.tensor.matmul(psum[0:NODE_TILES, 7, 0:P], weight[:], ident[:], start=True, stop=True).then_inc(wt_psum, 1)
                group(4)
                with pe.Fori(5, GROUPS - 1) as g:
                    group(g)
                group(GROUPS - 1, False)


def kernel(x, src, dst, edge_type_8, L0_gnn_conv_weights, L0_gnn_attn_l, L0_gnn_attn_r, L0_gnn_h_bias,
           L0_mix_w_qkv, L0_mix_w_out, L0_mix_b_out, L0_ffn_attention_mask, L0_ffn_wr, L0_ffn_br,
           L0_ffn_w1, L0_ffn_b1, L0_ffn_w2, L0_ffn_b2):
    import numpy as np
    import concourse.bacc as bacc
    from concourse.bass_utils import run_bass_kernel_spmd as run

    def chunks(values, fill):
        padded = np.full(EDGES_PAD, fill, values.dtype)
        padded[:EDGES] = values
        return padded

    def lay(padded):
        return padded.reshape(CHUNKS, P, CHUNK_COLS).transpose(1, 0, 2).reshape(P, -1)

    src, dst, kind = (np.asarray(v) for v in (src, dst, edge_type_8))
    dst_pad = chunks(dst, NODES_PAD - 1)
    before = np.concatenate([np.full(1, -1, dst.dtype), dst_pad[:-1]])
    after = np.concatenate([dst_pad[1:], np.full(1, -1, dst.dtype)])
    x = np.asarray(x)
    x_pad = np.zeros((NODES_PAD, DIM), x.dtype)
    x_pad[:NODES] = x
    arrays = {
        "edges": np.stack([lay(v) for v in (chunks(src, NODES_PAD - 1), dst_pad, before, after, chunks(kind, 0))], 1),
        "flat": np.stack([v.reshape(P, -1) for v in (dst_pad, before, chunks(kind, 0))], 1),
        "row_first": dst_pad[::SEARCH_ROW],
        "x": x_pad,
        "conv": np.asarray(L0_gnn_conv_weights),
        "attn_l": np.asarray(L0_gnn_attn_l), "attn_r": np.asarray(L0_gnn_attn_r),
        "h_bias": np.asarray(L0_gnn_h_bias), "b_out": np.asarray(L0_mix_b_out),
        "wqkv": np.asarray(L0_mix_w_qkv), "wout": np.asarray(L0_mix_w_out),
        "wr": np.asarray(L0_ffn_wr).reshape(DIM), "br": np.asarray(L0_ffn_br),
        "w1": np.asarray(L0_ffn_w1), "w2": np.asarray(L0_ffn_w2),
        "b1": np.asarray(L0_ffn_b1).reshape(HID_TILES, P).T, "b2": np.asarray(L0_ffn_b2).reshape(1, DIM),
    }
    nc = bacc.Bacc("TRN2", target_bir_lowering=False, num_devices=1)
    arrays = {f"in_{k}": np.ascontiguousarray(v) for k, v in arrays.items()}
    aps = {k[3:]: nc.dram_tensor(k, v.shape, mybir.dt.from_np(v.dtype), kind="ExternalInput").ap() for k, v in arrays.items()}
    out = nc.dram_tensor("out", (NODES, DIM), mybir.dt.float32, kind="ExternalOutput").ap()
    gps_layer(nc, aps, out)
    r = run(nc, [arrays], core_ids=[0])
    return r.results[0]["out"]
```

```python
import concourse.bass as bass
from concourse import mybir
from contextlib import ExitStack

NODES, DIM = 3750, 256
P = 128
NODE_TILES = -(-NODES // P)
NODES_PAD = NODE_TILES * P
RELS, HEADS, HEAD_DIM = 8, 4, 64
HEAD_COLS = HEAD_DIM + 1
ROW = HEADS * HEAD_COLS
EDGES = 120000
CHUNK_COLS = 15
SLOTS = 3
CHUNK_EDGES = P * CHUNK_COLS
CHUNKS = -(-EDGES // CHUNK_EDGES)
EDGES_PAD = CHUNKS * CHUNK_EDGES
CE = CHUNK_COLS * HEADS
ACT_COLS = 3
MIX_HEADS, MIX_DIM = 8, 64
INNER = MIX_HEADS * MIX_DIM
HIDDEN = 4 * DIM
HID_TILES = HIDDEN // P
SELECTED = NODES // 2 - 1
GROUP_TILES = 3
GROUPS = NODE_TILES // GROUP_TILES
GROUP_TOKENS = GROUP_TILES * P
ITERS = CHUNKS // SLOTS
KV_ITERS = NODE_TILES // 2
MIX_ITERS = ITERS - KV_ITERS
MIX_TILES = NODE_TILES // MIX_ITERS
SEARCH_ROW = 336
SEARCH_ROWS = EDGES_PAD // SEARCH_ROW
PART_EDGES = EDGES_PAD // P
PIECE = 105
PIECES = PART_EDGES // PIECE
EPS = 1e-5
SLOPE = 0.2
BIG = 1e38
assert CHUNKS % SLOTS == 0 and NODE_TILES % 2 == 0 and NODE_TILES % GROUP_TILES == 0
assert MIX_ITERS * MIX_TILES == NODE_TILES and MIX_TILES <= 2 * SLOTS
assert SEARCH_ROW * SEARCH_ROWS == EDGES_PAD and PART_EDGES * P == EDGES_PAD and PIECE * PIECES == PART_EDGES


def gps_layer(nc, a, out):
    f32, i32, bf16 = mybir.dt.float32, mybir.dt.int32, mybir.dt.bfloat16
    ALU, ACT, AX = mybir.AluOpType, mybir.ActivationFunctionType, mybir.AxisListType
    ds = bass.ds

    ctx = ExitStack()
    with ctx:
        def sb(name, shape, dt=f32, where=ctx):
            return where.enter_context(nc.sbuf_tensor(name, shape, dt))

        def sem(name):
            return ctx.enter_context(nc.semaphore(name))

        def dram(name, shape):
            return nc.dram_tensor(name, shape, f32, kind="Internal").ap()

        features = dram("features", (NODES_PAD * RELS, ROW))
        dst_logits = dram("dst_logits", (NODES_PAD, RELS * HEADS))
        heads_of_runs = dram("heads_of_runs", (EDGES_PAD, RELS * HEADS))
        edge_logits = dram("edge_logits", (EDGES_PAD, HEADS))
        node_weights = dram("node_weights", (NODE_TILES, P))

        ident = sb("ident", [P, P])
        iota_free = sb("iota_free", [P, P])
        block_base = sb("block_base", [P, NODE_TILES + 1])
        x_res = sb("x_res", [P, NODE_TILES, DIM])
        acc = sb("acc", [P, NODE_TILES, HEADS, HEAD_COLS])
        bn = sb("bn", [P, NODE_TILES, 6])
        ln_mean = sb("ln_mean", [P, NODE_TILES])
        ln_rstd = sb("ln_rstd", [P, NODE_TILES])
        ln_shift = sb("ln_shift", [P, NODE_TILES])
        ln_t = sb("ln_t", [P, NODE_TILES])
        ln_u = sb("ln_u", [P, NODE_TILES])
        ET = CHUNKS * CHUNK_COLS
        feat_idx = sb("feat_idx", [P, ET], i32)
        dst_f = sb("dst_f", [P, ET])
        prev_mask = sb("prev_mask", [P, ET], bf16)
        next_mask = sb("next_mask", [P, ET], bf16)
        first_run = sb("first_run", [P, ET], bf16)
        last_run = sb("last_run", [P, ET], bf16)
        prev_open = sb("prev_open", [P, CHUNKS])
        next_open = sb("next_open", [P, CHUNKS])
        prev_pass = sb("prev_pass", [P, CHUNKS])
        next_pass = sb("next_pass", [P, CHUNKS])
        last_block = sb("last_block", [P, CHUNKS + 2], i32)

        psum = ctx.enter_context(nc.psum_tensor("psum", [P, 8, 512], f32))

        def tile_of(tensor, t):
            return tensor[:, ds(t, 1), :].rearrange("p o d -> p (o d)")

        def moments(dve, then, lo, hi, eps=EPS):
            b, t, u, m = bn[:, lo:hi], ln_t[:, lo:hi], ln_u[:, lo:hi], ln_mean[:, lo:hi]
            dve.tensor_tensor(t, b[:, :, 1], b[:, :, 4], ALU.subtract)
            dve.tensor_tensor(u, b[:, :, 2], b[:, :, 5], ALU.add)
            then(dve.tensor_tensor(m, b[:, :, 1], b[:, :, 4], ALU.add))
            dve.tensor_scalar(m, m, 0.5, None, ALU.mult)
            then(dve.tensor_tensor(t, t, t, ALU.mult))
            then(dve.tensor_scalar(u, u, 1.0 / DIM, eps, ALU.mult, ALU.add))
            then(dve.scalar_tensor_tensor(u, t, 0.25, u, ALU.mult, ALU.add))

        row_first_in, flat_in, edges_in, conv_in = (sem(n) for n in ("row_first_in", "flat_in", "edges_in", "conv_in"))
        attn_in = [sem("attn_l_in"), sem("attn_r_in")]
        x_in = [sem("x_in0"), sem("x_in1"), sem("x_in2")]
        const_ready, setup_done, std_ready = sem("const_ready"), sem("setup_done"), sem("std_ready")
        xn_ready, xt_psum, xt_ready = sem("xn_ready"), sem("xt_psum"), sem("xt_ready")
        logit_psum, logit_ready, logits_stored = sem("logit_psum"), sem("logit_ready"), sem("logits_stored")
        feat_psum, feat_ready = sem("feat_psum"), sem("feat_ready")
        store = [sem("store0"), sem("store1")]
        zeroed, rows_found = sem("zeroed"), [sem("rows_found0"), sem("rows_found1")]
        firsts_shifted, scattered, start_in = sem("firsts_shifted"), sem("scattered"), sem("start_in")
        piece_in, piece_done, piece_stored = [sem("piece_in0"), sem("piece_in1")], sem("piece_done"), [sem("piece_stored0"), sem("piece_stored1")]
        staged_seen = sem("staged_seen")
        HALF = NODE_TILES // 2
        LOGITS = RELS * HEADS
        LOGIT_TILES = 6
        X_PARTS = 3
        PART_TILES = NODE_TILES // X_PARTS
        marks = {}

        with ExitStack() as st:
            conv = sb("conv", [P, 2, LOGITS, HEAD_COLS], f32, st)
            attn = sb("attn", [P, 2, LOGITS, HEAD_DIM], f32, st)
            conv_er = sb("conv_er", [P, 2, LOGITS], f32, st)
            table = sb("table", [P, 2, RELS, ROW], f32, st)
            er_all = sb("er_all", [P, NODE_TILES, LOGITS], f32, st)
            xn = sb("xn", [P, LOGIT_TILES, DIM], f32, st)
            xt = sb("xt", [P, LOGIT_TILES, 2, P], f32, st)
            zeros = sb("zeros", [P, PART_EDGES // 3], f32, st)
            pieces = sb("pieces", [P, 3, PIECE * LOGITS], f32, st)
            row_first_i = sb("row_first_i", [P, SEARCH_ROWS], i32, st)
            row_first = sb("row_first", [P, SEARCH_ROWS], f32, st)
            node_id = sb("node_id", [P, NODE_TILES], f32, st)
            below = sb("below", [P, NODE_TILES], f32, st)
            row_of = sb("row_of", [P, NODE_TILES], f32, st)
            row_idx = sb("row_idx", [P, NODE_TILES], i32, st)
            first_f = sb("first_f", [P, NODE_TILES], f32, st)
            next_first = sb("next_first", [P, NODE_TILES], f32, st)
            absent = sb("absent", [P, NODE_TILES], f32, st)
            scatter_idx = sb("scatter_idx", [P, NODE_TILES], i32, st)
            keep = sb("keep", [P, PART_EDGES], f32, st)
            kind_f = sb("kind_f", [P, PART_EDGES], f32, st)
            kind_no = sb("kind_no", [P, RELS], f32, st)
            kind_is = sb("kind_is", [P, PIECE, RELS], f32, st)
            start_idx = sb("start_idx", [P, 1], i32, st)
            start = sb("start", [P, LOGITS], f32, st)
            carry = sb("carry", [P, LOGITS], f32, st)
            edge_er = sb("edge_er", [P, 2, PIECE, HEADS], f32, st)
            scratch = acc[:].rearrange("p t h c -> p (t h c)").bitcast(i32)
            raw = scratch[:, 0:5 * ET].rearrange("p (j e) -> p j e", j=5)
            flat = scratch[:, 5 * ET:5 * ET + 3 * PART_EDGES].rearrange("p (j e) -> p j e", j=3)
            found = pieces[:].rearrange("p a b -> p (a b)").bitcast(i32)[:, 0:NODE_TILES * SEARCH_ROW].rearrange("p (t e) -> p t e", e=SEARCH_ROW)
            block = st.enter_context(nc.Block())

            @block.vector
            def _(dve):
                done = [0]

                def then(ins):
                    done[0] += 1
                    ins.then_inc(setup_done, 1)
                    dve.wait_ge(setup_done, done[0])

                then(dve.memset(zeros[:], 0.0))
                marks["zeros"] = done[0]
                then(dve.memset(next_first[:], -1.0))
                for j in range(X_PARTS):
                    dve.wait_ge(x_in[j], 16)
                    with dve.Fori(0, PART_TILES // 5) as i:
                        for u in range(5):
                            t = j * PART_TILES + i * 5 + u
                            dve.bn_stats(tile_of(bn, t), tile_of(x_res, t)).then_inc(setup_done, 1)
                    done[0] += PART_TILES
                dve.wait_ge(setup_done, done[0])
                moments(dve, then, 0, NODE_TILES)
                marks["variance"] = done[0]
                lower_row = pieces[:].rearrange("p a b -> p (a b)").bitcast(bf16)[:, 0:HALF * SEARCH_ROWS].rearrange("p (t e) -> p t e", e=SEARCH_ROWS)

                def search_rows(h):
                    ts = slice(h * HALF, (h + 1) * HALF)
                    then(dve.tensor_tensor(lower_row, row_first[:].unsqueeze(1).to_broadcast([P, HALF, SEARCH_ROWS]),
                                           node_id[:, ts].unsqueeze(2).to_broadcast([P, HALF, SEARCH_ROWS]), ALU.is_lt))
                    then(dve.tensor_reduce(row_of[:, ts], lower_row, AX.X, ALU.add))
                    then(dve.tensor_scalar(row_of[:, ts], row_of[:, ts], -1.0, 0.0, ALU.add, ALU.max))
                    then(dve.tensor_copy(row_idx[:, ts], row_of[:, ts]))
                    marks["rows %d" % h] = done[0]

                dve.wait_ge(const_ready, 7)
                dve.wait_ge(row_first_in, 16)
                then(dve.tensor_copy(row_first[:], row_first_i[:]))
                search_rows(0)
                prod = table[:].rearrange("p a b c -> p (a b c)")[:, 0:LOGITS * HEAD_DIM].rearrange("p (h d) -> p h d", d=HEAD_DIM)
                dve.wait_ge(conv_in, 32)
                dve.wait_ge(attn_in[1], 16)
                then(dve.tensor_tensor(prod, conv[:, 0, :, 0:HEAD_DIM], attn[:, 1], ALU.mult))
                dve.wait_ge(std_ready, 1)
                then(dve.reciprocal(ln_rstd[:], ln_rstd[:]))
                then(dve.scalar_tensor_tensor(ln_shift[:], ln_mean[:], -1.0, ln_rstd[:], ALU.mult, ALU.mult))
                marks["norm"] = done[0]
                then(dve.tensor_reduce(conv_er[:, 0], prod, AX.X, ALU.add))
                then(dve.tensor_tensor(prod, conv[:, 1, :, 0:HEAD_DIM], attn[:, 1], ALU.mult))
                then(dve.tensor_reduce(conv_er[:, 1], prod, AX.X, ALU.add))
                marks["dst weights"] = done[0]

                dve.wait_ge(flat_in, 16)
                then(dve.tensor_copy(start_idx[:], flat[:, 0, 0:1]))
                search_rows(1)
                dve.wait_ge(attn_in[0], 16)
                for k in range(2):
                    then(dve.tensor_tensor(prod, conv[:, k, :, 0:HEAD_DIM], attn[:, 0], ALU.mult))
                    then(dve.tensor_reduce(conv[:, k, :, HEAD_DIM], prod, AX.X, ALU.add))
                marks["src weights"] = done[0]
                dve.tensor_tensor(keep[:], flat[:, 0], flat[:, 1], ALU.is_equal)
                then(dve.tensor_copy(kind_f[:], flat[:, 2]))
                for h in range(2):
                    dve.wait_ge(rows_found[h], 16 * HALF)
                    for t in range(h * HALF, (h + 1) * HALF):
                        row = found[:, (t + HALF) % NODE_TILES]
                        last = dve.tensor_scalar(row, row, node_id[:, t:t + 1], None, ALU.is_lt, ALU.add, accum_out=below[:, t:t + 1])
                    then(last)
                then(dve.scalar_tensor_tensor(first_f[:], row_of[:], float(SEARCH_ROW), below[:], ALU.mult, ALU.add))
                marks["firsts"] = done[0]
                dve.wait_ge(firsts_shifted, 32)
                then(dve.tensor_tensor(absent[:], next_first[:], first_f[:], ALU.is_equal))
                then(dve.scalar_tensor_tensor(first_f[:], absent[:], float(2 * EDGES_PAD), first_f[:], ALU.mult, ALU.add))
                then(dve.tensor_copy(scatter_idx[:], first_f[:]))
                marks["scatter"] = done[0]

                dve.wait_ge(edges_in, 16)
                src, dst, before, after, kind = (raw[:, j] for j in range(5))
                run_start = pieces[:, 2, 0:ET]
                dve.scalar_tensor_tensor(feat_idx[:], src, float(RELS), kind, ALU.mult, ALU.add)
                dve.tensor_copy(dst_f[:], dst)
                dve.tensor_tensor(prev_mask[:], dst, before, ALU.is_equal)
                then(dve.tensor_tensor(next_mask[:], dst, after, ALU.is_equal))

                def cols(tile):
                    return tile.rearrange("p (t c) -> p t c", c=CHUNK_COLS)

                for mask, open_, pass_, run, edge, far, order in (
                        (prev_mask, prev_open, prev_pass, first_run, 0, CHUNK_COLS - 1, 1),
                        (next_mask, next_open, next_pass, last_run, CHUNK_COLS - 1, 0, -1)):
                    then(dve.tensor_scalar(open_[:], cols(mask[:])[:, :, edge], -1.0, BIG, ALU.add, ALU.mult))
                    then(dve.memset(cols(mask[:])[:, :, edge], 0.0))
                    then(dve.memset(run_start, 0.0))
                    then(dve.memset(cols(run_start)[:, :, edge], 1.0))
                    then(dve.tensor_tensor_scan(out=run[:, ::order], data0=mask[:, ::order], data1=run_start[:, ::order],
                                                initial=0.0, op0=ALU.mult, op1=ALU.max))
                    then(dve.tensor_scalar(run[:], run[:], -1.0, BIG, ALU.add, ALU.mult))
                    then(dve.tensor_tensor(pass_[:], cols(run[:])[:, :, far], open_[:], ALU.min))
                    then(dve.tensor_tensor(cols(run[:]), cols(run[:]), open_[:].unsqueeze(2).to_broadcast([P, CHUNKS, CHUNK_COLS]), ALU.min))
                    then(dve.tensor_scalar(mask[:], mask[:], -1.0, BIG, ALU.add, ALU.mult))
                then(dve.memset(last_block[:], 0))
                then(dve.tensor_single_scalar(last_block[:, 2:CHUNKS + 2], cols(dst)[:, :, CHUNK_COLS - 1],
                                              P.bit_length() - 1, ALU.arith_shift_right))

                marks["edge data"] = done[0]
                dve.wait_ge(start_in, 16)
                then(dve.tensor_copy(carry[:], start[:]))
                for i in range(PIECES):
                    z = i % 2
                    piece = pieces[:, z].rearrange("p (e j) -> p e j", j=LOGITS)
                    picked = pieces[:, 2].rearrange("p (e j) -> p e j", j=LOGITS)
                    part = slice(i * PIECE, (i + 1) * PIECE)
                    dve.tensor_tensor(kind_is[:], kind_f[:, part].unsqueeze(2).to_broadcast([P, PIECE, RELS]),
                                      kind_no[:].unsqueeze(1).to_broadcast([P, PIECE, RELS]), ALU.is_equal)
                    dve.wait_ge(piece_in[z], 16 * (i // 2 + 1))
                    for j in range(LOGITS):
                        last = dve.tensor_tensor_scan(out=piece[:, :, j], data0=keep[:, part], data1=piece[:, :, j],
                                                      initial=carry[:, j:j + 1], op0=ALU.mult, op1=ALU.add)
                    then(last)
                    dve.tensor_copy(carry[:], piece[:, PIECE - 1, :])
                    then(dve.tensor_tensor(picked.rearrange("p e (r h) -> p e r h", h=HEADS), piece.rearrange("p e (r h) -> p e r h", h=HEADS),
                                           kind_is[:].unsqueeze(3).to_broadcast([P, PIECE, RELS, HEADS]), ALU.mult))
                    marks["piece %d" % i] = done[0]
                    if i >= 2:
                        dve.wait_ge(piece_stored[z], 16 * (i // 2))
                    dve.tensor_reduce(edge_er[:, z], picked.rearrange("p e (r h) -> p e h r", h=HEADS), AX.X, ALU.add).then_inc(piece_done, 1)
                    dve.wait_ge(piece_done, i + 1)

            @block.sync
            def _(sp):
                for j in range(X_PARTS):
                    ts = slice(j * PART_TILES, (j + 1) * PART_TILES)
                    sp.dma_start(x_res[:, ts], a["x"].rearrange("(t p) d -> p t d", p=P)[:, ts]).then_inc(x_in[j], 16)
                sp.dma_start(row_first_i[:], a["row_first"].partition_broadcast(P)).then_inc(row_first_in, 16)
                for k in range(2):
                    sp.dma_start(conv[:, k, :, 0:HEAD_DIM],
                                 a["conv"].rearrange("r h (k p) d -> k p (r h) d", p=P)[k]).then_inc(conv_in, 16)
                sp.dma_start(attn[:, 1], a["attn_r"].rearrange("r h d -> (r h) d").partition_broadcast(P)).then_inc(attn_in[1], 16)
                sp.dma_start(flat, a["flat"]).then_inc(flat_in, 16)
                sp.dma_start(attn[:, 0], a["attn_l"].rearrange("r h d -> (r h) d").partition_broadcast(P)).then_inc(attn_in[0], 16)
                sp.dma_start(raw, a["edges"]).then_inc(edges_in, 16)
                runs = heads_of_runs.rearrange("(q e) j -> q (e j)", q=P)
                sp.wait_ge(setup_done, marks["zeros"])
                sp.dma_start(runs.rearrange("q (r e) -> q r e", e=PART_EDGES // 3),
                             zeros[:].unsqueeze(1).to_broadcast([P, 3 * LOGITS, PART_EDGES // 3])).then_inc(zeroed, 16)
                sp.wait_ge(setup_done, marks["firsts"])
                sp.dma_start(next_first[0:P - 1, :], first_f[1:P, :]).then_inc(firsts_shifted, 16)
                sp.dma_start(next_first[P - 1:P, 0:NODE_TILES - 1], first_f[0:1, 1:NODE_TILES]).then_inc(firsts_shifted, 16)
                sp.wait_ge(logit_ready, NODE_TILES // LOGIT_TILES + 1)
                sp.dma_start(dst_logits.rearrange("(t p) j -> p t j", p=P), er_all[:]).then_inc(logits_stored, 16)
                er_flat = edge_logits.rearrange("(q e) h -> q e h", q=P)
                sp.wait_ge(scattered, 16 * NODE_TILES)
                sp.wait_ge(setup_done, marks["edge data"])
                for i in range(PIECES + 1):
                    if i < PIECES:
                        if i >= 2:
                            sp.wait_ge(setup_done, marks["piece %d" % (i - 2)])
                        sp.dma_start(pieces[:, i % 2], runs[:, i * PIECE * LOGITS:(i + 1) * PIECE * LOGITS]).then_inc(piece_in[i % 2], 16)
                    if i >= 1:
                        sp.wait_ge(piece_done, i)
                        sp.dma_start(er_flat[:, (i - 1) * PIECE:i * PIECE, :], edge_er[:, (i - 1) % 2]).then_inc(piece_stored[(i - 1) % 2], 16)
                sp.wait_ge(piece_stored[0], 16 * ((PIECES + 1) // 2))
                sp.wait_ge(piece_stored[1], 16 * (PIECES // 2))

            @block.gpsimd
            def _(pool):
                pool.memset(ident[:], 0.0).then_inc(const_ready, 1)
                for tile, pattern, step in ((iota_free, [[1, P]], 0), (block_base, [[P, NODE_TILES + 1]], 0),
                                            (node_id, [[P, NODE_TILES]], 1), (kind_no, [[1, RELS]], 0)):
                    pool.iota(tile[:], pattern=pattern, base=0, channel_multiplier=step,
                              allow_small_or_imprecise_dtypes=True).then_inc(const_ready, 1)
                pool.wait_ge(const_ready, 5)
                pool.affine_select(out=ident[:], in_=ident[:], compare_op=ALU.not_equal, fill=1.0, base=0,
                                   pattern=[[-1, P]], channel_multiplier=1).then_inc(const_ready, 2)

                def gather(out_, table_, idx, rows_, signal):
                    pool.indirect_dma_start(out=out_, out_offset=None, in_=table_,
                                            in_offset=bass.IndirectOffsetOnAxis(ap=idx, axis=0),
                                            bounds_check=rows_ - 1, oob_is_err=True).then_inc(signal, 16)

                for t in range(NODE_TILES):
                    if t % HALF == 0:
                        pool.wait_ge(setup_done, marks["rows %d" % (t // HALF)])
                    gather(found[:, (t + HALF) % NODE_TILES], a["dst_rows"], row_idx[:, t:t + 1], SEARCH_ROWS, rows_found[t // HALF])
                pool.wait_ge(logits_stored, 16)
                gather(start[:], dst_logits, start_idx[:], NODES_PAD, start_in)
                pool.wait_ge(zeroed, 16)
                pool.wait_ge(setup_done, marks["scatter"])
                for t in range(NODE_TILES):
                    pool.indirect_dma_start(out=heads_of_runs, out_offset=bass.IndirectOffsetOnAxis(ap=scatter_idx[:, t:t + 1], axis=0),
                                            in_=er_all[:, t], in_offset=None,
                                            bounds_check=EDGES_PAD - 1, oob_is_err=False).then_inc(scattered, 16)

            @block.scalar
            def _(act):
                act.sem_inc(store[0], 16)
                act.sem_inc(store[1], 16)
                act.sem_inc(feat_ready, 4)
                act.wait_ge(setup_done, marks["variance"])
                nc.scalar.activation(ln_rstd[:], ln_u[:], ACT.Sqrt).then_inc(std_ready, 1)
                act.wait_ge(setup_done, marks["norm"])

                def norm(t, u):
                    act.wait_ge(xt_psum, t + 1)
                    nc.scalar.activation(xn[:, u], tile_of(x_res, t), ACT.Identity, bias=ln_shift[:, ds(t, 1)],
                                         scale=ln_rstd[:, ds(t, 1)]).then_inc(xn_ready, 1)

                def evacuate(n, u):
                    act.wait_ge(xt_psum, n + 1 + LOGIT_TILES)
                    nc.scalar.copy(xt[:, u], psum[:, u, 0:2 * P].rearrange("p (k n) -> p k n", k=2)).then_inc(xt_ready, 1)

                def logit_tiles(i, ahead=True):
                    for u in range(LOGIT_TILES):
                        evacuate(i * LOGIT_TILES + u, u)
                    for u in range(LOGIT_TILES if ahead else 0):
                        norm((i + 1) * LOGIT_TILES + u, u)
                    act.wait_ge(logit_psum, i + 1)
                    nc.scalar.copy(er_all[:, ds(i * LOGIT_TILES, LOGIT_TILES), :].rearrange("p t j -> p (t j)"),
                                   psum[:, 6, 0:LOGIT_TILES * LOGITS]).then_inc(logit_ready, 1)

                for u in range(LOGIT_TILES):
                    norm(u, u)
                with act.Fori(0, NODE_TILES // LOGIT_TILES - 1) as i:
                    logit_tiles(i)
                logit_tiles(NODE_TILES // LOGIT_TILES - 1, False)
                def norm2(t, u):
                    act.wait_ge(xt_psum, t + NODE_TILES + LOGIT_TILES - 1)
                    nc.scalar.activation(xn[:, u], tile_of(x_res, t), ACT.Identity, bias=ln_shift[:, ds(t, 1)],
                                         scale=ln_rstd[:, ds(t, 1)]).then_inc(xn_ready, 1)

                def tile(t, u, ahead):
                    if ahead:
                        norm2(t + 1, 1 - u)
                    act.wait_ge(store[u], (t // 2 if isinstance(t, int) else i_now[0]) * 16 + 16)
                    for r in range(RELS):
                        act.wait_ge(feat_psum, RELS * t + r + 1)
                        nc.scalar.copy(table[:, u, r], psum[:, 2 + r % 4, 0:ROW]).then_inc(feat_ready, 1)
                        if r == RELS // 2 and ahead:
                            evacuate(t + 1 + NODE_TILES, 1 - u)
                    act.wait_ge(feat_ready, RELS * t + RELS + 4)
                    act.dma_start(features.rearrange("(t n r) c -> t n (r c)", r=RELS, n=P)[ds(t, 1)].rearrange("o n c -> (o n) c"),
                                  table[:, u].rearrange("p r c -> p (r c)")).then_inc(store[u], 16)

                i_now = [0]
                norm2(0, 0)
                evacuate(NODE_TILES, 0)
                with act.Fori(0, NODE_TILES // 2 - 1) as i:
                    i_now[0] = i
                    for u in range(2):
                        tile(i * 2 + u, u, True)
                tile(NODE_TILES - 2, 0, True)
                tile(NODE_TILES - 1, 1, False)
                for u in range(2):
                    act.wait_ge(store[u], 16 * (NODE_TILES // 2) + 16)

            @block.tensor
            def _(pe):
                pe.sem_inc(xt_psum, LOGIT_TILES)
                pe.wait_ge(const_ready, 7)
                pe.sem_inc(logit_ready, 1)

                def transposes(t, u):
                    pe.wait_ge(xn_ready, t + 1)
                    for k in range(2):
                        last = nc.tensor.transpose(psum[:, u, k * P:(k + 1) * P], xn[:, u, k * P:(k + 1) * P], ident[:])
                    last.then_inc(xt_psum, 1)

                pe.wait_ge(setup_done, marks["dst weights"])
                with pe.Fori(0, NODE_TILES // LOGIT_TILES) as i:
                    for u in range(LOGIT_TILES):
                        transposes(i * LOGIT_TILES + u, u)
                    pe.wait_ge(logit_ready, i + 1)
                    for u in range(LOGIT_TILES):
                        pe.wait_ge(xt_ready, i * LOGIT_TILES + u + 1)
                        for k in range(2):
                            last = nc.tensor.matmul(psum[:, 6, u * LOGITS:(u + 1) * LOGITS], xt[:, u, k], conv_er[:, k],
                                                    start=(k == 0), stop=(k == 1))
                    last.then_inc(logit_psum, 1)

                def tile(t, u, ahead):
                    pe.wait_ge(xt_ready, t + NODE_TILES + 1)
                    for r in range(RELS):
                        pe.wait_ge(feat_ready, RELS * t + r + 1)
                        for k in range(2):
                            last = nc.tensor.matmul(psum[:, 2 + r % 4, 0:ROW], xt[:, u, k],
                                                    conv[:, k, r * HEADS:(r + 1) * HEADS, :].rearrange("p h c -> p (h c)"),
                                                    start=(k == 0), stop=(k == 1))
                        last.then_inc(feat_psum, 1)
                        if r == RELS // 4 and ahead:
                            transposes(t + 1 + NODE_TILES, 1 - u)

                transposes(NODE_TILES, 0)
                pe.wait_ge(setup_done, marks["src weights"])
                with pe.Fori(0, NODE_TILES // 2 - 1) as i:
                    for u in range(2):
                        tile(i * 2 + u, u, True)
                tile(NODE_TILES - 2, 0, True)
                tile(NODE_TILES - 1, 1, False)

        PREP = 12
        gathered = [sem(f"gathered{u}") for u in range(SLOTS)]
        er_in = [sem(f"er_in{u}") for u in range(SLOTS)]
        idx_staged, chunk_free, chunk_done, prep, er_seen = (sem(n) for n in ("idx_staged", "chunk_free", "chunk_done", "prep", "er_seen"))
        act_rows_ready, decay_psum, masks_ready, masks_free, masks_psum, tails_psum, masks_copied, carries_psum, exp_ready = sem("act_rows_ready"), sem("decay_psum"), sem("masks_ready"), sem("masks_free"), sem("masks_psum"), sem("tails_psum"), sem("masks_copied"), sem("carries_psum"), sem("exp_ready")
        onehot_ready, sums_psum = sem("onehot_ready"), sem("sums_psum")
        first_step, extra_added = sem("first_step"), sem("extra_added")
        main_init, mixw_in, bias_in, centred = sem("main_init"), sem("mixw_in"), sem("bias_in"), sem("centred")
        xnb_ready, xtb_psum, xtb_ready, keys_psum, values_psum = sem("xnb_ready"), sem("xtb_psum"), sem("xtb_ready"), sem("keys_psum"), sem("values_psum")
        squares_ready, v_ready, var_ready, stdb_ready = sem("squares_ready"), sem("v_ready"), sem("var_ready"), sem("stdb_ready")
        rk_ready, k_ready, dots_psum, dots_added = sem("rk_ready"), sem("k_ready"), sem("dots_psum"), sem("dots_added")
        wq_psum, wq_ready, g_psum, g_ready, eff_psum, eff_ready = (sem(n) for n in ("wq_psum", "wq_ready", "g_psum", "g_ready", "eff_psum", "eff_ready"))
        dots_masked, mix_psum, mix_added = sem("dots_masked"), sem("mix_psum"), sem("mix_added")
        PAIRS = MIX_HEADS // 2
        TAILS, SMALL, SUMS, MORE, KEYS, VALUES = 0, 1, 2, 5, 6, 7
        with ExitStack() as st:
            rows = sb("rows", [P, SLOTS, CHUNK_COLS, ROW], f32, st)
            er = sb("er", [P, SLOTS, CHUNK_COLS, HEADS], f32, st)
            idx_now = sb("idx_now", [P, SLOTS, CHUNK_COLS], i32, st)
            onehot = sb("onehot", [P, SLOTS + 1, CHUNK_COLS, P], f32, st)
            e = sb("e", [P, CE], f32, st)
            lin = sb("lin", [P, CE], f32, st)
            mask_f = sb("mask_f", [P, SLOTS, CE], f32, st)
            mask_b = sb("mask_b", [P, SLOTS, CE], f32, st)
            max_f = sb("max_f", [P, CE], f32, st)
            max_b = sb("max_b", [P, CE], f32, st)
            seg_max = sb("seg_max", [P, CE], f32, st)
            reach_f = sb("reach_f", [P, CE], f32, st)
            reach_b = sb("reach_b", [P, CE], f32, st)
            pass_now = sb("pass_now", [P, SLOTS, 2, HEADS], f32, st)
            pass_t = sb("pass_t", [HEADS, 2 * P], f32, st)
            carry_f = sb("carry_f", [HEADS, SLOTS, P + 1], f32, st)
            carry_b = sb("carry_b", [HEADS, P + 1], f32, st)
            from_prev = sb("from_prev", [P, HEADS], f32, st)
            ones_row = sb("ones_row", [P, CE], f32, st)
            arg = sb("arg", [P, CE + HEADS], f32, st)
            ex = sb("ex", [P, CE + HEADS], f32, st)
            decay = sb("decay", [1, SLOTS, HEADS], f32, st)
            factor = sb("factor", [P, HEADS], f32, st)
            wqkv = sb("wqkv", [P, 2, 3 * INNER], f32, st)
            wout = sb("wout", [P, PAIRS, DIM], f32, st)
            bias = sb("bias", [1, 2, DIM], f32, st)
            bsum = sb("bsum", [1, DIM], f32, st)
            ones_b = sb("ones_b", [1, P], f32, st)
            hmean = sb("hmean", [P, 2, 2 * MIX_HEADS], f32, st)
            xn = sb("xnb", [P, 2, DIM], f32, st)
            xt = sb("xtb", [P, 2, 2, P], f32, st)
            kv_work = sb("kv_work", [P, 6, INNER], f32, st)
            squares, ks, vs = kv_work[:, 0:2], kv_work[:, 2:4], kv_work[:, 4:6]
            wqt = sb("wqt", [P, PAIRS, 2, P], f32, st)
            g = kv_work[:, 2:4].rearrange("p a n -> p (a n)").rearrange("p (a n) -> p a n", a=PAIRS)
            kv_var = sb("kv_var", [P, 2 * MIX_HEADS], f32, st)
            kv_prod = sb("kv_prod", [P, MIX_HEADS], f32, st)
            rk = sb("rk", [P, MIX_HEADS], f32, st)
            dots = sb("dots", [P, PAIRS, P], f32, st)
            eff = sb("eff", [P, 2, DIM], f32, st)
            block = st.enter_context(nc.Block())

            def schedule(each):
                eng, body, between = each
                with eng.Fori(0, KV_ITERS) as i:
                    for u in range(SLOTS):
                        body(i * SLOTS + u, i, u, "kv", True)
                between()
                with eng.Fori(KV_ITERS, ITERS - 1) as i:
                    for u in range(SLOTS):
                        body(i * SLOTS + u, i, u, "mix", True)
                for u in range(SLOTS):
                    body((ITERS - 1) * SLOTS + u, ITERS - 1, u, "mix", u < SLOTS - 1)

            def mix_tiles(i, u):
                for j in range(2 * u, min(2 * u + 2, MIX_TILES)):
                    yield (i - KV_ITERS) * MIX_TILES + j, j % 2

            @block.sync
            def _(sp):
                sp.dma_start(wqkv[:], a["wqkv"].rearrange("(k p) n -> p k n", p=P)).then_inc(mixw_in, 16)
                sp.dma_start(wout[:], a["wout"].rearrange("(k p) n -> p k n", p=P)).then_inc(mixw_in, 16)
                sp.dma_start(bias[:, 0], a["h_bias"].rearrange("(o n) -> o n", o=1)).then_inc(bias_in, 16)
                sp.dma_start(bias[:, 1], a["b_out"].rearrange("(o n) -> o n", o=1)).then_inc(bias_in, 16)
                by_chunk = edge_logits.rearrange("(t p c) h -> t p (c h)", p=P, c=CHUNK_COLS)
                with sp.Fori(0, ITERS) as i:
                    for u in range(SLOTS):
                        t = i * SLOTS + u
                        sp.wait_ge(chunk_free, t + 1)
                        sp.sem_inc(er_seen, 1)
                        sp.dma_start(er[:, u].rearrange("p c h -> p (c h)"),
                                     by_chunk[ds(t, 1)].rearrange("o p n -> (o p) n")).then_inc(er_in[u], 16)

            @block.gpsimd
            def _(pool):
                pool.sem_inc(chunk_free, SLOTS)
                with pool.Fori(0, ITERS) as i:
                    for u in range(SLOTS):
                        t = i * SLOTS + u
                        pool.wait_ge(chunk_free, t + 1)
                        pool.tensor_copy(idx_now[:, u], feat_idx[:, ds(t * CHUNK_COLS, CHUNK_COLS)]).then_inc(idx_staged, 1)
                        pool.wait_ge(idx_staged, t + 1)
                        pool.sem_inc(staged_seen, 1)
                        for c in range(CHUNK_COLS):
                            pool.indirect_dma_start(out=rows[:, u, c], out_offset=None, in_=features,
                                                    in_offset=bass.IndirectOffsetOnAxis(ap=idx_now[:, u, c:c + 1], axis=0),
                                                    bounds_check=NODES_PAD * RELS - 1, oob_is_err=True).then_inc(gathered[u], 16)

            def hc(tile, n=CE):
                return tile[:, 0:n].rearrange("p (h c) -> p h c", h=HEADS)

            def by_head(edge_data, t):
                return edge_data[:, ds(t * CHUNK_COLS, CHUNK_COLS)].unsqueeze(1).to_broadcast([P, HEADS, CHUNK_COLS])

            @block.vector
            def _(dve):
                dve.memset(acc[:], 0.0).then_inc(main_init, 1)
                dve.memset(carry_f[:], -BIG).then_inc(main_init, 1)
                dve.memset(carry_b[:], -BIG).then_inc(main_init, 1)
                dve.memset(ones_b[:], 1.0).then_inc(main_init, 1)
                dve.memset(dots[:], 0.0).then_inc(main_init, 1)
                dve.memset(kv_work[:], 0.0).then_inc(main_init, 1)
                dve.memset(ones_row[:], 1.0).then_inc(main_init, 1)
                dve.wait_ge(main_init, 7)
                dve.sem_inc(extra_added, 1)
                dve.sem_inc(first_step, 1)
                dve.sem_inc(dots_added, 1)
                dve.wait_ge(mixw_in, 32)
                wkv = [wqkv[:, k, INNER:3 * INNER].rearrange("p (h d) -> p h d", d=MIX_DIM) for k in range(2)]
                for k in range(2):
                    dve.tensor_reduce(hmean[:, k], wkv[k], AX.X, ALU.add).then_inc(centred, 1)
                dve.wait_ge(centred, 2)
                dve.tensor_scalar(hmean[:], hmean[:], 1.0 / MIX_DIM, None, ALU.mult).then_inc(centred, 1)
                dve.wait_ge(centred, 3)
                for k in range(2):
                    dve.tensor_tensor(wkv[k], wkv[k], hmean[:, k].unsqueeze(2).to_broadcast([P, 2 * MIX_HEADS, MIX_DIM]),
                                      ALU.subtract).then_inc(centred, 1)
                dve.wait_ge(bias_in, 32)
                dve.tensor_tensor(bsum[:], bias[:, 0], bias[:, 1], ALU.add).then_inc(centred, 1)

                def after(t, n):
                    dve.wait_ge(prep, PREP * t + n)

                def front(t, i, u):
                    dve.wait_ge(gathered[u], (i + 1) * 16 * CHUNK_COLS)
                    dve.wait_ge(er_in[u], (i + 1) * 16)
                    dve.tensor_tensor(hc(lin), rows[:, u, :, HEAD_DIM::HEAD_COLS].rearrange("p c h -> p h c"),
                                      er[:, u].rearrange("p c h -> p h c"), ALU.add).then_inc(prep, 2)
                    after(t, 2)
                    dve.scalar_tensor_tensor(e[:], lin[:], SLOPE, lin[:], ALU.mult, ALU.max).then_inc(prep, 1)
                    after(t, 3)
                    dve.wait_ge(masks_ready, t + 1)
                    dve.tensor_tensor_scan(out=max_f[:], data0=mask_f[:, u], data1=e[:], initial=-BIG, op0=ALU.add, op1=ALU.max)
                    dve.tensor_tensor_scan(out=max_b[:, ::-1], data0=mask_b[:, u, ::-1], data1=e[:, ::-1], initial=-BIG,
                                           op0=ALU.add, op1=ALU.max).then_inc(prep, 1)
                    after(t, 4)
                    dve.tensor_tensor(seg_max[:], max_f[:], max_b[:], ALU.max).then_inc(prep, 1)

                def across(t, u):
                    dve.wait_ge(tails_psum, t + 1)
                    dve.tensor_tensor_scan(out=carry_f[:, u, 1:P + 1], data0=pass_t[:, 0:P], data1=psum[0:HEADS, TAILS, 0:P],
                                           initial=carry_f[:, u, 0:1], op0=ALU.add, op1=ALU.max)
                    dve.tensor_tensor_scan(out=carry_b[:, 0:P][:, ::-1], data0=pass_t[:, P:2 * P][:, ::-1],
                                           data1=psum[0:HEADS, TAILS, P:2 * P][:, ::-1],
                                           initial=-BIG, op0=ALU.add, op1=ALU.max).then_inc(prep, 1)

                def numerators(t, u, beside=lambda: None):
                    dve.wait_ge(carries_psum, t + 1)
                    dve.tensor_tensor(hc(reach_f), by_head(first_run, t),
                                      psum[:, SMALL, 0:HEADS].unsqueeze(2).to_broadcast([P, HEADS, CHUNK_COLS]), ALU.add)
                    dve.tensor_tensor(hc(reach_b), by_head(last_run, t),
                                      psum[:, SMALL, HEADS:2 * HEADS].unsqueeze(2).to_broadcast([P, HEADS, CHUNK_COLS]), ALU.add)
                    dve.tensor_scalar(from_prev[:], psum[:, SMALL, 0:HEADS], prev_open[:, ds(t, 1)], None, ALU.add)
                    beside()
                    dve.tensor_copy(carry_f[:, (u + 1) % SLOTS, 0:1], carry_f[:, u, P:P + 1]).then_inc(prep, 1)
                    after(t, 7)
                    dve.tensor_tensor(reach_f[:], reach_f[:], reach_b[:], ALU.max).then_inc(prep, 1)
                    after(t, 8)
                    dve.tensor_tensor(seg_max[:], seg_max[:], reach_f[:], ALU.max).then_inc(prep, 1)
                    after(t, 9)
                    dve.tensor_tensor(arg[:, 0:CE], e[:], seg_max[:], ALU.subtract)
                    dve.tensor_tensor(arg[:, CE:], from_prev[:], hc(seg_max)[:, :, 0], ALU.subtract).then_inc(prep, 1)
                    dve.wait_ge(exp_ready, t + 1)
                    dve.tensor_scalar(decay[:, u], ex[0:1, CE:], -1.0, None, ALU.add).then_inc(prep, 1)
                    own = CHUNK_COLS - ACT_COLS
                    row4 = rows[:, u].rearrange("p c (h d) -> p c h d", d=HEAD_COLS)[:, 0:own]
                    dve.tensor_tensor(row4, row4, hc(ex).rearrange("p h c -> p c h")[:, 0:own].unsqueeze(3).to_broadcast(
                        [P, own, HEADS, HEAD_COLS]), ALU.mult).then_inc(prep, 1)

                first_of = {}

                def blocks(t, u):
                    for j in range(0 if u == 0 else 2, 3):
                        first_of[u + j] = dve.value_load(last_block[P - 1:P, ds(t + j, 1)], min_val=0, max_val=NODE_TILES - 1)
                    return first_of[u], first_of[u + 1], first_of[u + 2]

                def one_hot(z, t, b):
                    dve.scalar_tensor_tensor(onehot[:, z], iota_free[:].unsqueeze(1).to_broadcast([P, CHUNK_COLS, P]),
                                             block_base[:, ds(b, 1)],
                                             dst_f[:, ds(t * CHUNK_COLS, CHUNK_COLS)].unsqueeze(2).to_broadcast([P, CHUNK_COLS, P]),
                                             ALU.add, ALU.is_equal).then_inc(onehot_ready, 1)

                def block_sums(b):
                    return acc[:, ds(b, 1)].rearrange("p o h c -> p (o h) c")

                def get_factor(t):
                    dve.wait_ge(first_step, 2 * t + 1)
                    dve.wait_ge(decay_psum, t + 1)
                    dve.tensor_scalar(factor[:], psum[:, SMALL, 16:16 + HEADS], 1.0, None, ALU.add).then_inc(first_step, 1)

                def add_first(t, u, b):
                    dve.wait_ge(sums_psum, t + b + 1)
                    dve.wait_ge(first_step, 2 * t + 2)
                    dve.wait_ge(extra_added, b + 1)
                    sums = block_sums(b)
                    for h in range(HEADS):
                        last = dve.scalar_tensor_tensor(sums[:, h, :], sums[:, h, :], factor[:, h:h + 1],
                                                        psum[:, SUMS + u, h * HEAD_COLS:(h + 1) * HEAD_COLS], ALU.mult, ALU.add)
                    last.then_inc(first_step, 1)

                def add_last(t, first, last):
                    with dve.If(first < last):
                        dve.wait_ge(sums_psum, t + last + 1)
                        dve.tensor_tensor(block_sums(last), block_sums(last),
                                          psum[:, MORE, 0:ROW].rearrange("p (h c) -> p h c", h=HEADS), ALU.add).then_inc(extra_added, 1)

                def kv_variance(k, z):
                    dve.wait_ge(squares_ready, 2 * k + 2)
                    dve.tensor_reduce(kv_var[:], squares.rearrange("p a (h d) -> p (a h) d", d=MIX_DIM), AX.X,
                                      ALU.add).then_inc(var_ready, 1)
                    dve.wait_ge(var_ready, 3 * k + 1)
                    dve.tensor_scalar(kv_var[:], kv_var[:], 1.0 / MIX_DIM, EPS, ALU.mult, ALU.add).then_inc(var_ready, 1)
                    dve.wait_ge(var_ready, 3 * k + 2)
                    dve.tensor_tensor(kv_prod[:], kv_var[:, 0:MIX_HEADS], kv_var[:, MIX_HEADS:], ALU.mult).then_inc(var_ready, 1)

                def kv_scale(k, z):
                    dve.wait_ge(stdb_ready, k + 1)
                    dve.reciprocal(rk[:], rk[:]).then_inc(rk_ready, 1)
                    dve.wait_ge(rk_ready, k + 1)
                    keys = ks[:, z].rearrange("p (h d) -> p h d", d=MIX_DIM)
                    dve.tensor_tensor(keys, keys, rk[:].unsqueeze(2).to_broadcast([P, MIX_HEADS, MIX_DIM]), ALU.mult).then_inc(k_ready, 1)

                def kv_add(n):
                    dve.wait_ge(dots_psum, n + 1)
                    flat_dots = dots[:].rearrange("p a b -> p (a b)")
                    dve.tensor_tensor(flat_dots, flat_dots, psum[:, TAILS, :], ALU.add).then_inc(dots_added, 1)

                front(0, 0, 0)
                across(0, 0)
                one_hot(0, 0, 0)
                numerators(0, 0)

                def body(t, i, u, phase, more):
                    before, first, last = blocks(t, u)
                    k = i * 2 + u - 1
                    if more:
                        front(t + 1, i + (u + 1) // SLOTS, (u + 1) % SLOTS)
                    add_last(t - 1, before, first)
                    with dve.If(first < last):
                        one_hot(SLOTS, t, first + 1)
                    with dve.If(first + 1 < last):
                        if more:
                            across(t + 1, (u + 1) % SLOTS)
                        with dve.Fori(first + 2, last + 1) as b:
                            dve.wait_ge(sums_psum, t + b)
                            dve.tensor_tensor(block_sums(b - 1), block_sums(b - 1),
                                              psum[:, MORE, 0:ROW].rearrange("p (h c) -> p h c", h=HEADS), ALU.add).then_inc(extra_added, 1)
                            one_hot(SLOTS, t, b)
                    if more:
                        one_hot((u + 1) % SLOTS, t + 1, last)
                        with dve.If(last < first + 2):
                            across(t + 1, (u + 1) % SLOTS)
                    if phase == "kv" and u:
                        kv_variance(k, u - 1)
                    if more:
                        numerators(t + 1, (u + 1) % SLOTS, lambda: get_factor(t))
                    else:
                        get_factor(t)
                    add_first(t, u, first)
                    dve.sem_inc(chunk_done, 1)
                    if phase == "kv" and u:
                        kv_scale(k, u - 1)
                    if phase == "kv" and u != 1:
                        kv_add(i * 2 + u // 2)

                def between():
                    kv_add(NODE_TILES)
                    dve.wait_ge(dots_added, NODE_TILES + 2)
                    for lo in (0, MIX_DIM):
                        own, other = slice(lo, lo + MIX_DIM), slice(MIX_DIM - lo, 2 * MIX_DIM - lo)
                        dve.tensor_scalar(dots[own, :, own], dots[own, :, own], 1.0 / NODES, None, ALU.mult).then_inc(dots_masked, 1)
                        dve.memset(dots[own, :, other], 0.0).then_inc(dots_masked, 1)
                    dve.wait_ge(g_psum, 1)
                    dve.tensor_copy(g.rearrange("p a b -> p (a b)").rearrange("p (a b) -> p a b", a=2), psum[:, KEYS:KEYS + 2, :]).then_inc(g_ready, 1)
                    dve.wait_ge(eff_psum, 1)
                    dve.tensor_copy(eff[:].rearrange("p a b -> p (a b)"), psum[:, TAILS, :]).then_inc(eff_ready, 1)

                def mixed_body(t, i, u, phase, more):
                    body(t, i, u, phase, more)
                    if phase == "mix":
                        pair = list(mix_tiles(i, u))
                        dve.wait_ge(mix_psum, pair[-1][0] + 1)
                        for n, z in pair:
                            dve.tensor_tensor(tile_of(x_res, n), tile_of(x_res, n), psum[:, VALUES, z * DIM:(z + 1) * DIM],
                                              ALU.add).then_inc(mix_added, 1)

                schedule((dve, mixed_body, between))
                add_last(CHUNKS - 1, first_of[SLOTS], first_of[SLOTS + 1])

            @block.scalar
            def _(act):
                def norm(n, t, z):
                    act.wait_ge(xtb_psum, n + 1)
                    nc.scalar.activation(xn[:, z], tile_of(x_res, t), ACT.Identity, bias=ln_shift[:, ds(t, 1)],
                                         scale=ln_rstd[:, ds(t, 1)]).then_inc(xnb_ready, 1)

                def evacuate(n, through, z, bank, at):
                    act.wait_ge(xtb_psum, through + 2)
                    nc.scalar.copy(xt[:, z], psum[:, bank, at:at + 2 * P].rearrange("p (k n) -> p k n", k=2)).then_inc(xtb_ready, 1)

                def masks(t, u):
                    nc.scalar.copy(hc(mask_f[:, u]), by_head(prev_mask, t))
                    nc.scalar.copy(hc(mask_b[:, u]), by_head(next_mask, t))
                    nc.scalar.copy(pass_now[:, u, 0], prev_pass[:, ds(t, 1)].to_broadcast([P, HEADS]))
                    nc.scalar.copy(pass_now[:, u, 1], next_pass[:, ds(t, 1)].to_broadcast([P, HEADS])).then_inc(masks_ready, 1)

                def open_masks(t):
                    act.wait_ge(masks_psum, t + 1)
                    nc.scalar.copy(pass_t[:], psum[0:HEADS, TAILS, 2 * P:4 * P]).then_inc(masks_copied, 1)

                def exponentials(t, u):
                    act.wait_ge(prep, PREP * t + 2)
                    act.sem_inc(masks_free, 1)
                    nc.scalar.copy(rows[:, u, :, HEAD_DIM::HEAD_COLS], ones_row[:].rearrange("p (c h) -> p c h", h=HEADS))
                    act.wait_ge(prep, PREP * t + 10)
                    nc.scalar.activation(ex[:], arg[:], ACT.Exp).then_inc(exp_ready, 1)
                    act.wait_ge(exp_ready, t + 1)
                    for c in range(CHUNK_COLS - ACT_COLS, CHUNK_COLS):
                        for h in range(HEADS):
                            n = h * CHUNK_COLS + c
                            row = rows[:, u, c, h * HEAD_COLS:(h + 1) * HEAD_COLS]
                            last = nc.scalar.activation(row, row, ACT.Copy, scale=ex[:, n:n + 1])
                    last.then_inc(act_rows_ready, 1)

                act.wait_ge(main_init, 7)
                act.wait_ge(wq_psum, 1)
                nc.scalar.copy(wqt[:].rearrange("p a k n -> p (a k n)").rearrange("p (b n) -> p b n", b=2),
                               psum[:, KEYS:KEYS + 2, :]).then_inc(wq_ready, 1)
                masks(0, 0)
                open_masks(0)
                masks(1, 1)
                exponentials(0, 0)

                def body(t, i, u, phase, more):
                    k = i * 2 + u
                    ahead = more and (u < SLOTS - 2 or not isinstance(t, int))
                    pair = [(n + NODE_TILES, n, z) for n, z in mix_tiles(i, u)] if phase == "mix" else []
                    if phase == "kv" and u < 2:
                        norm(k, k, u)
                    for n, tile, z in pair:
                        norm(n, tile, z)
                    if more:
                        open_masks(t + 1)
                    if phase == "kv" and u < 2:
                        evacuate(k, k + 1, u, VALUES, 0)
                        act.wait_ge(keys_psum, k + 1)
                        nc.scalar.copy(ks[:, u], psum[:, KEYS, :])
                    if phase == "kv" and u:
                        act.wait_ge(v_ready, k + 1)
                        for j, tile in enumerate((ks, vs)):
                            nc.scalar.activation(squares[:, j], tile[:, u - 1], ACT.Square).then_inc(squares_ready, 1)
                    for n, tile, z in pair:
                        evacuate(n, pair[-1][0] + 1, z, KEYS, z * DIM)
                    if more:
                        exponentials(t + 1, (u + 1) % SLOTS)
                    if ahead:
                        masks(t + 2, (u + 2) % SLOTS)
                    if phase == "kv" and u:
                        act.wait_ge(var_ready, 3 * (k - 1) + 3)
                        nc.scalar.activation(rk[:], kv_prod[:], ACT.Sqrt).then_inc(stdb_ready, 1)
                    if phase == "kv" and u < 2:
                        act.wait_ge(values_psum, k + 1)
                        nc.scalar.copy(vs[:, u], psum[:, VALUES, :]).then_inc(v_ready, 1)

                def between():
                    pass

                schedule((act, body, between))

            @block.tensor
            def _(pe):
                pe.sem_inc(xtb_psum, 2)
                pe.sem_inc(mix_added, 1)
                pe.sem_inc(chunk_done, 1)
                pe.sem_inc(v_ready, 1)
                pe.sem_inc(k_ready, 1)
                pe.wait_ge(mixw_in, 32)

                def mask_tails(t, u):
                    pe.wait_ge(masks_ready, t + 1)
                    for j in range(2):
                        last = nc.tensor.matmul(psum[0:HEADS, TAILS, (2 + j) * P:(3 + j) * P], pass_now[:, u, j], ident[:], start=True, stop=True)
                    last.then_inc(masks_psum, 1)

                def tails(t):
                    pe.wait_ge(prep, PREP * t + 4)
                    pe.wait_ge(masks_copied, t + 1)
                    for j, tile in enumerate((hc(max_f)[:, :, CHUNK_COLS - 1], hc(max_b)[:, :, 0])):
                        last = nc.tensor.matmul(psum[0:HEADS, TAILS, j * P:(j + 1) * P], tile, ident[:], start=True, stop=True)
                    last.then_inc(tails_psum, 1)

                def carries(t, u):
                    pe.wait_ge(prep, PREP * t + 6)
                    nc.tensor.matmul(psum[:, SMALL, 0:HEADS], carry_f[:, u, 0:P], ident[0:HEADS, 0:HEADS], start=True, stop=True)
                    nc.tensor.matmul(psum[:, SMALL, HEADS:2 * HEADS], carry_b[:, 1:P + 1], ident[0:HEADS, 0:HEADS],
                                     start=True, stop=True).then_inc(carries_psum, 1)

                def products(n, z):
                    pe.wait_ge(v_ready, n + 1)
                    pe.wait_ge(k_ready, n + 1)
                    for j in range(PAIRS):
                        last = nc.tensor.matmul(psum[:, TAILS, j * P:(j + 1) * P], vs[:, z, j * P:(j + 1) * P],
                                                ks[:, z, j * P:(j + 1) * P], start=True, stop=True)
                    last.then_inc(dots_psum, 1)

                def step(t, u, b, z, bank, between=lambda c: None):
                    pe.wait_ge(onehot_ready, t + b + 1)
                    if z < SLOTS:
                        pe.wait_ge(prep, PREP * t + PREP)
                    for c in range(CHUNK_COLS):
                        if c == CHUNK_COLS - ACT_COLS and z < SLOTS:
                            pe.wait_ge(act_rows_ready, t + 1)
                        last = nc.tensor.matmul(psum[:, bank, 0:ROW], onehot[:, z, c], rows[:, u, c],
                                                start=(c == 0), stop=(c == CHUNK_COLS - 1))
                        between(c)
                    last.then_inc(sums_psum, 1)

                for j in range(PAIRS):
                    for half in range(2):
                        n = (2 * j + half) * P
                        last = nc.tensor.transpose(psum[:, KEYS + n // 512, n % 512:n % 512 + P], wqkv[:, half, j * P:(j + 1) * P], ident[:])
                last.then_inc(wq_psum, 1)
                pe.wait_ge(wq_ready, 1)
                first_of = {}
                mask_tails(0, 0)
                tails(0)
                carries(0, 0)
                pe.wait_ge(centred, 6)

                def transposes(n, z, bank, at):
                    pe.wait_ge(xnb_ready, n + 1)
                    for j in range(2):
                        last = nc.tensor.transpose(psum[:, bank, at + j * P:at + (j + 1) * P], xn[:, z, j * P:(j + 1) * P], ident[:])
                    last.then_inc(xtb_psum, 1)

                def body(t, i, u, phase, more):
                    if u == 0:
                        first_of[0] = pe.value_load(last_block[P - 1:P, ds(t + 1, 1)], min_val=0, max_val=NODE_TILES - 1)
                    first_of[u + 1] = pe.value_load(last_block[P - 1:P, ds(t + 2, 1)], min_val=0, max_val=NODE_TILES - 1)
                    first, last_b = first_of[u], first_of[u + 1]

                    k = i * 2 + u
                    pair = list(mix_tiles(i, u)) if phase == "mix" else []

                    def mix():
                        if pair:
                            pe.wait_ge(mix_added, pair[0][0] + 1)
                        for n, z in pair:
                            pe.wait_ge(xtb_ready, n + NODE_TILES + 1)
                            nc.tensor.matmul(psum[:, VALUES, z * DIM:(z + 1) * DIM], ones_b[:], bsum[:], start=True, stop=False)
                            for half in range(2):
                                last = nc.tensor.matmul(psum[:, VALUES, z * DIM:(z + 1) * DIM], xt[:, z, half], eff[:, half],
                                                        start=False, stop=(half == 1))
                            last.then_inc(mix_psum, 1)

                    def project(z, part, bank, signal):
                        for half in range(2):
                            last = nc.tensor.matmul(psum[:, bank, :], xt[:, z, half], wqkv[:, half, part * INNER:(part + 1) * INNER],
                                                    start=(half == 0), stop=(half == 1))
                        last.then_inc(signal, 1)

                    def between_products(c):
                        if c == 7:
                            pe.wait_ge(chunk_done, t + 1)
                            nc.tensor.matmul(psum[:, SMALL, 16:16 + HEADS], onehot[0:1, u, 0, :], decay[:, u],
                                             start=True, stop=True).then_inc(decay_psum, 1)
                        if more and c == 0:
                            if phase == "kv" and u != 2:
                                pe.wait_ge(dots_added, i * 2 + u + 1)
                            mask_tails(t + 1, (u + 1) % SLOTS)
                        if more and c == 3:
                            tails(t + 1)
                        if c == 0 and phase == "kv" and u < 2:
                            transposes(k, u, VALUES, 0)
                        if c == 2 and phase == "kv" and u < 2:
                            pe.wait_ge(xtb_ready, k + 1)
                            project(u, 1, KEYS, keys_psum)
                        if c == 5:
                            for n, z in pair:
                                transposes(n + NODE_TILES, z, KEYS, z * DIM)
                        if more and c == 8:
                            carries(t + 1, (u + 1) % SLOTS)
                        if c == CHUNK_COLS - 4 and phase == "kv" and u != 1:
                            products(i * 2 + u // 2, 1 - u // 2)
                        if c == CHUNK_COLS - 2:
                            mix()

                    step(t, u, first, u, SUMS + u, between_products)
                    with pe.If(first < last_b):
                        with pe.Fori(first + 1, last_b + 1) as b:
                            step(t, u, b, SLOTS, MORE)
                    pe.wait_ge(sums_psum, t + last_b + 1)
                    pe.sem_inc(chunk_free, 1)
                    if phase == "kv" and u < 2:
                        project(u, 2, VALUES, values_psum)

                def between():
                    pe.wait_ge(dots_added, NODE_TILES + 1)
                    products(NODE_TILES, 1)
                    pe.wait_ge(dots_masked, 4)
                    for j in range(PAIRS):
                        n = j * DIM
                        last = nc.tensor.matmul(psum[:, KEYS + n // 512, n % 512:n % 512 + DIM], dots[:, j], wout[:, j], start=True, stop=True)
                    last.then_inc(g_psum, 1)
                    pe.wait_ge(g_ready, 1)
                    for half in range(2):
                        for j in range(PAIRS):
                            last = nc.tensor.matmul(psum[:, TAILS, half * DIM:(half + 1) * DIM], wqt[:, j, half], g[:, j],
                                                    start=(j == 0), stop=(j == PAIRS - 1))
                    last.then_inc(eff_psum, 1)
                    pe.wait_ge(eff_ready, 1)

                schedule((pe, body, between))

        tail_step, ln2_std, wts_in, small_in = sem("tail_step"), sem("ln2_std"), sem("wts_in"), sem("small_in")
        wt_psum, wt_ready, w_stored, w_row_in = sem("wt_psum"), sem("wt_ready"), sem("w_stored"), sem("w_row_in")
        xf_staged, xf_psum, xf_ready = sem("xf_staged"), sem("xf_psum"), sem("xf_ready")
        h_psum, h_ready, y_psum, y_ready, ones_ready = (sem(n) for n in ("h_psum", "h_ready", "y_psum", "y_ready", "ones_ready"))
        out_ready, out_stored = sem("out_ready"), sem("out_stored")
        LN_PARTS = ((0, GROUP_TILES), (GROUP_TILES, 3 * GROUP_TILES), (3 * GROUP_TILES, NODE_TILES))
        OUT_TILES = 5
        with ExitStack() as st:
            w1 = sb("w1", [P, 2, HIDDEN], f32, st)
            w2 = sb("w2", [P, HID_TILES, DIM], f32, st)
            b1 = sb("b1", [P, HID_TILES], f32, st)
            wr = sb("wr", [P, DIM], f32, st)
            br = sb("br", [P, 1], f32, st)
            b2 = sb("b2", [1, DIM], f32, st)
            ones = sb("ones", [1, P], f32, st)
            rden = sb("rden", [P, NODE_TILES * HEADS], f32, st)
            y_all = sb("y_all", [P, NODE_TILES, DIM], f32, st)
            weight = sb("weight", [P, NODE_TILES], f32, st)
            weight_t = sb("weight_t", [NODE_TILES, P], f32, st)
            w_row = sb("w_row", [P, NODES], f32, st)
            junk = sb("junk", [P, 2, NODES], bf16, st)
            junk_diag = sb("junk_diag", [P, P], bf16, st)
            lower = sb("lower", [P, P], f32, st)
            count = sb("count", [P, 3, NODE_TILES], f32, st)
            chosen = sb("chosen", [P, NODE_TILES], f32, st)
            weighted = sb("weighted", [P, 2, DIM], f32, st)
            xf = sb("xf", [P, GROUP_TILES, DIM], f32, st)
            xft = sb("xft", [P, 2, GROUP_TOKENS], f32, st)
            hid = sb("hid", [P, HID_TILES, GROUP_TOKENS], f32, st)
            xn2 = acc[:].rearrange("p t h c -> p (t h c)")[:, 0:NODE_TILES * DIM].rearrange("p (t d) -> p t d", d=DIM)
            flat_x = x_res[:].rearrange("p t d -> p (t d)")
            heads = acc[:].rearrange("p t h c -> p (t h) c")
            block = st.enter_context(nc.Block())

            @block.vector
            def _(dve):
                done = [0]

                def then(ins):
                    done[0] += 1
                    ins.then_inc(tail_step, 1)
                    dve.wait_ge(tail_step, done[0])

                x_heads = flat_x.rearrange("p (t d) -> p t d", d=HEAD_DIM)
                then(dve.tensor_scalar(rden[:], heads[:, :, HEAD_DIM], 1e-30, None, ALU.max))
                then(dve.reciprocal(rden[:], rden[:]))
                for part, (lo, hi) in enumerate(LN_PARTS):
                    hs = slice(lo * HEADS, hi * HEADS)
                    then(dve.tensor_tensor(heads[:, hs, 0:HEAD_DIM], heads[:, hs, 0:HEAD_DIM],
                                           rden[:, hs].unsqueeze(2).to_broadcast([P, (hi - lo) * HEADS, HEAD_DIM]), ALU.mult))
                    then(dve.tensor_tensor(x_heads[:, hs], x_heads[:, hs], heads[:, hs, 0:HEAD_DIM], ALU.add))
                    with dve.Fori(lo // GROUP_TILES, hi // GROUP_TILES) as i:
                        for u in range(GROUP_TILES):
                            t = i * GROUP_TILES + u
                            dve.bn_stats(tile_of(bn, t), tile_of(x_res, t)).then_inc(tail_step, 1)
                    done[0] += hi - lo
                    dve.wait_ge(tail_step, done[0])
                    moments(dve, then, lo, hi)
                    marks["variance %d" % part] = done[0]
                    dve.wait_ge(ln2_std, part + 1)
                    then(dve.reciprocal(ln_rstd[:, lo:hi], ln_rstd[:, lo:hi]))
                    with dve.Fori(lo // GROUP_TILES, hi // GROUP_TILES) as i:
                        for u in range(GROUP_TILES):
                            t = i * GROUP_TILES + u
                            dve.tensor_scalar(tile_of(xn2, t), tile_of(x_res, t), ln_mean[:, ds(t, 1)], ln_rstd[:, ds(t, 1)],
                                              ALU.subtract, ALU.mult).then_inc(tail_step, 1)
                    done[0] += hi - lo
                    marks["xn %d" % part] = done[0]
                    dve.wait_ge(tail_step, done[0])
                dve.wait_ge(small_in, 64)
                for t in range(NODE_TILES):
                    dve.scalar_tensor_tensor(weighted[:, t % 2], xn2[:, t], 1.0, wr[:], ALU.mult, ALU.mult,
                                             accum_out=weight[:, t:t + 1]).then_inc(tail_step, 1)
                    done[0] += 1
                    if t:
                        dve.wait_ge(tail_step, done[0] - 1)
                dve.wait_ge(tail_step, done[0])
                then(dve.tensor_scalar(weight[:], weight[:], br[:], None, ALU.add))
                marks["weight"] = done[0]
                then(dve.tensor_tensor(x_res[:], x_res[:], xn2, ALU.add))
                dve.wait_ge(w_row_in, 16)
                dve.wait_ge(ones_ready, 3)
                then(dve.memset(count[:], 0.0))
                for t in range(NODE_TILES):
                    lo, hi = t * P, min((t + 1) * P, NODES)
                    w_t = weight[:, t:t + 1]
                    if t:
                        dve.tensor_scalar(junk[:, 0, 0:lo], w_row[:, 0:lo], w_t, None, ALU.is_ge, ALU.add,
                                          accum_out=count[:, 0, t:t + 1])
                    dve.tensor_scalar(junk[:, 1, lo:NODES], w_row[:, lo:NODES], w_t, None, ALU.is_gt, ALU.add,
                                      accum_out=count[:, 1, t:t + 1])
                    then(dve.scalar_tensor_tensor(junk_diag[:, 0:hi - lo], w_row[:, lo:hi], w_t, lower[:, 0:hi - lo],
                                                  ALU.is_equal, ALU.mult, accum_out=count[:, 2, t:t + 1]))
                    if t % OUT_TILES == OUT_TILES - 1:
                        ts = slice(t + 1 - OUT_TILES, t + 1)
                        then(dve.tensor_tensor(count[:, 0, ts], count[:, 0, ts], count[:, 1, ts], ALU.add))
                        then(dve.tensor_tensor(count[:, 0, ts], count[:, 0, ts], count[:, 2, ts], ALU.add))
                        then(dve.scalar_tensor_tensor(chosen[:, ts], count[:, 0, ts], float(SELECTED), weight[:, ts],
                                                      ALU.is_lt, ALU.mult))
                        for o in range(t + 1 - OUT_TILES, t + 1):
                            dve.wait_ge(y_ready, o + 1)
                            dve.scalar_tensor_tensor(y_all[:, o], y_all[:, o], chosen[:, o:o + 1], x_res[:, o],
                                                     ALU.mult, ALU.add).then_inc(out_ready, 1)

            @block.sync
            def _(sp):
                sp.dma_start(w1[:], a["w1"].rearrange("(k p) n -> p k n", p=P)).then_inc(wts_in, 16)
                sp.dma_start(w2[:], a["w2"].rearrange("(k p) n -> p k n", p=P)).then_inc(wts_in, 16)
                sp.dma_start(wr[:], a["wr"].partition_broadcast(P)).then_inc(small_in, 16)
                sp.dma_start(br[:], a["br"].partition_broadcast(P)).then_inc(small_in, 16)
                sp.dma_start(b1[:], a["b1"]).then_inc(small_in, 16)
                sp.dma_start(b2[:], a["b2"]).then_inc(small_in, 16)
                sp.wait_ge(wt_ready, 1)
                sp.dma_start(node_weights, weight_t[:]).then_inc(w_stored, 16)
                sp.wait_ge(w_stored, 16)
                sp.dma_start(w_row[:], node_weights.rearrange("t p -> (t p)")[0:NODES].partition_broadcast(P)).then_inc(w_row_in, 16)
                full = NODES // P
                for t in range(0, NODE_TILES, OUT_TILES):
                    n = min(OUT_TILES, full - t)
                    sp.wait_ge(out_ready, t + OUT_TILES)
                    sp.dma_start(out[t * P:(t + n) * P, :].rearrange("(t p) d -> p t d", p=P), y_all[:, t:t + n]).then_inc(out_stored, 16)
                sp.dma_start(out[full * P:NODES, :], y_all[0:NODES - full * P, full]).then_inc(out_stored, 16)
                sp.wait_ge(out_stored, 16 * (NODE_TILES // OUT_TILES + 1))

            @block.gpsimd
            def _(pool):
                pool.memset(ones[:], 1.0).then_inc(ones_ready, 1)
                pool.memset(lower[:], 1.0).then_inc(ones_ready, 1)
                pool.wait_ge(ones_ready, 2)
                pool.affine_select(out=lower[:], in_=lower[:], compare_op=ALU.is_gt, fill=0.0, base=0,
                                   pattern=[[-1, P]], channel_multiplier=1).then_inc(ones_ready, 1)

            @block.scalar
            def _(act):
                def root(part):
                    lo, hi = LN_PARTS[part]
                    act.wait_ge(tail_step, marks["variance %d" % part])
                    nc.scalar.activation(ln_rstd[:, lo:hi], ln_u[:, lo:hi], ACT.Sqrt).then_inc(ln2_std, 1)

                def stage(g):
                    for j in range(GROUP_TILES):
                        act.wait_ge(xf_psum, GROUP_TILES * g + j + 1)
                        nc.scalar.copy(xf[:, j], tile_of(xn2, g * GROUP_TILES + j)).then_inc(xf_staged, 1)

                def evacuate(g):
                    for j in range(GROUP_TILES):
                        act.wait_ge(xf_psum, GROUP_TILES * g + j + 1 + GROUP_TILES)
                        nc.scalar.copy(xft[:, :, j * P:(j + 1) * P], psum[:, j % 2, 0:2 * P].rearrange("p (k n) -> p k n", k=2)).then_inc(xf_ready, 1)

                def group(g, more=True, root_of=None, part=None):
                    for c in range(HID_TILES):
                        if c == HID_TILES // 2 and root_of is not None:
                            root(root_of)
                        if c == HID_TILES // 2 and part is not None:
                            act.wait_ge(tail_step, marks["xn %d" % part])
                        if c == HID_TILES // 2 and more:
                            stage(g + 1)
                        act.wait_ge(h_psum, HID_TILES * g + c + 1)
                        nc.scalar.activation(hid[:, c], psum[:, 2 + c % 2, 0:GROUP_TOKENS], ACT.Gelu_apprx_tanh,
                                             bias=b1[:, c:c + 1]).then_inc(h_ready, 1)
                    if more:
                        evacuate(g + 1)
                    for j in range(GROUP_TILES):
                        act.wait_ge(y_psum, GROUP_TILES * g + j + 1)
                        nc.scalar.copy(tile_of(y_all, g * GROUP_TILES + j), psum[:, 4 + j % 2, 0:DIM]).then_inc(y_ready, 1)

                root(0)
                act.wait_ge(tail_step, marks["xn 0"])
                stage(0)
                evacuate(0)
                act.wait_ge(small_in, 64)
                group(0, root_of=1, part=1)
                group(1, root_of=2)
                group(2, part=2)
                act.wait_ge(wt_psum, 1)
                nc.scalar.copy(weight_t[:], psum[0:NODE_TILES, 7, 0:P]).then_inc(wt_ready, 1)
                with act.Fori(3, GROUPS - 1) as g:
                    group(g)
                group(GROUPS - 1, False)

            @block.tensor
            def _(pe):
                pe.sem_inc(xf_psum, GROUP_TILES)

                def transposes(g):
                    for j in range(GROUP_TILES):
                        pe.wait_ge(xf_staged, GROUP_TILES * g + j + 1)
                        if j == 2:
                            pe.wait_ge(xf_ready, GROUP_TILES * g + 1)
                        for k in range(2):
                            last = nc.tensor.transpose(psum[:, j % 2, k * P:(k + 1) * P], xf[:, j, k * P:(k + 1) * P], ident[:])
                        last.then_inc(xf_psum, 1)

                def group(g, more=True):
                    pe.wait_ge(xf_ready, GROUP_TILES * g + GROUP_TILES)
                    for c in range(HID_TILES):
                        if c >= 2:
                            pe.wait_ge(h_ready, HID_TILES * g + c - 1)
                        for k in range(2):
                            last = nc.tensor.matmul(psum[:, 2 + c % 2, 0:GROUP_TOKENS], w1[:, k, c * P:(c + 1) * P], xft[:, k],
                                                    start=(k == 0), stop=(k == 1))
                        last.then_inc(h_psum, 1)
                    if more:
                        transposes(g + 1)
                    pe.wait_ge(h_ready, HID_TILES * g + HID_TILES)
                    for j in range(GROUP_TILES):
                        if j == 2:
                            pe.wait_ge(y_ready, GROUP_TILES * g + 1)
                        nc.tensor.matmul(psum[:, 4 + j % 2, 0:DIM], ones[:], b2[:], start=True, stop=False)
                        for c in range(HID_TILES):
                            last = nc.tensor.matmul(psum[:, 4 + j % 2, 0:DIM], hid[:, c, j * P:(j + 1) * P], w2[:, c],
                                                    start=False, stop=(c == HID_TILES - 1))
                        last.then_inc(y_psum, 1)

                transposes(0)
                pe.wait_ge(wts_in, 32)
                pe.wait_ge(small_in, 64)
                pe.wait_ge(ones_ready, 3)
                for g in range(3):
                    group(g)
                pe.wait_ge(tail_step, marks["weight"])
                nc.tensor.matmul(psum[0:NODE_TILES, 7, 0:P], weight[:], ident[:], start=True, stop=True).then_inc(wt_psum, 1)
                with pe.Fori(3, GROUPS - 1) as g:
                    group(g)
                group(GROUPS - 1, False)


def kernel(x, src, dst, edge_type_8, L0_gnn_conv_weights, L0_gnn_attn_l, L0_gnn_attn_r, L0_gnn_h_bias,
           L0_mix_w_qkv, L0_mix_w_out, L0_mix_b_out, L0_ffn_attention_mask, L0_ffn_wr, L0_ffn_br,
           L0_ffn_w1, L0_ffn_b1, L0_ffn_w2, L0_ffn_b2):
    import numpy as np
    import concourse.bacc as bacc
    from concourse.bass_utils import run_bass_kernel_spmd as run

    def chunks(values, fill):
        padded = np.full(EDGES_PAD, fill, values.dtype)
        padded[:EDGES] = values
        return padded

    def lay(padded):
        return padded.reshape(CHUNKS, P, CHUNK_COLS).transpose(1, 0, 2).reshape(P, -1)

    src, dst, kind = (np.asarray(v) for v in (src, dst, edge_type_8))
    dst_pad = chunks(dst, NODES_PAD - 1)
    before = np.concatenate([np.full(1, -1, dst.dtype), dst_pad[:-1]])
    after = np.concatenate([dst_pad[1:], np.full(1, -1, dst.dtype)])
    x = np.asarray(x)
    x_pad = np.zeros((NODES_PAD, DIM), x.dtype)
    x_pad[:NODES] = x
    arrays = {
        "edges": np.stack([lay(v) for v in (chunks(src, NODES_PAD - 1), dst_pad, before, after, chunks(kind, 0))], 1),
        "flat": np.stack([v.reshape(P, -1) for v in (dst_pad, before, chunks(kind, 0))], 1),
        "row_first": dst_pad[::SEARCH_ROW],
        "dst_rows": dst_pad.reshape(SEARCH_ROWS, SEARCH_ROW),
        "x": x_pad,
        "conv": np.asarray(L0_gnn_conv_weights),
        "attn_l": np.asarray(L0_gnn_attn_l), "attn_r": np.asarray(L0_gnn_attn_r),
        "h_bias": np.asarray(L0_gnn_h_bias), "b_out": np.asarray(L0_mix_b_out),
        "wqkv": np.asarray(L0_mix_w_qkv), "wout": np.asarray(L0_mix_w_out),
        "wr": np.asarray(L0_ffn_wr).reshape(DIM), "br": np.asarray(L0_ffn_br),
        "w1": np.asarray(L0_ffn_w1), "w2": np.asarray(L0_ffn_w2),
        "b1": np.asarray(L0_ffn_b1).reshape(HID_TILES, P).T, "b2": np.asarray(L0_ffn_b2).reshape(1, DIM),
    }
    nc = bacc.Bacc("TRN2", target_bir_lowering=False, num_devices=1)
    arrays = {f"in_{k}": np.ascontiguousarray(v) for k, v in arrays.items()}
    aps = {k[3:]: nc.dram_tensor(k, v.shape, mybir.dt.from_np(v.dtype), kind="ExternalInput").ap() for k, v in arrays.items()}
    out = nc.dram_tensor("out", (NODES, DIM), mybir.dt.float32, kind="ExternalOutput").ap()
    gps_layer(nc, aps, out)
    r = run(nc, [arrays], core_ids=[0])
    return r.results[0]["out"]
```
